# Optimizing a Trainium2 kernel written in Bass

```python
import numpy as np
import jax
import jax.numpy as jnp

def _softmax(x, axis=-1):
    return jax.nn.softmax(x, axis=axis)

def _gelu(x):
    return jax.nn.gelu(x, approximate=True)

def _silu(x):
    return jax.nn.silu(x)

def _sigmoid(x):
    return jax.nn.sigmoid(x)

def _layernorm(x, axis=-1, eps=1e-05):
    m = jnp.mean(x, axis=axis, keepdims=True)
    v = jnp.var(x, axis=axis, keepdims=True)
    return (x - m) / jnp.sqrt(v + eps)

def _scatter_add(tgt, idx, src, axis=0):
    return tgt.at[idx].add(src)

def _segment_sum(src, seg, n):
    return jax.ops.segment_sum(src, seg, n)
kernel_name = 'mk_adaln_ffn_d2_seqx_r4_2459a0'

def setup_inputs(seed: int=0):
    np.random.seed(seed)
    _w = jnp.asarray

    def _rec_inputs():
        import jax
        import jax.numpy as jnp
        _rk = jax.random.key(seed)
        x = -0.0002928 + 1 * jax.random.normal(jax.random.fold_in(_rk, 1), (2, 1024, 256), jnp.float32)
        _lenS = 1024 - jax.random.randint(jax.random.fold_in(_rk, 7), (2,), 0, max(1, 1024 // 4) + 1, jnp.int32)
        _lenS2 = 1024 - jax.random.randint(jax.random.fold_in(_rk, 8), (2,), 0, max(1, 1024 // 4) + 1, jnp.int32)
        itok_Sx32_0_1023 = jax.random.randint(jax.random.fold_in(_rk, 12), (1024, 32), 0, 256, jnp.int32)
        condB_uprev = -0.456674 + 0.753242 * jax.random.normal(jax.random.fold_in(_rk, 14), (2,), jnp.float32)
        itok_B_0_15 = jax.random.randint(jax.random.fold_in(_rk, 15), (2,), 0, 16, jnp.int32)
        _validS = jnp.arange(1024)[None, :] < _lenS[:, None]
        _validS2 = jnp.arange(1024)[None, :] < _lenS2[:, None]
        _causal = jnp.tril(jnp.ones((1024, 1024), dtype=bool))
        mask_SxS_bk0 = jnp.logical_not(jnp.broadcast_to(_validS[0:1, :], (1024, 1024)))
        mask_Sx32_bk1 = jnp.ones((1024, 32), dtype=bool)
        return (x, itok_Sx32_0_1023, condB_uprev, itok_B_0_15, mask_SxS_bk0, mask_Sx32_bk1)
    x, itok_Sx32_0_1023, condB_uprev, itok_B_0_15, mask_SxS_bk0, mask_Sx32_bk1 = _rec_inputs()

    def _L0_cond_setup():
        import jax, jax.numpy as jnp
        import numpy as np
        B, S, D, H = (4, 256, 256, 16)
        DH = D // H
        K_SPARSE = 32
        LAMBDA_MAX, ALPHA = (10.0, 5.0)
        SPARSE_THRESHOLD = 1.0
        key = jax.random.key(seed)
        ks = jax.random.split(key, 12)
        x = jax.random.normal(ks[0], (B, S, D), dtype=jnp.float32)
        prior_mask = jax.random.bernoulli(ks[1], 0.1, (S, S))
        prior_indices = jax.random.randint(ks[2], (S, K_SPARSE), 0, S)
        prior_index_mask = jax.random.bernoulli(ks[3], 0.9, (S, K_SPARSE))
        prior_index_mask = prior_index_mask.at[:, 0].set(True)
        u_prev = jax.random.normal(ks[4], (B, 1), dtype=jnp.float32)
        sc = 1.0 / np.sqrt(D)
        Wq = jax.random.normal(ks[5], (D, D), dtype=jnp.float32) * sc
        Wk = jax.random.normal(ks[6], (D, D), dtype=jnp.float32) * sc
        Wv = jax.random.normal(ks[7], (D, D), dtype=jnp.float32) * sc
        Wo = jax.random.normal(ks[8], (D, D), dtype=jnp.float32) * sc
        bq = jnp.zeros((D,), jnp.float32)
        bk = jnp.zeros((D,), jnp.float32)
        bv = jnp.zeros((D,), jnp.float32)
        bo = jnp.zeros((D,), jnp.float32)
        return {'x': x, 'prior_mask': prior_mask, 'prior_indices': prior_indices, 'prior_index_mask': prior_index_mask, 'u_prev': u_prev, 'Wq': Wq, 'bq': bq, 'Wk': Wk, 'bk': bk, 'Wv': Wv, 'bv': bv, 'Wo': Wo, 'bo': bo}
    _L0_cond_all = _L0_cond_setup()
    _L0_cond_in = {k: v for k, v in _L0_cond_all.items() if k in ('Wq', 'bq', 'Wk', 'bk', 'Wv', 'bv', 'Wo', 'bo')}
    del _L0_cond_all

    def _L0_ffn_setup():
        import jax, jax.numpy as jnp
        import numpy as np
        B, S, D = (4, 512, 256)
        N_EXPERTS, EXPERT_SIZE = (16, 64)
        WIDTH = N_EXPERTS * EXPERT_SIZE
        key = jax.random.key(seed)
        k_x, k_w1, k_w2, k_g = jax.random.split(key, 4)
        x = jax.random.normal(k_x, (B, S, D), dtype=jnp.float32)
        w1 = jax.random.normal(k_w1, (D, WIDTH), dtype=jnp.float32) / np.sqrt(D).astype(np.float32)
        b1 = jnp.zeros((WIDTH,), dtype=jnp.float32)
        w2 = jax.random.normal(k_w2, (WIDTH, D), dtype=jnp.float32) / np.sqrt(WIDTH).astype(np.float32)
        b2 = jnp.zeros((D,), dtype=jnp.float32)
        return {'x': x, 'w1': w1, 'b1': b1, 'w2': w2, 'b2': b2}
    _L0_ffn_all = _L0_ffn_setup()
    _L0_ffn_in = {k: v for k, v in _L0_ffn_all.items() if k in ('w1', 'b1', 'w2', 'b2')}
    del _L0_ffn_all

    def _L1_cond_setup():
        import jax, jax.numpy as jnp
        import numpy as np
        B, N, DIM = (32, 256, 256)
        HID = 1024
        PART = 64
        OUT = 256
        SHARED = OUT - PART
        E = 16
        key = jax.random.key(seed)
        ks = jax.random.split(key, 8)
        s = 0.02
        return {'x': jax.random.normal(ks[0], (B, N, DIM), dtype=jnp.float32), 'indices': jax.random.randint(ks[1], (B,), 0, E, dtype=jnp.int64), 'fc1_w': jax.random.normal(ks[2], (HID, DIM), dtype=jnp.float32) * s, 'fc1_b': jnp.zeros((HID,), dtype=jnp.float32), 'fc2_w': jax.random.normal(ks[3], (SHARED, HID), dtype=jnp.float32) * s, 'fc2_b': jnp.zeros((SHARED,), dtype=jnp.float32), 'experts_w': jax.random.normal(ks[4], (E, PART, HID), dtype=jnp.float32) * s, 'experts_b': jnp.zeros((E, PART), dtype=jnp.float32)}
    _L1_cond_all = _L1_cond_setup()
    _L1_cond_in = {k: v for k, v in _L1_cond_all.items() if k in ('fc1_w', 'fc1_b', 'fc2_w', 'fc2_b', 'experts_w', 'experts_b')}
    del _L1_cond_all

    def _L1_ffn_setup():
        import jax, jax.numpy as jnp
        import numpy as np
        K_TOP = 2
        key = jax.random.key(seed)
        k1, k2, k3 = jax.random.split(key, 3)
        B, S, H, E = (4, 512, 256, 8)
        hidden_states = jax.random.normal(k1, (B, S, H), dtype=jnp.float32)
        router_w = jax.random.normal(k2, (E, H), dtype=jnp.float32) * 0.02
        expert_weights = jax.random.normal(k3, (E, H, H), dtype=jnp.float32) * 0.02
        return {'hidden_states': hidden_states, 'router_w': router_w, 'expert_weights': expert_weights}
    _L1_ffn_all = _L1_ffn_setup()
    _L1_ffn_in = {k: v for k, v in _L1_ffn_all.items() if k in ('router_w', 'expert_weights')}
    del _L1_ffn_all
    return {'x': x, 'itok_Sx32_0_1023': itok_Sx32_0_1023, 'condB_uprev': condB_uprev, 'itok_B_0_15': itok_B_0_15, 'mask_SxS_bk0': mask_SxS_bk0, 'mask_Sx32_bk1': mask_Sx32_bk1, 'L0_cond_Wq': _L0_cond_in['Wq'], 'L0_cond_bq': _L0_cond_in['bq'], 'L0_cond_Wk': _L0_cond_in['Wk'], 'L0_cond_bk': _L0_cond_in['bk'], 'L0_cond_Wv': _L0_cond_in['Wv'], 'L0_cond_bv': _L0_cond_in['bv'], 'L0_cond_Wo': _L0_cond_in['Wo'], 'L0_cond_bo': _L0_cond_in['bo'], 'L0_ffn_w1': _L0_ffn_in['w1'], 'L0_ffn_b1': _L0_ffn_in['b1'], 'L0_ffn_w2': _L0_ffn_in['w2'], 'L0_ffn_b2': _L0_ffn_in['b2'], 'L1_cond_fc1_w': _L1_cond_in['fc1_w'], 'L1_cond_fc1_b': _L1_cond_in['fc1_b'], 'L1_cond_fc2_w': _L1_cond_in['fc2_w'], 'L1_cond_fc2_b': _L1_cond_in['fc2_b'], 'L1_cond_experts_w': _L1_cond_in['experts_w'], 'L1_cond_experts_b': _L1_cond_in['experts_b'], 'L1_ffn_router_w': _L1_ffn_in['router_w'], 'L1_ffn_expert_weights': _L1_ffn_in['expert_weights']}

def reference(x, itok_Sx32_0_1023, condB_uprev, itok_B_0_15, mask_SxS_bk0, mask_Sx32_bk1, L0_cond_Wq, L0_cond_bq, L0_cond_Wk, L0_cond_bk, L0_cond_Wv, L0_cond_bv, L0_cond_Wo, L0_cond_bo, L0_ffn_w1, L0_ffn_b1, L0_ffn_w2, L0_ffn_b2, L1_cond_fc1_w, L1_cond_fc1_b, L1_cond_fc2_w, L1_cond_fc2_b, L1_cond_experts_w, L1_cond_experts_b, L1_ffn_router_w, L1_ffn_expert_weights):
    import jax
    import jax.numpy as jnp

    def _L0_cond_ref(x, prior_mask, prior_indices, prior_index_mask, u_prev, Wq, bq, Wk, bk, Wv, bv, Wo, bo):
        import jax, jax.numpy as jnp
        import numpy as np
        B, S, D, H = (4, 256, 256, 16)
        DH = D // H
        K_SPARSE = 32
        LAMBDA_MAX, ALPHA = (10.0, 5.0)
        SPARSE_THRESHOLD = 1.0
        Bb, Ss, Dd = x.shape
        scale = 1.0 / jnp.sqrt(jnp.asarray(DH, x.dtype))

        def proj(W, b):
            return (x @ W.T + b).reshape(Bb, Ss, H, DH).transpose(0, 2, 1, 3)
        Q, K, V = (proj(Wq, bq), proj(Wk, bk), proj(Wv, bv))
        lam = LAMBDA_MAX * jnp.exp(-ALPHA * u_prev.reshape(Bb))
        use_sparse = lam >= SPARSE_THRESHOLD
        scores = jnp.einsum('bhqd,bhkd->bhqk', Q, K) * scale
        prior_bias = jnp.where(prior_mask[:Ss, :Ss], 0.0, -1.0).astype(x.dtype)
        bias = lam[:, None, None, None] * prior_bias[None, None]
        dense_out = jnp.einsum('bhqk,bhkd->bhqd', jax.nn.softmax(scores + bias, axis=-1), V)
        idx = prior_indices[:Ss]
        Kg = K[:, :, idx]
        Vg = V[:, :, idx]
        s_scores = jnp.einsum('bhsd,bhskd->bhsk', Q, Kg) * scale
        s_scores = jnp.where(prior_index_mask[:Ss][None, None], s_scores, jnp.asarray(-jnp.inf, x.dtype))
        sparse_out = jnp.einsum('bhsk,bhskd->bhsd', jax.nn.softmax(s_scores, axis=-1), Vg)
        out = jnp.where(use_sparse[:, None, None, None], sparse_out, dense_out)
        out = out.transpose(0, 2, 1, 3).reshape(Bb, Ss, Dd)
        return out @ Wo.T + bo

    def _L0_ffn_ref(x, w1, b1, w2, b2):
        import jax, jax.numpy as jnp
        import numpy as np
        B, S, D = (4, 512, 256)
        N_EXPERTS, EXPERT_SIZE = (16, 64)
        WIDTH = N_EXPERTS * EXPERT_SIZE
        h = jax.nn.relu(jnp.einsum('bsd,dw->bsw', x, w1) + b1)
        return jnp.einsum('bsw,wd->bsd', h, w2) + b2

    def _L1_cond_ref(x, indices, fc1_w, fc1_b, fc2_w, fc2_b, experts_w, experts_b):
        import jax, jax.numpy as jnp
        import numpy as np
        B, N, DIM = (32, 256, 256)
        HID = 1024
        PART = 64
        OUT = 256
        SHARED = OUT - PART
        E = 16
        h = jax.nn.gelu(jnp.einsum('bnd,hd->bnh', x, fc1_w) + fc1_b, approximate=False)
        shared = jnp.einsum('bnh,sh->bns', h, fc2_w) + fc2_b
        We = experts_w[indices]
        be = experts_b[indices]
        expert_x = jnp.einsum('bnh,bph->bnp', h, We) + be[:, None, :]
        return jnp.concatenate([shared, expert_x], axis=-1)

    def _L1_ffn_ref(hidden_states, router_w, expert_weights):
        import jax, jax.numpy as jnp
        import numpy as np
        K_TOP = 2
        B, S, H = hidden_states.shape
        x = hidden_states.reshape(-1, H)
        logits = x @ router_w.T
        probs = jax.nn.softmax(logits, axis=-1)
        topk_vals, topk_idx = jax.lax.top_k(probs, K_TOP)
        topk_w = topk_vals / (topk_vals.sum(-1, keepdims=True) + 1e-06)
        expert_out = jnp.einsum('nh,eho->eno', x, expert_weights)
        combined = jnp.take_along_axis(expert_out.transpose(1, 0, 2), topk_idx[:, :, None], axis=1)
        combined = combined.transpose(1, 0, 2)
        remap_bias = jnp.take_along_axis(probs, topk_idx, axis=1).T[:, :, None]
        weights = topk_w.T[:, :, None]
        out = ((combined + remap_bias) * weights).sum(axis=0)
        return out.reshape(B, S, H)
    x = x + _L0_ffn_ref(_L0_cond_ref(x, mask_SxS_bk0, itok_Sx32_0_1023, mask_Sx32_bk1, condB_uprev[:, None], L0_cond_Wq, L0_cond_bq, L0_cond_Wk, L0_cond_bk, L0_cond_Wv, L0_cond_bv, L0_cond_Wo, L0_cond_bo), L0_ffn_w1, L0_ffn_b1, L0_ffn_w2, L0_ffn_b2)
    x = x + _L1_ffn_ref(_L1_cond_ref(x, itok_B_0_15, L1_cond_fc1_w, L1_cond_fc1_b, L1_cond_fc2_w, L1_cond_fc2_b, L1_cond_experts_w, L1_cond_experts_b), L1_ffn_router_w, L1_ffn_expert_weights)
    return x

_drawn_inputs = setup_inputs


def setup_inputs(seed=0):
    import zlib

    import numpy as np

    out = dict(_drawn_inputs(seed))
    spreads = {'L0_cond_bq': (0.0, 0.504),
     'L0_cond_bk': (0.0, 0.8),
     'L0_cond_bv': (0.0, 0.1),
     'L0_cond_bo': (0.0, 0.1),
     'L0_ffn_b1': (0.0, 0.1),
     'L0_ffn_b2': (0.0, 0.1),
     'L1_cond_fc1_b': (0.0, 0.417),
     'L1_cond_fc2_b': (0.0, 0.1),
     'L1_cond_experts_b': (0.0, 0.374)}
    factors = {'L1_cond_experts_w': 2.67}
    for name, (base, spread) in spreads.items():
        noise = np.random.default_rng([zlib.crc32(name.encode()), seed]).standard_normal(out[name].shape)
        drawn = base * np.exp(spread * noise) if base else spread * noise
        out[name] = jnp.asarray(drawn.astype(out[name].dtype))
    for name, factor in factors.items():
        out[name] = (out[name] * factor).astype(out[name].dtype)
    return out
```

```python
import concourse.bass as bass
from concourse import mybir
from contextlib import ExitStack
import numpy as np

F32 = mybir.dt.float32
F32R = mybir.dt.float32r
F16 = mybir.dt.float16
BF16 = mybir.dt.bfloat16
I32 = mybir.dt.int32
U8 = mybir.dt.uint8
U32 = mybir.dt.uint32
ALU = mybir.AluOpType
ACT = mybir.ActivationFunctionType
AX = mybir.AxisListType

P = 128
B, S, D, H = 2, 1024, 256, 16
DH = D // H
K_SPARSE = 32
N = B * S
KD = D // P
WIDTH = 1024
KW = WIDTH // P
SHARED = 192
PART = D - SHARED
NE = 8
HG = 4
GROUPS = H // HG
AUG = 64
VW = 32
VC = DH + 1
LAMBDA_MAX, ALPHA = 10.0, 5.0
SCALE = 1.0 / 4.0
BIG = 1.0e30
FMAX = 3.0e38
QC = 512
CHUNKS = N // QC
UNITS = B * GROUPS
JOBS = 8
LAG = 10

C_ID, C_HM, C_SEL, C_E8, C_END = 0, 128, 136, 264, 272


class Shape:

    def __init__(self, keys):
        self.T = keys
        self.NT = keys // P
        self.SQ = 2048 * P // keys
        self.NQ = self.SQ // P
        self.NC = S // self.SQ
        self.NBK = keys // 256
        self.CP = min(512, self.SQ)
        self.NB = 2 if keys <= 256 else 1
        self.LEAD = 4 if self.NB == 2 else 0
        self.TP = min(self.NT, 4)
        self.QP = min(self.NQ, 4)


def bass_adaln_ffn(nc, io, out, general_only=True, fast_only=False):
    ctx = ExitStack()
    with ctx:
        def sb(name, shape, dt, at=ctx):
            return at.enter_context(nc.sbuf_tensor(name, shape, dt))

        def sem(name):
            return ctx.enter_context(nc.semaphore(name))

        cst = sb("cst", [P, C_END], F32)
        ident, headmask, sel, iota8 = (cst[:, C_ID:C_ID + P], cst[:, C_HM:C_HM + 8],
                                       cst[:, C_SEL:C_SEL + P], cst[:, C_E8:C_E8 + 8])
        xT = sb("xT", [P, KD, N], F32)
        attT = sb("attT", [P, GROUPS, N], F32)
        cols = sb("cols", [P, 20], F32)
        cbias = sb("cbias", [P, B, KD], F32)
        small = sb("small", [1, 8], I32)

        PS = [ctx.enter_context(nc.psum_tensor(f"bank{i}", [P, 512], F32)) for i in range(0)]
        psG = ctx.enter_context(nc.psum_tensor("psG", [P, 2, 512], F32))
        psS = ctx.enter_context(nc.psum_tensor("psS", [P, 2, 512], F32))
        psO = ctx.enter_context(nc.psum_tensor("psO", [P, 2, 512], F32))
        psM = ctx.enter_context(nc.psum_tensor("psM", [P, 2, 512], F32))
        RING = [psG[:, 0, :], psG[:, 1, :], psS[:, 0, :], psS[:, 1, :]]

        actx = ExitStack()
        shapes = [Shape(1024)] if general_only else [Shape(256)] if fast_only else [Shape(256), Shape(1024)]
        wqkv = sb("wqkv", [P, KD, 3 * D], F32, actx)
        bqkv = sb("bqkv", [P, 3 * D], F32, actx)
        idm = sb("idm", [P, S // P, K_SPARSE // 4], I32, actx)
        idx1 = sb("idx1", [P, S // P, K_SPARSE], F32, actx)
        iota16 = sb("iota16", [P, 1024], F16, actx)
        ident16 = sb("ident16", [P, P], F16, actx)
        identm = sb("identm", [P, B, P], BF16, actx)
        lam = sb("lam", [P, 6, B], F32, actx)
        Pr = sb("Pr", [P, 2 * HG, 1024], F32, actx)
        W = sb("W", [P, 2048], F32, actx)
        ramp = W[:, 0:1024]
        idx = W[:, 1024:1280].bitcast(I32).rearrange("p (q k) -> p q k", k=K_SPARSE)
        idmf = W[:, 1280:1536].rearrange("p (q k) -> p q k", k=K_SPARSE)
        Mneg = sb("Mneg", [P, 2048], BF16, actx)
        shift = sb("shift", [P, 2, HG], F32, actx)
        shiftb = sb("shiftb", [P, HG, 4], F32, actx)
        Qa = sb("Qa", [P, 2, HG, AUG], F32R, actx)
        Ka = sb("Ka", [P, 2, HG, AUG], F32R, actx)

        L = {k: sem("ld_" + k) for k in ("cst", "x", "wqkv", "idx", "u", "small", "cols", "mask", "wo", "w1")}
        s = {k: sem(k) for k in (
            "consts_ready", "idx_ready", "lam_exp", "self_dve", "self_pool", "cleared", "zeroed",
            "kv_full", "kv_out", "q_full", "q_out",
            "eq_ready", "cnt_full", "eq_used", "cnt_out", "cntT_full", "cntT_out",
            "bias_exp", "w_ready",
            "qg_full", "qg_out", "kt_full", "kt_out", "kg_ready",
            "ka_ready", "ka_full", "kp_out", "qa_split", "qa_shift", "qa_full", "qat_out",
            "g_scores", "g_max", "s_scores", "s_exp", "s_prob", "pv_done",
            "ot_out", "den_full", "recip", "att_ready")}

        def setup_pool(pool):
            nc.gpsimd.memset(Qa[:, :, :, :].bitcast(F32), 0.0).then_inc(s["cleared"], 1)
            nc.gpsimd.memset(Ka[:, :, :, :].bitcast(F32), 0.0).then_inc(s["cleared"], 1)
            pool.wait_ge(s["cleared"], 2)
            nc.gpsimd.memset(Ka[:, :, :, 48:50].bitcast(F32), 1.0).then_inc(s["cleared"], 1)

        def setup_dve(dve):
            dve.wait_ge(L["cst"], 32)
            nc.vector.tensor_copy(iota16[:, :], ramp).then_inc(s["consts_ready"], 1)
            nc.vector.tensor_copy(ident16[:, :], ident).then_inc(s["consts_ready"], 1)
            dve.wait_ge(L["idx"], 32)
            nc.vector.tensor_copy(idmf, idm[:, :, :].bitcast(U8)).then_inc(s["self_dve"], 1)
            nc.vector.tensor_copy(idx1[:, :, :], idx).then_inc(s["self_dve"], 1)
            dve.wait_ge(s["self_dve"], 2)
            nc.vector.scalar_tensor_tensor(idx1[:, :, :], idx1[:, :, :], 1.0, idmf,
                                           ALU.add, ALU.mult).then_inc(s["idx_ready"], 1)
            dve.wait_ge(s["lam_exp"], 1)
            nc.vector.tensor_scalar(lam[:, 1, :], lam[:, 1, :], LAMBDA_MAX, None, ALU.mult).then_inc(s["self_dve"], 1)
            dve.wait_ge(s["self_dve"], 3)
            nc.vector.tensor_scalar(lam[:, 2, :], lam[:, 1, :], 1.0, None, ALU.is_ge).then_inc(s["self_dve"], 1)
            nc.vector.tensor_scalar(lam[:, 3, :], lam[:, 1, :], 1.0, None, ALU.min).then_inc(s["self_dve"], 1)
            nc.vector.tensor_scalar(lam[:, 4, :], lam[:, 1, :], 1.0, -1.0, ALU.min, ALU.mult).then_inc(s["self_dve"], 1)
            dve.wait_ge(s["self_dve"], 6)
            nc.vector.tensor_scalar(lam[:, 5, :], lam[:, 2, :], -1.0, 1.0, ALU.mult, ALU.add).then_inc(s["self_dve"], 1)
            for b in range(B):
                nc.vector.tensor_scalar(identm[:, b, :], ident, lam[:, 2, b:b + 1], None,
                                        ALU.mult).then_inc(s["consts_ready"], 1)
            dve.wait_ge(s["self_dve"], 7)

        def setup_act(act):
            act.wait_ge(L["u"], 16)
            nc.scalar.activation(lam[:, 1, :], lam[:, 0, :], ACT.Exp, scale=-ALPHA).then_inc(s["lam_exp"], 1)

        class Attention:

            def __init__(self, sh, tag, at):
                self.sh = sh
                self.Kn = sb("Kn" + tag, [P, B, sh.NT, D], F32, at)
                self.VA = sb("VA" + tag, [P, B, sh.NT, H * VC], F32, at)
                self.Qn = sb("Qn" + tag, [P, B, sh.NQ, D], F32, at)
                self.QG = sb("QG" + tag, [P, 2, sh.SQ], F32R, at)
                self.KT = sb("KT" + tag, [P, sh.T], F32, at)
                self.KG = sb("KG" + tag, [P, sh.NB, HG, sh.T], F32R, at)
                self.KP = sb("KP" + tag, [P, sh.NB, HG, sh.T], F32R, at)
                self.QAT = sb("QAT" + tag, [P, 2, 2, sh.SQ], F32R, at)
                self.OTs = sb("OTs" + tag, [P, sh.SQ], F32, at)
                self.Rr = sb("Rr" + tag, [P, sh.SQ], F32, at)
                self.NE = 4 if sh.NB == 2 else 2
                self.EQ = sb("EQ" + tag, [P, self.NE, sh.T], F16, at)
                self.Cn = sb("Cn" + tag, [P, sh.T], F32, at)
                self.dense = sh.T == S
                if self.dense:
                    self.CT = sb("CT" + tag, [P, 2048], BF16, at)
                    self.maskT = sb("maskT" + tag, [P, 512], I32, at)
                else:
                    self.CT = W

            def due(self, c):
                sh = self.sh
                n_jobs = UNITS * JOBS
                for t in range(-sh.LEAD, n_jobs + LAG + 11):
                    n = t - LAG
                    if (t + sh.LEAD) % JOBS == 0 and 0 <= (t + sh.LEAD) // JOBS < UNITS:
                        yield "guard_keys", (t + sh.LEAD) // JOBS
                    if (n + sh.LEAD) % JOBS == 0 and 0 <= (n + sh.LEAD) // JOBS < UNITS:
                        yield "score_keys", (n + sh.LEAD) // JOBS
                    if 1 <= t <= n_jobs and t % sh.NBK == 0:
                        yield "query_rows", t // sh.NBK - 1
                    if 0 <= t < n_jobs:
                        yield "guard", t
                    if 0 <= n < n_jobs:
                        yield "score", n
                    if n >= 5 and (n - 5) % HG == 0 and (n - 5) // HG < 2 * UNITS:
                        yield "values", (n - 5) // HG
                    if n >= 10 and (n - 10) % JOBS == 0 and (n - 10) // JOBS < UNITS:
                        yield "norm", (n - 10) // JOBS

            def pool(self, pool):
                sh = self.sh
                for c in range(sh.NC):
                    for what, i in self.due(c):
                        if what == "guard_keys":
                            g = i % GROUPS
                            ug = c * UNITS + i
                            pool.wait_ge(s["kt_out"], (ug // 2 + 1) * (sh.NT // sh.TP))
                            if ug >= sh.NB:
                                pool.wait_ge(s["g_scores"], JOBS * (ug - sh.NB + 1))
                            hm = headmask[:, HG * (g % 2):HG * (g % 2) + HG]
                            nc.gpsimd.tensor_tensor(
                                self.KG[:, ug % sh.NB, :, :],
                                self.KT[:, None, :].to_broadcast([P, HG, sh.T]),
                                hm[:, :, None].to_broadcast([P, HG, sh.T]), ALU.mult).then_inc(s["kg_ready"], 1)
                        if what == "score_keys":
                            b, g = divmod(i, GROUPS)
                            ug = c * UNITS + i
                            for tt in range(sh.NT):
                                m = ug * sh.NT + tt
                                if m >= 2:
                                    pool.wait_ge(s["ka_full"], m - 1)
                                k = self.Kn[:, b, tt, g * HG * DH:(g + 1) * HG * DH].rearrange("p (h d) -> p h d", d=DH)
                                ka = Ka[:, m % 2, :, :]
                                nc.gpsimd.tensor_copy(ka[:, :, 0:16], k).then_inc(s["self_pool"], 1)
                                nc.gpsimd.tensor_copy(ka[:, :, 32:48], k)
                                self.np += 1
                                pool.wait_ge(s["self_pool"], self.np)
                                nc.gpsimd.tensor_tensor(ka[:, :, 16:32], k, ka[:, :, 0:16].bitcast(F32),
                                                        ALU.subtract).then_inc(s["ka_ready"], 1)
                        if what == "guard" and i % sh.NBK == 0:
                            u = i // JOBS
                            b, g = divmod(u, GROUPS)
                            m = c * UNITS * sh.NQ + i // sh.NBK
                            st = m % sh.NQ
                            if m >= 2:
                                pool.wait_ge(s["qa_full"], m - 1)
                            pool.wait_ge(s["q_out"], (c + 1) * B * sh.NQ)
                            q = self.Qn[:, b, st, g * HG * DH:(g + 1) * HG * DH].rearrange("p (h d) -> p h d", d=DH)
                            qa = Qa[:, m % 2, :, :]
                            nc.gpsimd.tensor_copy(qa[:, :, 0:16], q).then_inc(s["self_pool"], 1)
                            nc.gpsimd.tensor_copy(qa[:, :, 16:32], q)
                            self.np += 1
                            pool.wait_ge(s["self_pool"], self.np)
                            nc.gpsimd.tensor_tensor(qa[:, :, 32:48], q, qa[:, :, 0:16].bitcast(F32),
                                                    ALU.subtract).then_inc(s["qa_split"], 1)

            def tensor(self, pe):
                sh = self.sh
                log = []

                def misc(kind, n):
                    if len(log) >= 2:
                        pe.wait_ge(s[log[-2][0]], log[-2][1] + 1)
                    log.append((kind, n))
                    return psM[:, len(log) % 2, :]

                pe.wait_ge(L["cst"], 32)
                pe.wait_ge(L["x"], 16)
                pe.wait_ge(L["wqkv"], 32)
                for m in range(B * sh.NT):
                    b, tt = divmod(m, sh.NT)
                    if m >= 4:
                        pe.wait_ge(s["kv_out"], m - 3)
                    for k in range(KD):
                        mm = nc.tensor.matmul(RING[m % 4], xT[:, k, b * S + tt * P:b * S + tt * P + P],
                                              wqkv[:, k, D:3 * D], start=(k == 0), stop=(k == KD - 1))
                    mm.then_inc(s["kv_full"], 1)
                pe.wait_ge(s["consts_ready"], 2 + B)
                for c in range(sh.NC):
                    u0 = c * UNITS
                    pe.wait_ge(s["kv_out"], B * sh.NT)
                    if c:
                        pe.wait_ge(s["g_max"], JOBS * u0)
                        pe.wait_ge(s["s_exp"], JOBS * u0)
                    for i in range(B * sh.NQ):
                        m = c * B * sh.NQ + i
                        b, st = divmod(i, sh.NQ)
                        if i >= 4:
                            pe.wait_ge(s["q_out"], m - 3)
                        t0 = b * S + c * sh.SQ + st * P
                        for k in range(KD):
                            mm = nc.tensor.matmul(RING[i % 4][:, 0:D], xT[:, k, t0:t0 + P],
                                                  wqkv[:, k, 0:D], start=(k == 0), stop=(k == KD - 1))
                        mm.then_inc(s["q_full"], 1)
                    if c:
                        pe.wait_ge(s["recip"], u0)
                    pe.wait_ge(s["zeroed"], 3)
                    for i in range(sh.NQ):
                        m = c * sh.NQ + i
                        if i:
                            pe.wait_ge(s["cnt_out"], 2 * m)
                        for k in range(K_SPARSE):
                            e = m * K_SPARSE + k
                            pe.wait_ge(s["eq_ready"], e + 1)
                            for f in range(0, sh.T, 512):
                                w = min(512, sh.T)
                                mm = nc.tensor.matmul(psO[:, f // 512, 0:w], ident16[:, :],
                                                      self.EQ[:, e % self.NE, f:f + w],
                                                      start=(k == 0), stop=(k == K_SPARSE - 1))
                            mm.then_inc(s["eq_used"], 1)
                        pe.wait_ge(s["cnt_out"], 2 * (m + 1))
                        for t4 in range(0, sh.NT, sh.TP):
                            ps = misc("cntT_out", m * (sh.NT // sh.TP) + t4 // sh.TP)
                            for j in range(sh.TP):
                                mm = nc.tensor.transpose(ps[:, j * P:j * P + P],
                                                         self.Cn[:, (t4 + j) * P:(t4 + j + 1) * P], ident)
                            mm.then_inc(s["cntT_full"], 1)
                    pe.wait_ge(s["q_out"], (c + 1) * B * sh.NQ)
                    for what, i in self.due(c):
                        u = i // JOBS
                        if what == "guard_keys":
                            b, g = divmod(i, GROUPS)
                            ug = u0 + i
                            half = ug // 2
                            if g % 2 == 0:
                                for q4 in range(0, sh.NQ, sh.QP):
                                    ps = misc("qg_out", half * (sh.NQ // sh.QP) + q4 // sh.QP)
                                    for j in range(sh.QP):
                                        mm = nc.tensor.transpose(ps[:, j * P:j * P + P],
                                                                 self.Qn[:, b, q4 + j, (g // 2) * P:(g // 2) * P + P], ident)
                                    mm.then_inc(s["qg_full"], 1)
                                for t4 in range(0, sh.NT, sh.TP):
                                    ps = misc("kt_out", half * (sh.NT // sh.TP) + t4 // sh.TP)
                                    for j in range(sh.TP):
                                        mm = nc.tensor.transpose(ps[:, j * P:j * P + P],
                                                                 self.Kn[:, b, t4 + j, (g // 2) * P:(g // 2) * P + P], ident)
                                    mm.then_inc(s["kt_full"], 1)
                        if what == "score_keys":
                            for tt in range(sh.NT):
                                m = (u0 + i) * sh.NT + tt
                                pe.wait_ge(s["ka_ready"], m + 1)
                                ps = misc("kp_out", m)
                                for p in range(2):
                                    mm = nc.tensor.transpose(ps[:, p * P:p * P + P],
                                                             Ka[:, m % 2, 2 * p:2 * p + 2, :].rearrange("p h a -> p (h a)").bitcast(F32), ident)
                                mm.then_inc(s["ka_full"], 1)
                        if what == "query_rows":
                            m = u0 * sh.NQ + i
                            pe.wait_ge(s["qa_split"], m + 1)
                            pe.wait_ge(s["qa_shift"], m + 1)
                            ps = misc("qat_out", m)
                            for p in range(2):
                                mm = nc.tensor.transpose(ps[:, p * P:p * P + P],
                                                         Qa[:, m % 2, 2 * p:2 * p + 2, :].rearrange("p h a -> p (h a)").bitcast(F32), ident)
                            mm.then_inc(s["qa_full"], 1)
                        if what == "guard":
                            b, g = divmod(u, GROUPS)
                            ug = u0 + u
                            st, blk = divmod(i % JOBS, sh.NBK)
                            pe.wait_ge(s["kg_ready"], ug + 1)
                            pe.wait_ge(s["qg_out"], (ug // 2 + 1) * (sh.NQ // sh.QP))
                            if u0 * JOBS + i >= 1:
                                pe.wait_ge(s["g_max"], u0 * JOBS + i)
                            for p in range(2):
                                o = psG[:, p, :].rearrange("p (h t) -> p h t", h=2)
                                nc.tensor.matmul(o, self.QG[:, (ug // 2) % 2, st * P:st * P + P],
                                                 self.KG[:, ug % sh.NB, 2 * p:2 * p + 2, blk * 256:blk * 256 + 256],
                                                 start=True, stop=False)
                                a = st * sh.T + blk * 256
                                mm = nc.tensor.matmul(o, identm[:, b, :],
                                                      Mneg[:, None, a:a + 256].to_broadcast([P, 2, 256]),
                                                      start=False, stop=True)
                            mm.then_inc(s["g_scores"], 1)
                        if what == "score":
                            ug = u0 + u
                            r, j = divmod(i % JOBS, HG)
                            pe.wait_ge(s["kp_out"], (ug + 1) * sh.NT)
                            pe.wait_ge(s["qat_out"], (ug + 1) * sh.NQ)
                            if u0 * JOBS + i >= 1:
                                pe.wait_ge(s["s_exp"], u0 * JOBS + i)
                            flat = psS[:, :, :].rearrange("p a b -> p (a b)")
                            for f in range(0, 1024, sh.CP):
                                tt, q = divmod(r * 1024 + f, sh.SQ)
                                mm = nc.tensor.matmul(flat[:, f:f + sh.CP],
                                                      self.KP[:, ug % sh.NB, j, tt * P:tt * P + P],
                                                      self.QAT[:, ug % 2, j // 2, q:q + sh.CP], start=True, stop=True)
                            mm.then_inc(s["s_scores"], 1)
                        if what == "values":
                            v = 2 * u0 + i
                            ug, r = divmod(v, 2)
                            b, g = divmod(i // 2, GROUPS)
                            pe.wait_ge(s["s_prob"], HG * (v + 1))
                            if r == 0 and ug:
                                pe.wait_ge(s["recip"], ug)
                            for f in range(0, 1024, sh.CP):
                                tt, q = divmod(r * 1024 + f, sh.SQ)
                                for j in range(HG):
                                    h = g * HG + j
                                    mm = nc.tensor.matmul(
                                        psO[VW * j:VW * j + VC, q // 512, q % 512:q % 512 + sh.CP],
                                        self.VA[:, b, tt, h * VC:h * VC + VC], Pr[:, HG * r + j, f:f + sh.CP],
                                        start=(tt == 0), stop=(tt == sh.NT - 1), tile_position=(0, VW * j))
                            mm.then_inc(s["pv_done"], 1)
                        if what == "norm":
                            ug = u0 + i
                            pe.wait_ge(s["ot_out"], ug + 1)
                            for q in range(0, sh.SQ, sh.CP):
                                mm = nc.tensor.matmul(psO[:, q // 512, 0:sh.CP], sel, self.OTs[:, q:q + sh.CP],
                                                      start=True, stop=True)
                            mm.then_inc(s["den_full"], 1)

            def act(self, act):
                sh = self.sh
                act.wait_ge(s["zeroed"], 3)
                mi = 0

                def misc():
                    nonlocal mi
                    mi += 1
                    return psM[:, mi % 2, :]

                for c in range(sh.NC):
                    u0 = c * UNITS
                    for i in range(sh.NQ):
                        m = c * sh.NQ + i
                        for t4 in range(0, sh.NT, sh.TP):
                            act.wait_ge(s["cntT_full"], m * (sh.NT // sh.TP) + t4 // sh.TP + 1)
                            if self.dense and c and i == 0 and t4 == 0:
                                act.wait_ge(s["w_ready"], B * c)
                            ct = self.CT[:, :].rearrange("p (t q) -> p t q", q=sh.SQ)
                            nc.scalar.copy(ct[:, t4:t4 + sh.TP, i * P:i * P + P],
                                           misc()[:, 0:sh.TP * P].rearrange("p (t q) -> p t q", q=P)).then_inc(s["cntT_out"], 1)
                    for what, i in self.due(c):
                        u = i // JOBS
                        if what == "guard_keys" and i % 2 == 0:
                            ug = u0 + i
                            half = ug // 2
                            if half >= 2:
                                act.wait_ge(s["g_scores"], JOBS * 2 * (half - 1))
                            for q4 in range(0, sh.NQ, sh.QP):
                                act.wait_ge(s["qg_full"], half * (sh.NQ // sh.QP) + q4 // sh.QP + 1)
                                nc.scalar.copy(self.QG[:, half % 2, q4 * P:(q4 + sh.QP) * P],
                                               misc()[:, 0:sh.QP * P]).then_inc(s["qg_out"], 1)
                            if ug:
                                act.wait_ge(s["kg_ready"], ug)
                            for t4 in range(0, sh.NT, sh.TP):
                                act.wait_ge(s["kt_full"], half * (sh.NT // sh.TP) + t4 // sh.TP + 1)
                                nc.scalar.copy(self.KT[:, t4 * P:(t4 + sh.TP) * P],
                                               misc()[:, 0:sh.TP * P]).then_inc(s["kt_out"], 1)
                        if what == "score_keys":
                            ug = u0 + i
                            if ug >= sh.NB:
                                act.wait_ge(s["s_scores"], JOBS * (ug - sh.NB + 1))
                            for tt in range(sh.NT):
                                act.wait_ge(s["ka_full"], ug * sh.NT + tt + 1)
                                ps = misc()[:, 0:2 * P].rearrange("p (a t) -> p a t", t=P)
                                kp = self.KP[:, ug % sh.NB, :, tt * P:tt * P + P]
                                nc.scalar.copy(kp[0:AUG, 0::2, :], ps[0:AUG, :, :])
                                nc.scalar.copy(kp[AUG:P, 1::2, :], ps[AUG:P, :, :]).then_inc(s["kp_out"], 1)
                        if what == "query_rows":
                            m = u0 * sh.NQ + i
                            ug, st = divmod(m, sh.NQ)
                            act.wait_ge(s["qa_full"], m + 1)
                            if ug >= 2 and st == 0:
                                act.wait_ge(s["s_scores"], JOBS * (ug - 1))
                            ps = misc()[:, 0:2 * P].rearrange("p (a t) -> p a t", t=P)
                            nc.scalar.copy(self.QAT[:, ug % 2, :, st * P:st * P + P], ps).then_inc(s["qat_out"], 1)
                        if what == "score":
                            n = u0 * JOBS + i
                            if self.dense and i % (GROUPS * JOBS) == 0:
                                b = i // (GROUPS * JOBS)
                                k = c * B + b
                                act.wait_ge(L["mask"], 16 * (c + 1))
                                act.wait_ge(s["idx_ready"], 1)
                                if k:
                                    act.wait_ge(s["s_prob"], k * GROUPS * JOBS)
                                nc.scalar.activation(W[:, :], self.maskT[:, :].bitcast(U8), ACT.Exp, bias=lam[:, 4, b:b + 1],
                                                     scale=lam[:, 3, b:b + 1]).then_inc(s["bias_exp"], 1)
                            act.wait_ge(s["s_scores"], n + 1)
                            if n >= JOBS:
                                act.wait_ge(s["pv_done"], (n - JOBS) // HG + 1)
                            nc.scalar.activation(Pr[:, n % JOBS, :], psS[:, :, :].rearrange("p a b -> p (a b)"),
                                                 ACT.Exp, scale=SCALE).then_inc(s["s_exp"], 1)
                        if what == "norm":
                            ug = u0 + i
                            act.wait_ge(s["pv_done"], 2 * (ug + 1))
                            if ug:
                                act.wait_ge(s["att_ready"], ug)
                            nc.scalar.copy(self.OTs[:, 0:sh.SQ], psO[:, :, :].rearrange("p a b -> p (a b)")[:, 0:sh.SQ]
                                           ).then_inc(s["ot_out"], 1)

            def vector(self, dve):
                sh = self.sh
                nc.vector.memset(self.KP[:, :, :, :].bitcast(F32), 0.0).then_inc(s["zeroed"], 1)
                va = self.VA[:, :, :, :].rearrange("p b t (h w) -> p (b t) h w", w=VC)
                nc.vector.memset(va[:, :, :, DH:VC], 1.0).then_inc(s["zeroed"], 1)
                nc.vector.memset(psO[:, :, :], 0.0).then_inc(s["zeroed"], 1)
                for m in range(B * sh.NT):
                    b, tt = divmod(m, sh.NT)
                    dve.wait_ge(s["kv_full"], m + 1)
                    nc.vector.tensor_tensor(self.Kn[:, b, tt, :], RING[m % 4][:, 0:D], bqkv[:, D:2 * D], ALU.add)
                    nc.vector.tensor_tensor(va[:, m, :, 0:DH],
                                            RING[m % 4][:, D:2 * D].rearrange("p (h d) -> p h d", d=DH),
                                            bqkv[:, 2 * D:3 * D].rearrange("p (h d) -> p h d", d=DH),
                                            ALU.add).then_inc(s["kv_out"], 1)
                for c in range(sh.NC):
                    u0 = c * UNITS
                    for i in range(B * sh.NQ):
                        m = c * B * sh.NQ + i
                        b, st = divmod(i, sh.NQ)
                        dve.wait_ge(s["q_full"], m + 1)
                        if c and i == 0:
                            dve.wait_ge(s["qa_split"], u0 * sh.NQ)
                            dve.wait_ge(s["qg_full"], u0 // 2 * (sh.NQ // sh.QP))
                        nc.vector.tensor_tensor(self.Qn[:, b, st, :], RING[i % 4][:, 0:D], bqkv[:, 0:D],
                                                ALU.add).then_inc(s["q_out"], 1)
                    for i in range(sh.NQ):
                        m = c * sh.NQ + i
                        for k in range(K_SPARSE):
                            e = m * K_SPARSE + k
                            if e >= self.NE:
                                dve.wait_ge(s["eq_used"], e - self.NE + 1)
                            nc.vector.tensor_scalar(self.EQ[:, e % self.NE, :], iota16[:, 0:sh.T], idx1[:, m, k:k + 1], None,
                                                    ALU.is_equal).then_inc(s["eq_ready"], 1)
                        dve.wait_ge(s["eq_used"], (m + 1) * K_SPARSE)
                        if m:
                            dve.wait_ge(s["cntT_full"], m * (sh.NT // sh.TP))
                        cnt = psO[:, :, :].rearrange("p a b -> p (a b)")[:, 0:sh.T]
                        nc.vector.tensor_copy(self.Cn[:, :], cnt).then_inc(s["cnt_out"], 1)
                        nc.vector.tensor_scalar(Mneg[:, i * sh.T:(i + 1) * sh.T], cnt, 0.0, -BIG, ALU.is_equal,
                                                ALU.mult).then_inc(s["cnt_out"], 1)
                    for what, i in self.due(c):
                        u = i // JOBS
                        if what == "guard":
                            gj = u0 * JOBS + i
                            st_, blk = divmod(gj, sh.NBK)
                            dve.wait_ge(s["g_scores"], gj + 1)
                            src = psG[:, :, :].rearrange("p a (h t) -> p (a h) t", h=2)
                            last = blk == sh.NBK - 1
                            if sh.NBK == 1:
                                dst = shift[:, st_ % 2, :]
                            else:
                                dst = shiftb[:, :, blk]
                            nc.vector.tensor_reduce(dst, src, AX.X, ALU.max, negate=True).then_inc(s["g_max"], 1)
                            if last:
                                dve.wait_ge(s["g_max"], gj + 1)
                                if sh.NBK > 1:
                                    nc.vector.tensor_reduce(shift[:, st_ % 2, :], shiftb[:, :, :], AX.X,
                                                            ALU.min).then_inc(s["self_dve"], 1)
                                    self.nd += 1
                                    dve.wait_ge(s["self_dve"], self.nd)
                                if st_ >= 2:
                                    dve.wait_ge(s["qa_full"], st_ - 1)
                                if st_ < 2:
                                    dve.wait_ge(s["cleared"], 3)
                                qa = Qa[:, st_ % 2, :, :]
                                nc.vector.tensor_copy(qa[:, :, 48], shift[:, st_ % 2, :]).then_inc(s["self_dve"], 1)
                                self.nd += 1
                                dve.wait_ge(s["self_dve"], self.nd)
                                nc.vector.tensor_tensor(qa[:, :, 49], shift[:, st_ % 2, :],
                                                        qa[:, :, 48].bitcast(F32), ALU.subtract).then_inc(s["qa_shift"], 1)
                        if what == "score":
                            n = u0 * JOBS + i
                            r = (n % JOBS) // HG
                            if i % (GROUPS * JOBS) == 0:
                                dve.wait_ge(s["cntT_out"], (c + 1) * sh.NQ * (sh.NT // sh.TP))
                                if self.dense:
                                    b = i // (GROUPS * JOBS)
                                    dve.wait_ge(s["bias_exp"], c * B + b + 1)
                                    nc.vector.tensor_scalar(W[:, :], W[:, :], lam[:, 5, b:b + 1], None,
                                                            ALU.mult).then_inc(s["self_dve"], 1)
                                    self.nd += 1
                                    dve.wait_ge(s["self_dve"], self.nd)
                                    nc.vector.scalar_tensor_tensor(W[:, :], self.CT[:, :], lam[:, 2, b:b + 1], W[:, :],
                                                                   ALU.mult, ALU.add).then_inc(s["w_ready"], 1)
                                    dve.wait_ge(s["w_ready"], c * B + b + 1)
                            dve.wait_ge(s["s_exp"], n + 1)
                            pr = Pr[:, n % JOBS, :]
                            nc.vector.scalar_tensor_tensor(pr, pr, FMAX, W[:, r * 1024:r * 1024 + 1024], ALU.min,
                                                           ALU.mult).then_inc(s["s_prob"], 1)
                        if what == "norm":
                            ug = u0 + i
                            b, g = divmod(i, GROUPS)
                            dve.wait_ge(s["den_full"], ug + 1)
                            den = psO[:, :, :].rearrange("p a b -> p (a b)")[:, 0:sh.SQ]
                            nc.vector.reciprocal(self.Rr[:, :], den).then_inc(s["recip"], 1)
                            dve.wait_ge(s["recip"], ug + 1)
                            t0 = b * S + c * sh.SQ
                            nc.vector.tensor_tensor(attT[:, g, t0:t0 + sh.SQ], self.OTs[:, :], self.Rr[:, :],
                                                    ALU.mult).then_inc(s["att_ready"], 1)

        atts = []
        for n_, sh in enumerate(shapes):
            at = ExitStack()
            atts.append(Attention(sh, f"_{sh.T}", at))
            at.close()
        actx.close()

        WoT = sb("WoT", [P, GROUPS, D], F32)
        w1 = sb("w1", [P, KD, WIDTH], F32)
        w2 = sb("w2", [P, KW, D], F32)
        fc1 = sb("fc1", [P, KD, WIDTH], F32)
        Wc = sb("Wc", [P, B, KW, D], F32)
        rw = sb("rw", [P, KD, NE], F32)
        ew = sb("ew", [P, KD, NE * D], F32)
        aoT = sb("aoT", [P, 2, KD, QC], F32)
        hT = sb("hT", [P, 2, KW, QC], F32)
        x1T = sb("x1T", [P, 2, KD, QC], F32)
        cT = sb("cT", [P, 2, KD, QC], F32)
        top = sb("top", [P, 4, 8], F32)
        topi = sb("topi", [P, 4, 8], U32)
        rt = sb("rt", [P, 12, 4], F32)
        lg = sb("lg", [P, 4, 8], F32)
        dl = sb("dl", [P, 4, 8], F32)
        oh = sb("oh", [P, 2, 4, 8], F32)
        gate = sb("gate", [P, 2, 4, 8], F32)
        pw = sb("pw", [P, 2, 4], F32)
        y = sb("y", [P, 2, D], F32)
        LD = {k: sem("ld_" + k) for k in ("w2", "fc1", "wc", "rw", "ew")}
        d = {k: sem(k) for k in (
            "a_full", "a_out", "v_full", "v_out", "ao_out", "x1_out", "ct_out", "xn_full",
            "rt_full", "rt_out", "rt_exp", "rt_sub", "gate_ready", "ex_full", "ex_out", "y_ready", "stored0", "stored1")}
        TT = QC // P
        ABANK = RING
        VBANK = [psO[:, 0, :], psO[:, 1, :], psM[:, 0, :], psM[:, 1, :]]
        bo, b1, b2, f1b = cols[:, 0:2], cols[:, 2:10], cols[:, 10:12], cols[:, 12:20]
        STAGES = ("ao", "h", "y", "gelu", "c", "router", "experts")

        def dense_order():
            for pair in range(CHUNKS // 2):
                for stage in STAGES:
                    for c in (2 * pair, 2 * pair + 1):
                        yield stage, c

        def dense_jobs():
            na = nv = 0
            for stage, c in dense_order():
                if stage == "ao":
                    js = ["act"] * KD
                elif stage == "h":
                    js = ["act", "dve"] * (KW // 2)
                elif stage == "y":
                    js = ["dve"] * KD
                elif stage == "gelu":
                    js = ["act"] * KW
                elif stage == "c":
                    js = ["act"] * KD
                elif stage == "router":
                    js = ["dve"]
                else:
                    js = ["dve"] * (TT * 5)
                for i, e in enumerate(js):
                    if e == "act":
                        yield stage, c, i, e, na
                        na += 1
                    else:
                        yield stage, c, i, e, nv
                        nv += 1

        jobs = list(dense_jobs())
        upto = {}
        for stage, c, i, e, n in jobs:
            key = (stage, c, e)
            upto[key] = max(upto.get(key, 0), n + 1)
        n_att = UNITS * (1 if not general_only else 4)

        def dense_tensor(pe):
            pe.wait_ge(s["att_ready"], n_att)
            pe.wait_ge(L["wo"], 16)

            def bank(e, n):
                if n >= 4:
                    pe.wait_ge(d["a_out" if e == "act" else "v_out"], n - 3)
                return (ABANK if e == "act" else VBANK)[n % 4]

            def full(mm, e):
                mm.then_inc(d["a_full" if e == "act" else "v_full"], 1)

            def done(stage, c):
                for e, q in (("act", "a_out"), ("dve", "v_out")):
                    if (stage, c, e) in upto:
                        pe.wait_ge(d[q], upto[(stage, c, e)])

            loaded = set()

            def need(k, sm, v):
                if k not in loaded:
                    loaded.add(k)
                    pe.wait_ge(sm, v)

            pe.wait_ge(s["recip"], n_att)
            for stage, c, i, e, n in jobs:
                q = c % 2
                ps = bank(e, n)
                if stage == "ao":
                    for g in range(GROUPS):
                        mm = nc.tensor.matmul(ps, WoT[:, g, i * P:i * P + P], attT[:, g, c * QC:(c + 1) * QC],
                                              start=(g == 0), stop=(g == GROUPS - 1))
                if stage == "h":
                    need("w1", L["w1"], 16)
                    if i == 0:
                        done("ao", c)
                    for k in range(KD):
                        mm = nc.tensor.matmul(ps, w1[:, k, i * P:i * P + P], aoT[:, q, k, :],
                                              start=(k == 0), stop=(k == KD - 1))
                if stage == "y":
                    need("w2", LD["w2"], 16)
                    if i == 0:
                        done("h", c)
                    for k in range(KW):
                        mm = nc.tensor.matmul(ps, w2[:, k, i * P:i * P + P], hT[:, q, k, :],
                                              start=(k == 0), stop=(k == KW - 1))
                if stage == "gelu":
                    need("fc1", LD["fc1"], 16)
                    if i == 0:
                        done("y", c)
                    for k in range(KD):
                        mm = nc.tensor.matmul(ps, fc1[:, k, i * P:i * P + P], x1T[:, q, k, :],
                                              start=(k == 0), stop=(k == KD - 1))
                if stage == "c":
                    need("wc", LD["wc"], 16 * 2 * B)
                    if i == 0:
                        done("gelu", c)
                    for k in range(KW):
                        mm = nc.tensor.matmul(ps, Wc[:, c * QC // S, k, i * P:i * P + P], hT[:, q, k, :],
                                              start=(k == 0), stop=(k == KW - 1))
                if stage == "router":
                    need("rw", LD["rw"], 16)
                    done("c", c)
                    for t in range(TT):
                        for k in range(KD):
                            mm = nc.tensor.matmul(ps[:, t * NE:(t + 1) * NE], cT[:, q, k, t * P:t * P + P], rw[:, k, :],
                                                  start=(k == 0), stop=(k == KD - 1))
                if stage == "experts":
                    need("ew", LD["ew"], 16)
                    t, j = divmod(i, 5)
                    if j == 0:
                        for k in range(KD):
                            mm = nc.tensor.transpose(ps[:, k * P:k * P + P], x1T[:, q, k, t * P:t * P + P], ident)
                    else:
                        for k in range(KD):
                            mm = nc.tensor.matmul(ps, cT[:, q, k, t * P:t * P + P], ew[:, k, (j - 1) * 512:j * 512],
                                                  start=(k == 0), stop=(k == KD - 1))
                full(mm, e)

        def dense_act(act):
            act.wait_ge(L["cols"], 16)
            first_c = True
            for stage, c, i, e, n in jobs:
                q = c % 2
                ps = ABANK[n % 4]
                if stage == "router":
                    act.wait_ge(d["rt_sub"], c + 1)
                    nc.scalar.activation(dl[:, :, :], dl[:, :, :], ACT.Exp).then_inc(d["rt_exp"], 1)
                if e != "act":
                    continue
                act.wait_ge(d["a_full"], n + 1)
                if stage == "ao":
                    nc.scalar.activation(aoT[:, q, i, :], ps, ACT.Identity, bias=bo[:, i:i + 1]).then_inc(d["a_out"], 1)
                if stage == "h":
                    nc.scalar.activation(hT[:, q, i, :], ps, ACT.Relu, bias=b1[:, i:i + 1]).then_inc(d["a_out"], 1)
                if stage == "gelu":
                    nc.scalar.activation(hT[:, q, i, :], ps, ACT.Gelu, bias=f1b[:, i:i + 1]).then_inc(d["a_out"], 1)
                if stage == "c":
                    if first_c:
                        act.wait_ge(L["small"], 16 * 6)
                        first_c = False
                    nc.scalar.activation(cT[:, q, i, :], ps, ACT.Identity,
                                         bias=cbias[:, c * QC // S, i:i + 1]).then_inc(d["a_out"], 1)

        def dense_vector(dve):
            dve.wait_ge(L["cols"], 16)
            nd = [self_count[0]]

            def link(ins):
                nd[0] += 1
                ins.then_inc(s["self_dve"], 1)

            def settle():
                dve.wait_ge(s["self_dve"], nd[0])

            for stage, c, i, e, n in jobs:
                if e != "dve":
                    continue
                q = c % 2
                ps = VBANK[n % 4]
                dve.wait_ge(d["v_full"], n + 1)
                if stage == "h":
                    nc.vector.tensor_scalar(hT[:, q, i, :], ps, b1[:, i:i + 1], 0.0, ALU.add, ALU.max).then_inc(d["v_out"], 1)
                if stage == "y":
                    nc.vector.scalar_tensor_tensor(x1T[:, q, i, :], ps, b2[:, i:i + 1], xT[:, i, c * QC:(c + 1) * QC],
                                                   ALU.add, ALU.add).then_inc(d["v_out"], 1)
                if stage == "router":
                    if c:
                        dve.wait_ge(d["rt_exp"], c)
                    nc.vector.tensor_copy(lg[:, :, :], ps[:, 0:TT * NE].rearrange("p (t e) -> p t e", e=NE)).then_inc(d["v_out"], 1)
                    dve.wait_ge(d["v_out"], n + 1)
                    for t in range(TT):
                        link(nc.vector.max(top[:, t, :], lg[:, t, :]))
                    settle()
                    for t in range(TT):
                        link(nc.vector.max_index(topi[:, t, :], top[:, t, :], lg[:, t, :]))
                    nc.vector.tensor_tensor(dl[:, :, :], lg[:, :, :], top[:, :, 0:1].to_broadcast([P, TT, NE]),
                                            ALU.subtract).then_inc(d["rt_sub"], 1)
                    settle()
                    link(nc.vector.tensor_copy(rt[:, 0:2, :].rearrange("p k t -> p t k"), topi[:, :, 0:2]))
                    settle()
                    for k in range(2):
                        link(nc.vector.tensor_tensor(oh[:, k, :, :], iota8[:, None, :].to_broadcast([P, TT, NE]),
                                                     rt[:, k, :, None].to_broadcast([P, TT, NE]), ALU.is_equal))
                    dve.wait_ge(d["rt_exp"], c + 1)
                    link(nc.vector.tensor_reduce(rt[:, 2, :], dl[:, :, :], AX.X, ALU.add))
                    settle()
                    link(nc.vector.reciprocal(rt[:, 3, :], rt[:, 2, :]))
                    settle()
                    link(nc.vector.tensor_tensor(dl[:, :, :], dl[:, :, :], rt[:, 3, :, None].to_broadcast([P, TT, NE]), ALU.mult))
                    settle()
                    for k in range(2):
                        link(nc.vector.tensor_tensor(lg[:, :, :], dl[:, :, :], oh[:, k, :, :], ALU.mult))
                        settle()
                        link(nc.vector.tensor_reduce(rt[:, 4 + k, :], lg[:, :, :], AX.X, ALU.add))
                        settle()
                    link(nc.vector.scalar_tensor_tensor(rt[:, 6, :], rt[:, 4, :], 1e-6, rt[:, 5, :], ALU.add, ALU.add))
                    settle()
                    link(nc.vector.reciprocal(rt[:, 7, :], rt[:, 6, :]))
                    settle()
                    for k in range(2):
                        link(nc.vector.tensor_tensor(rt[:, 8 + k, :], rt[:, 4 + k, :], rt[:, 7, :], ALU.mult))
                    settle()
                    for k in range(2):
                        link(nc.vector.tensor_tensor(rt[:, 10 + k, :], rt[:, 4 + k, :], rt[:, 8 + k, :], ALU.mult))
                        link(nc.vector.tensor_tensor(oh[:, k, :, :], oh[:, k, :, :],
                                                     rt[:, 8 + k, :, None].to_broadcast([P, TT, NE]), ALU.mult))
                    settle()
                    link(nc.vector.tensor_tensor(pw[:, q, :], rt[:, 10, :], rt[:, 11, :], ALU.add))
                    link(nc.vector.tensor_tensor(gate[:, q, :, :], oh[:, 0, :, :], oh[:, 1, :, :], ALU.add))
                    settle()
                if stage == "experts":
                    t, j = divmod(i, 5)
                    k = c * TT + t
                    if j == 0:
                        if k >= 2:
                            dve.wait_ge(d[f"stored{k % 2}"], 16 * (k // 2))
                        ins = nc.vector.tensor_scalar(y[:, k % 2, :], ps[:, 0:D], pw[:, q, t:t + 1], None, ALU.add)
                        ins.then_inc(d["v_out"], 1)
                        dve.wait_ge(d["v_out"], n + 1)
                    else:
                        e0 = 2 * (j - 1)
                        link(nc.vector.scalar_tensor_tensor(y[:, k % 2, :], ps[:, 0:D], gate[:, q, t, e0:e0 + 1],
                                                            y[:, k % 2, :], ALU.mult, ALU.add))
                        settle()
                        nc.vector.scalar_tensor_tensor(y[:, k % 2, :], ps[:, D:2 * D], gate[:, q, t, e0 + 1:e0 + 2],
                                                       y[:, k % 2, :], ALU.mult, ALU.add).then_inc(d["v_out"], 1)
                        dve.wait_ge(d["v_out"], n + 1)
                        if j == 4:
                            pass

        self_count = [0]
        block = ctx.enter_context(nc.Block())

        @block.sync
        def _(sp):
            sp.dma_start(cst[:, :], io["consts"]).then_inc(L["cst"], 16)
            sp.dma_start(ramp, io["ramp"]).then_inc(L["cst"], 16)
            sp.dma_start(wqkv[:, :, :], io["wqkv"]).then_inc(L["wqkv"], 16)
            sp.dma_start(bqkv[:, :], io["bqkv"]).then_inc(L["wqkv"], 16)
            sp.dma_start(xT[:, :, :], io["xT"]).then_inc(L["x"], 16)
            sp.dma_start(idx, io["idx"]).then_inc(L["idx"], 16)
            sp.dma_start(idm[:, :, :], io["idm"]).then_inc(L["idx"], 16)
            sp.dma_start(lam[:, 0, :], io["u"]).then_inc(L["u"], 16)
            sp.dma_start(small[:, 0:2], io["expert_id"]).then_inc(L["small"], 16)
            sp.dma_start(cols[:, :], io["cols"]).then_inc(L["cols"], 16)
            sp.wait_ge(L["small"], 16)
            eid = [sp.value_load(small[0:1, b:b + 1], min_val=0, max_val=15) for b in range(B)]
            for b in range(B):
                sp.dma_start(cbias[:, b, 0:1], io["cshared"][:, 0:1], allow_slow_non_contiguous=True).then_inc(L["small"], 16)
                sp.dma_start(cbias[0:64, b, 1:2], io["cshared"][0:64, 1:2], allow_slow_non_contiguous=True).then_inc(L["small"], 16)
            for b in range(B):
                sp.dma_start(cbias[64:128, b, 1:2],
                             io["eb"][bass.ds(eid[b], 1), :].rearrange("a p -> p a"), allow_slow_non_contiguous=True).then_inc(L["small"], 16)
            for att in atts:
                if att.dense:
                    for c in range(att.sh.NC):
                        if c:
                            sp.wait_ge(s["bias_exp"], B * c)
                        sp.dma_start(att.maskT[:, :].rearrange("p (t q) -> p t q", q=att.sh.SQ // 4),
                                     io["maskT"][:, :, c * att.sh.SQ // 4:(c + 1) * att.sh.SQ // 4]).then_inc(L["mask"], 16)
            sp.wait_ge(s["att_ready"], n_att)
            sp.wait_ge(s["s_prob"], n_att * JOBS)
            sp.dma_start(WoT[:, :, :], io["WoT"]).then_inc(L["wo"], 16)
            sp.dma_start(w1[:, :, :], io["w1"]).then_inc(L["w1"], 16)
            sp.dma_start(w2[:, :, :], io["w2"]).then_inc(LD["w2"], 16)
            sp.dma_start(fc1[:, :, :], io["fc1"]).then_inc(LD["fc1"], 16)
            for b in range(B):
                sp.dma_start(Wc[:, b, :, 0:SHARED], io["fc2"]).then_inc(LD["wc"], 16)
                sp.dma_start(Wc[:, b, :, SHARED:D], io["experts"][:, bass.ds(eid[b], 1), :, :].rearrange(
                    "p a k o -> p (a k) o")).then_inc(LD["wc"], 16)
            sp.dma_start(rw[:, :, :], io["rw"]).then_inc(LD["rw"], 16)
            sp.dma_start(ew[:, :, :], io["ew"]).then_inc(LD["ew"], 16)
            k = 0
            for stage, c, i, e, n in jobs:
                if stage == "experts" and i % 5 == 4:
                    sp.wait_ge(d["v_out"], n + 1)
                    t0 = (c * TT + i // 5) * P
                    sp.dma_start(out[t0:t0 + P, :], y[:, k % 2, :]).then_inc(d[f"stored{k % 2}"], 16)
                    k += 1
            for i in range(2):
                sp.wait_ge(d[f"stored{i}"], 16 * (k // 2))

        @block.gpsimd
        def _(pool):
            setup_pool(pool)
            atts[0].np = 0
            pool.wait_ge(s["kv_out"], B * atts[0].sh.NT)
            atts[0].pool(pool)

        @block.tensor
        def _(pe):
            atts[0].tensor(pe)
            dense_tensor(pe)

        @block.scalar
        def _(act):
            setup_act(act)
            atts[0].act(act)
            dense_act(act)

        @block.vector
        def _(dve):
            setup_dve(dve)
            dve.wait_ge(L["wqkv"], 32)
            atts[0].nd = 7
            atts[0].vector(dve)
            self_count[0] = atts[0].nd
            dense_vector(dve)


_OUT = "out_dram"


def _consts():
    c = np.zeros((P, C_END), np.float32)
    p = np.arange(P)
    c[:, C_ID:C_ID + P] = np.eye(P, dtype=np.float32)
    c[:, C_HM:C_HM + 8] = (p[:, None] // DH == np.arange(8)[None, :])
    c[:, C_SEL:C_SEL + P] = (p[:, None] == VW * (p[None, :] // VW) + DH)
    c[:, C_E8:C_E8 + 8] = np.arange(8)
    return c


def kernel(x, itok_Sx32_0_1023, condB_uprev, itok_B_0_15, mask_SxS_bk0, mask_Sx32_bk1, L0_cond_Wq, L0_cond_bq,
           L0_cond_Wk, L0_cond_bk, L0_cond_Wv, L0_cond_bv, L0_cond_Wo, L0_cond_bo, L0_ffn_w1, L0_ffn_b1, L0_ffn_w2,
           L0_ffn_b2, L1_cond_fc1_w, L1_cond_fc1_b, L1_cond_fc2_w, L1_cond_fc2_b, L1_cond_experts_w,
           L1_cond_experts_b, L1_ffn_router_w, L1_ffn_expert_weights):
    import concourse.bacc as bacc
    from concourse.bass_utils import run_bass_kernel_spmd

    def rows(a):
        a = np.asarray(a)
        return np.ascontiguousarray(a.reshape(a.shape[0] // P, P, -1).transpose(1, 0, 2))

    def spread(*vs):
        return np.ascontiguousarray(np.broadcast_to(np.concatenate([np.asarray(v) for v in vs])[None, :],
                                                    (P, sum(v.shape[0] for v in vs))))

    def column(v):
        return np.asarray(v).reshape(-1, P).T

    A = np.asarray
    wo = np.zeros((H, VW, D), np.float32)
    wo[:, 0:DH, :] = A(L0_cond_Wo).T.reshape(H, DH, D)
    fc2b = np.zeros((2, P), np.float32)
    fc2b.reshape(-1)[0:SHARED] = A(L1_cond_fc2_b)
    arrays = {
        "consts": _consts(),
        "ramp": np.ascontiguousarray(np.broadcast_to(np.arange(1, S + 1, dtype=np.float32), (P, S))),
        "xT": rows(A(x).reshape(N, D).T),
        "wqkv": rows(np.concatenate([A(L0_cond_Wq).T, A(L0_cond_Wk).T, A(L0_cond_Wv).T], axis=1)),
        "bqkv": spread(L0_cond_bq, L0_cond_bk, L0_cond_bv),
        "idx": np.ascontiguousarray(A(itok_Sx32_0_1023).reshape(S // P, P, K_SPARSE).transpose(1, 0, 2)),
        "idm": np.ascontiguousarray(A(mask_Sx32_bk1).view(np.int32).reshape(S // P, P, K_SPARSE // 4).transpose(1, 0, 2)),
        "u": spread(condB_uprev),
        "expert_id": np.ascontiguousarray(A(itok_B_0_15).reshape(1, B)),
        "cols": np.ascontiguousarray(np.concatenate(
            [column(L0_cond_bo), column(L0_ffn_b1), column(L0_ffn_b2), column(L1_cond_fc1_b)], axis=1)),
        "cshared": np.ascontiguousarray(fc2b.T),
        "eb": A(L1_cond_experts_b),
        "WoT": rows(wo.reshape(H * VW, D)),
        "w1": rows(L0_ffn_w1),
        "maskT": rows(np.ascontiguousarray(A(mask_SxS_bk0).T).view(np.int32)),
        "w2": rows(L0_ffn_w2),
        "fc1": rows(A(L1_cond_fc1_w).T),
        "fc2": rows(A(L1_cond_fc2_w).T),
        "experts": np.ascontiguousarray(A(L1_cond_experts_w).transpose(2, 0, 1).reshape(KW, P, 16, PART).transpose(1, 2, 0, 3)),
        "rw": rows(A(L1_ffn_router_w).T),
        "ew": rows(A(L1_ffn_expert_weights).transpose(1, 0, 2).reshape(D, NE * D)),
    }
    nc = bacc.Bacc("TRN2", target_bir_lowering=False, num_devices=1)
    io = {k: nc.dram_tensor(k + "_dram", v.shape, mybir.dt.from_np(v.dtype), kind="ExternalInput").ap()
          for k, v in arrays.items()}
    out = nc.dram_tensor(_OUT, (N, D), F32, kind="ExternalOutput").ap()
    bass_adaln_ffn(nc, io, out, **OPTIONS)
    r = run_bass_kernel_spmd(nc, [{k + "_dram": v for k, v in arrays.items()}], core_ids=[0])
    return r.results[0][_OUT].reshape(B, S, D)


OPTIONS = dict(general_only=True)
```

```python
import concourse.bass as bass
from concourse import mybir
from contextlib import ExitStack
import numpy as np

F32 = mybir.dt.float32
F32R = mybir.dt.float32r
F16 = mybir.dt.float16
BF16 = mybir.dt.bfloat16
I32 = mybir.dt.int32
U8 = mybir.dt.uint8
U32 = mybir.dt.uint32
ALU = mybir.AluOpType
ACT = mybir.ActivationFunctionType
AX = mybir.AxisListType

P = 128
B, S, D, H = 2, 1024, 256, 16
DH = D // H
K_SPARSE = 32
N = B * S
KD = D // P
WIDTH = 1024
KW = WIDTH // P
SHARED = 192
PART = D - SHARED
NE = 8
HG = 4
GROUPS = H // HG
AUG = 64
VW = 32
VC = DH + 1
FEW_KEYS = 256
LAMBDA_MAX, ALPHA = 10.0, 5.0
SCALE = 1.0 / 4.0
BIG = 1.0e30
FMAX = 3.0e38
QC = 512
CHUNKS = N // QC
UNITS = B * GROUPS
JOBS = 8
LAG = 10

C_ID, C_HM, C_SEL, C_E8, C_END = 0, 128, 136, 264, 272


class Shape:

    def __init__(self, keys):
        self.T = keys
        self.NT = keys // P
        self.SQ = 2048 * P // keys
        self.NQ = self.SQ // P
        self.NC = S // self.SQ
        self.NBK = keys // 256
        self.CP = min(512, self.SQ)
        self.NB = 2 if keys <= 256 else 1
        self.LEAD = 4 if self.NB == 2 else 0
        self.TP = min(self.NT, 4)
        self.QP = min(self.NQ, 4)


def bass_adaln_ffn(nc, io, out, general_only=False, fast_only=False):
    ctx = ExitStack()
    with ctx:
        def sb(name, shape, dt, at=ctx):
            return at.enter_context(nc.sbuf_tensor(name, shape, dt))

        def sem(name):
            return ctx.enter_context(nc.semaphore(name))

        cst = sb("cst", [P, C_END], F32)
        ident, headmask, sel, iota8 = (cst[:, C_ID:C_ID + P], cst[:, C_HM:C_HM + 8],
                                       cst[:, C_SEL:C_SEL + P], cst[:, C_E8:C_E8 + 8])
        xT = sb("xT", [P, KD, N], F32)
        attT = sb("attT", [P, GROUPS, N], F32)
        cols = sb("cols", [P, 20], F32)
        cbias = sb("cbias", [P, B, KD], F32)
        small = sb("small", [1, 8], I32)
        flags = sb("flags", [P, 4], F32)
        few = sb("few", [1, 4], I32)

        PS = [ctx.enter_context(nc.psum_tensor(f"bank{i}", [P, 512], F32)) for i in range(0)]
        psG = ctx.enter_context(nc.psum_tensor("psG", [P, 2, 512], F32))
        psS = ctx.enter_context(nc.psum_tensor("psS", [P, 2, 512], F32))
        psO = ctx.enter_context(nc.psum_tensor("psO", [P, 2, 512], F32))
        psM = ctx.enter_context(nc.psum_tensor("psM", [P, 2, 512], F32))
        RING = [psG[:, 0, :], psG[:, 1, :], psS[:, 0, :], psS[:, 1, :]]

        actx = ExitStack()
        shapes = [Shape(1024)] if general_only else [Shape(256)] if fast_only else [Shape(256), Shape(1024)]
        wqkv = sb("wqkv", [P, KD, 3 * D], F32, actx)
        bqkv = sb("bqkv", [P, 3 * D], F32, actx)
        idm = sb("idm", [P, S // P, K_SPARSE // 4], I32, actx)
        idx1 = sb("idx1", [P, S // P, K_SPARSE], F32, actx)
        iota16 = sb("iota16", [P, 1024], F16, actx)
        ident16 = sb("ident16", [P, P], F16, actx)
        identm = sb("identm", [P, B, P], BF16, actx)
        lam = sb("lam", [P, 6, B], F32, actx)
        Pr = sb("Pr", [P, 2 * HG, 1024], F32, actx)
        W = sb("W", [P, 2048], F32, actx)
        ramp = W[:, 0:1024]
        idx = W[:, 1024:1280].bitcast(I32).rearrange("p (q k) -> p q k", k=K_SPARSE)
        idmf = W[:, 1280:1536].rearrange("p (q k) -> p q k", k=K_SPARSE)
        Mneg = sb("Mneg", [P, 2048], BF16, actx)
        shift = sb("shift", [P, 2, HG], F32, actx)
        shiftb = sb("shiftb", [P, HG, 4], F32, actx)
        Qa = sb("Qa", [P, 2, HG, AUG], F32R, actx)
        Ka = sb("Ka", [P, 2, HG, AUG], F32R, actx)

        L = {k: sem("ld_" + k) for k in ("cst", "x", "wqkv", "idx", "u", "small", "cols", "mask", "wo", "w1")}
        s = {k: sem(k) for k in ("consts_ready", "idx_ready", "lam_exp", "cleared", "self_setup", "greatest", "greatest_full",
                                 "flag_ready", "attention_done")}
        ATTENTION_SEMS = (
            "self_dve", "self_pool", "zeroed", "kv_full", "kv_out", "q_full", "q_out", "eq_ready",
            "cnt_full", "eq_used", "cnt_out", "cntT_full", "cntT_out", "bias_exp", "w_ready", "qg_full",
            "qg_out", "kt_full", "kt_out", "kg_ready", "ka_ready", "ka_full", "kp_out", "qa_split",
            "qa_shift", "qa_full", "qat_out", "g_scores", "g_max", "s_scores", "s_exp", "s_prob",
            "pv_done", "ot_out", "den_full", "recip", "att_ready")

        def setup_pool(pool):
            nc.gpsimd.memset(Qa[:, :, :, :].bitcast(F32), 0.0).then_inc(s["cleared"], 1)
            nc.gpsimd.memset(Ka[:, :, :, :].bitcast(F32), 0.0).then_inc(s["cleared"], 1)
            pool.wait_ge(s["cleared"], 2)
            nc.gpsimd.memset(Ka[:, :, :, 48:50].bitcast(F32), 1.0).then_inc(s["cleared"], 1)

        def setup_dve(dve):
            dve.wait_ge(L["cst"], 32)
            nc.vector.tensor_copy(iota16[:, :], ramp).then_inc(s["consts_ready"], 1)
            nc.vector.tensor_copy(ident16[:, :], ident).then_inc(s["consts_ready"], 1)
            dve.wait_ge(L["idx"], 32)
            nc.vector.tensor_copy(idmf, idm[:, :, :].bitcast(U8)).then_inc(s["self_setup"], 1)
            nc.vector.tensor_copy(idx1[:, :, :], idx).then_inc(s["self_setup"], 1)
            dve.wait_ge(s["self_setup"], 2)
            nc.vector.scalar_tensor_tensor(idx1[:, :, :], idx1[:, :, :], 1.0, idmf,
                                           ALU.add, ALU.mult).then_inc(s["idx_ready"], 1)
            dve.wait_ge(s["lam_exp"], 1)
            nc.vector.tensor_scalar(lam[:, 1, :], lam[:, 1, :], LAMBDA_MAX, None, ALU.mult).then_inc(s["self_setup"], 1)
            dve.wait_ge(s["self_setup"], 3)
            nc.vector.tensor_scalar(lam[:, 2, :], lam[:, 1, :], 1.0, None, ALU.is_ge).then_inc(s["self_setup"], 1)
            nc.vector.tensor_scalar(lam[:, 3, :], lam[:, 1, :], 1.0, None, ALU.min).then_inc(s["self_setup"], 1)
            nc.vector.tensor_scalar(lam[:, 4, :], lam[:, 1, :], 1.0, -1.0, ALU.min, ALU.mult).then_inc(s["self_setup"], 1)
            dve.wait_ge(s["self_setup"], 6)
            nc.vector.tensor_scalar(lam[:, 5, :], lam[:, 2, :], -1.0, 1.0, ALU.mult, ALU.add).then_inc(s["self_setup"], 1)
            for b in range(B):
                nc.vector.tensor_scalar(identm[:, b, :], ident, lam[:, 2, b:b + 1], None,
                                        ALU.mult).then_inc(s["consts_ready"], 1)
            dve.wait_ge(s["self_setup"], 7)
            dve.wait_ge(s["idx_ready"], 1)
            nc.vector.tensor_reduce(flags[:, 0:1], idx1[:, :, :], AX.XY, ALU.max).then_inc(s["greatest"], 1)
            dve.wait_ge(s["greatest_full"], 1)
            nc.vector.tensor_reduce(flags[0:1, 1:2], psM[0:1, 0, 0:P], AX.X, ALU.max).then_inc(s["self_setup"], 1)
            dve.wait_ge(s["self_setup"], 8)
            nc.vector.scalar_tensor_tensor(flags[0:1, 2:3], flags[0:1, 1:2], float(FEW_KEYS), lam[0:1, 2, 0:1],
                                           ALU.is_le, ALU.mult).then_inc(s["self_setup"], 1)
            dve.wait_ge(s["self_setup"], 9)
            nc.vector.tensor_tensor(few[0:1, 0:1], flags[0:1, 2:3], lam[0:1, 2, 1:2],
                                    ALU.mult).then_inc(s["flag_ready"], 1)

        def setup_tensor(pe):
            pe.wait_ge(s["greatest"], 1)
            pe.wait_ge(L["cst"], 32)
            nc.tensor.transpose(psM[0:1, 0, 0:P], flags[:, 0:1], ident).then_inc(s["greatest_full"], 1)

        def either(eng, run):
            if len(atts) == 1:
                run(atts[0])
                return
            eng.wait_ge(s["flag_ready"], 1)
            flag = eng.value_load(few[0:1, 0:1], min_val=0, max_val=1)
            with eng.If(flag == 1):
                run(atts[0])
            with eng.Else():
                run(atts[1])

        def setup_act(act):
            act.wait_ge(L["u"], 16)
            nc.scalar.activation(lam[:, 1, :], lam[:, 0, :], ACT.Exp, scale=-ALPHA).then_inc(s["lam_exp"], 1)

        class Attention:

            def __init__(self, sh, tag, at):
                self.sh = sh
                self.s = {k: sem(k + tag) for k in ATTENTION_SEMS}
                self.nd = self.np = 0
                self.Kn = sb("Kn" + tag, [P, B, sh.NT, D], F32, at)
                self.VA = sb("VA" + tag, [P, B, sh.NT, H * VC], F32, at)
                self.Qn = sb("Qn" + tag, [P, B, sh.NQ, D], F32, at)
                self.QG = sb("QG" + tag, [P, 2, sh.SQ], F32R, at)
                self.KT = sb("KT" + tag, [P, sh.T], F32, at)
                self.KG = sb("KG" + tag, [P, sh.NB, HG, sh.T], F32R, at)
                self.KP = sb("KP" + tag, [P, sh.NB, HG, sh.T], F32R, at)
                self.QAT = sb("QAT" + tag, [P, 2, 2, sh.SQ], F32R, at)
                self.OTs = sb("OTs" + tag, [P, sh.SQ], F32, at)
                self.Rr = sb("Rr" + tag, [P, sh.SQ], F32, at)
                self.NE = 4 if sh.NB == 2 else 2
                self.EQ = sb("EQ" + tag, [P, self.NE, sh.T], F16, at)
                self.Cn = sb("Cn" + tag, [P, sh.T], F32, at)
                self.dense = sh.T == S
                if self.dense:
                    self.CT = sb("CT" + tag, [P, 2048], BF16, at)
                    self.maskT = sb("maskT" + tag, [P, 512], I32, at)
                else:
                    self.CT = W

            def due(self, c):
                sh = self.sh
                n_jobs = UNITS * JOBS
                for t in range(-sh.LEAD, n_jobs + LAG + 11):
                    n = t - LAG
                    if (t + sh.LEAD) % JOBS == 0 and 0 <= (t + sh.LEAD) // JOBS < UNITS:
                        yield "guard_keys", (t + sh.LEAD) // JOBS
                    if (n + sh.LEAD) % JOBS == 0 and 0 <= (n + sh.LEAD) // JOBS < UNITS:
                        yield "score_keys", (n + sh.LEAD) // JOBS
                    if 1 <= t <= n_jobs and t % sh.NBK == 0:
                        yield "query_rows", t // sh.NBK - 1
                    if 0 <= t < n_jobs:
                        yield "guard", t
                    if 0 <= n < n_jobs:
                        yield "score", n
                    if n >= 5 and (n - 5) % HG == 0 and (n - 5) // HG < 2 * UNITS:
                        yield "values", (n - 5) // HG
                    if n >= 10 and (n - 10) % JOBS == 0 and (n - 10) // JOBS < UNITS:
                        yield "norm", (n - 10) // JOBS

            def pool(self, pool):
                sh = self.sh
                pool.wait_ge(self.s["kv_out"], B * sh.NT)
                for c in range(sh.NC):
                    for what, i in self.due(c):
                        if what == "guard_keys":
                            g = i % GROUPS
                            ug = c * UNITS + i
                            pool.wait_ge(self.s["kt_out"], (ug // 2 + 1) * (sh.NT // sh.TP))
                            if ug >= sh.NB:
                                pool.wait_ge(self.s["g_scores"], JOBS * (ug - sh.NB + 1))
                            hm = headmask[:, HG * (g % 2):HG * (g % 2) + HG]
                            nc.gpsimd.tensor_tensor(
                                self.KG[:, ug % sh.NB, :, :],
                                self.KT[:, None, :].to_broadcast([P, HG, sh.T]),
                                hm[:, :, None].to_broadcast([P, HG, sh.T]), ALU.mult).then_inc(self.s["kg_ready"], 1)
                        if what == "score_keys":
                            b, g = divmod(i, GROUPS)
                            ug = c * UNITS + i
                            for tt in range(sh.NT):
                                m = ug * sh.NT + tt
                                if m >= 2:
                                    pool.wait_ge(self.s["ka_full"], m - 1)
                                k = self.Kn[:, b, tt, g * HG * DH:(g + 1) * HG * DH].rearrange("p (h d) -> p h d", d=DH)
                                ka = Ka[:, m % 2, :, :]
                                nc.gpsimd.tensor_copy(ka[:, :, 0:16], k).then_inc(self.s["self_pool"], 1)
                                nc.gpsimd.tensor_copy(ka[:, :, 32:48], k)
                                self.np += 1
                                pool.wait_ge(self.s["self_pool"], self.np)
                                nc.gpsimd.tensor_tensor(ka[:, :, 16:32], k, ka[:, :, 0:16].bitcast(F32),
                                                        ALU.subtract).then_inc(self.s["ka_ready"], 1)
                        if what == "guard" and i % sh.NBK == 0:
                            u = i // JOBS
                            b, g = divmod(u, GROUPS)
                            m = c * UNITS * sh.NQ + i // sh.NBK
                            st = m % sh.NQ
                            if m >= 2:
                                pool.wait_ge(self.s["qa_full"], m - 1)
                            pool.wait_ge(self.s["q_out"], (c + 1) * B * sh.NQ)
                            q = self.Qn[:, b, st, g * HG * DH:(g + 1) * HG * DH].rearrange("p (h d) -> p h d", d=DH)
                            qa = Qa[:, m % 2, :, :]
                            nc.gpsimd.tensor_copy(qa[:, :, 0:16], q).then_inc(self.s["self_pool"], 1)
                            nc.gpsimd.tensor_copy(qa[:, :, 16:32], q)
                            self.np += 1
                            pool.wait_ge(self.s["self_pool"], self.np)
                            nc.gpsimd.tensor_tensor(qa[:, :, 32:48], q, qa[:, :, 0:16].bitcast(F32),
                                                    ALU.subtract).then_inc(self.s["qa_split"], 1)

            def tensor(self, pe):
                sh = self.sh
                log = []

                def misc(kind, n):
                    if len(log) >= 2:
                        pe.wait_ge(self.s[log[-2][0]], log[-2][1] + 1)
                    log.append((kind, n))
                    return psM[:, len(log) % 2, :]

                pe.wait_ge(L["cst"], 32)
                pe.wait_ge(L["x"], 16)
                pe.wait_ge(L["wqkv"], 32)
                for m in range(B * sh.NT):
                    b, tt = divmod(m, sh.NT)
                    if m >= 4:
                        pe.wait_ge(self.s["kv_out"], m - 3)
                    for k in range(KD):
                        mm = nc.tensor.matmul(RING[m % 4], xT[:, k, b * S + tt * P:b * S + tt * P + P],
                                              wqkv[:, k, D:3 * D], start=(k == 0), stop=(k == KD - 1))
                    mm.then_inc(self.s["kv_full"], 1)
                pe.wait_ge(s["consts_ready"], 2 + B)
                for c in range(sh.NC):
                    u0 = c * UNITS
                    pe.wait_ge(self.s["kv_out"], B * sh.NT)
                    if c:
                        pe.wait_ge(self.s["g_max"], JOBS * u0)
                        pe.wait_ge(self.s["s_exp"], JOBS * u0)
                    for i in range(B * sh.NQ):
                        m = c * B * sh.NQ + i
                        b, st = divmod(i, sh.NQ)
                        if i >= 4:
                            pe.wait_ge(self.s["q_out"], m - 3)
                        t0 = b * S + c * sh.SQ + st * P
                        for k in range(KD):
                            mm = nc.tensor.matmul(RING[i % 4][:, 0:D], xT[:, k, t0:t0 + P],
                                                  wqkv[:, k, 0:D], start=(k == 0), stop=(k == KD - 1))
                        mm.then_inc(self.s["q_full"], 1)
                    if c:
                        pe.wait_ge(self.s["recip"], u0)
                    pe.wait_ge(self.s["zeroed"], 3)
                    for i in range(sh.NQ):
                        m = c * sh.NQ + i
                        if i:
                            pe.wait_ge(self.s["cnt_out"], 2 * m)
                        for k in range(K_SPARSE):
                            e = m * K_SPARSE + k
                            pe.wait_ge(self.s["eq_ready"], e + 1)
                            for f in range(0, sh.T, 512):
                                w = min(512, sh.T)
                                mm = nc.tensor.matmul(psO[:, f // 512, 0:w], ident16[:, :],
                                                      self.EQ[:, e % self.NE, f:f + w],
                                                      start=(k == 0), stop=(k == K_SPARSE - 1))
                            mm.then_inc(self.s["eq_used"], 1)
                        pe.wait_ge(self.s["cnt_out"], 2 * (m + 1))
                        for t4 in range(0, sh.NT, sh.TP):
                            ps = misc("cntT_out", m * (sh.NT // sh.TP) + t4 // sh.TP)
                            for j in range(sh.TP):
                                mm = nc.tensor.transpose(ps[:, j * P:j * P + P],
                                                         self.Cn[:, (t4 + j) * P:(t4 + j + 1) * P], ident)
                            mm.then_inc(self.s["cntT_full"], 1)
                    pe.wait_ge(self.s["q_out"], (c + 1) * B * sh.NQ)
                    for what, i in self.due(c):
                        u = i // JOBS
                        if what == "guard_keys":
                            b, g = divmod(i, GROUPS)
                            ug = u0 + i
                            half = ug // 2
                            if g % 2 == 0:
                                for q4 in range(0, sh.NQ, sh.QP):
                                    ps = misc("qg_out", half * (sh.NQ // sh.QP) + q4 // sh.QP)
                                    for j in range(sh.QP):
                                        mm = nc.tensor.transpose(ps[:, j * P:j * P + P],
                                                                 self.Qn[:, b, q4 + j, (g // 2) * P:(g // 2) * P + P], ident)
                                    mm.then_inc(self.s["qg_full"], 1)
                                for t4 in range(0, sh.NT, sh.TP):
                                    ps = misc("kt_out", half * (sh.NT // sh.TP) + t4 // sh.TP)
                                    for j in range(sh.TP):
                                        mm = nc.tensor.transpose(ps[:, j * P:j * P + P],
                                                                 self.Kn[:, b, t4 + j, (g // 2) * P:(g // 2) * P + P], ident)
                                    mm.then_inc(self.s["kt_full"], 1)
                        if what == "score_keys":
                            for tt in range(sh.NT):
                                m = (u0 + i) * sh.NT + tt
                                pe.wait_ge(self.s["ka_ready"], m + 1)
                                ps = misc("kp_out", m)
                                for p in range(2):
                                    mm = nc.tensor.transpose(ps[:, p * P:p * P + P],
                                                             Ka[:, m % 2, 2 * p:2 * p + 2, :].rearrange("p h a -> p (h a)").bitcast(F32), ident)
                                mm.then_inc(self.s["ka_full"], 1)
                        if what == "query_rows":
                            m = u0 * sh.NQ + i
                            pe.wait_ge(self.s["qa_split"], m + 1)
                            pe.wait_ge(self.s["qa_shift"], m + 1)
                            ps = misc("qat_out", m)
                            for p in range(2):
                                mm = nc.tensor.transpose(ps[:, p * P:p * P + P],
                                                         Qa[:, m % 2, 2 * p:2 * p + 2, :].rearrange("p h a -> p (h a)").bitcast(F32), ident)
                            mm.then_inc(self.s["qa_full"], 1)
                        if what == "guard":
                            b, g = divmod(u, GROUPS)
                            ug = u0 + u
                            st, blk = divmod(i % JOBS, sh.NBK)
                            pe.wait_ge(self.s["kg_ready"], ug + 1)
                            pe.wait_ge(self.s["qg_out"], (ug // 2 + 1) * (sh.NQ // sh.QP))
                            if u0 * JOBS + i >= 1:
                                pe.wait_ge(self.s["g_max"], u0 * JOBS + i)
                            for p in range(2):
                                o = psG[:, p, :].rearrange("p (h t) -> p h t", h=2)
                                nc.tensor.matmul(o, self.QG[:, (ug // 2) % 2, st * P:st * P + P],
                                                 self.KG[:, ug % sh.NB, 2 * p:2 * p + 2, blk * 256:blk * 256 + 256],
                                                 start=True, stop=False)
                                a = st * sh.T + blk * 256
                                mm = nc.tensor.matmul(o, identm[:, b, :],
                                                      Mneg[:, None, a:a + 256].to_broadcast([P, 2, 256]),
                                                      start=False, stop=True)
                            mm.then_inc(self.s["g_scores"], 1)
                        if what == "score":
                            ug = u0 + u
                            r, j = divmod(i % JOBS, HG)
                            pe.wait_ge(self.s["kp_out"], (ug + 1) * sh.NT)
                            pe.wait_ge(self.s["qat_out"], (ug + 1) * sh.NQ)
                            if u0 * JOBS + i >= 1:
                                pe.wait_ge(self.s["s_exp"], u0 * JOBS + i)
                            flat = psS[:, :, :].rearrange("p a b -> p (a b)")
                            for f in range(0, 1024, sh.CP):
                                tt, q = divmod(r * 1024 + f, sh.SQ)
                                mm = nc.tensor.matmul(flat[:, f:f + sh.CP],
                                                      self.KP[:, ug % sh.NB, j, tt * P:tt * P + P],
                                                      self.QAT[:, ug % 2, j // 2, q:q + sh.CP], start=True, stop=True)
                            mm.then_inc(self.s["s_scores"], 1)
                        if what == "values":
                            v = 2 * u0 + i
                            ug, r = divmod(v, 2)
                            b, g = divmod(i // 2, GROUPS)
                            pe.wait_ge(self.s["s_prob"], HG * (v + 1))
                            if r == 0 and ug:
                                pe.wait_ge(self.s["recip"], ug)
                            for f in range(0, 1024, sh.CP):
                                tt, q = divmod(r * 1024 + f, sh.SQ)
                                for j in range(HG):
                                    h = g * HG + j
                                    mm = nc.tensor.matmul(
                                        psO[VW * j:VW * j + VC, q // 512, q % 512:q % 512 + sh.CP],
                                        self.VA[:, b, tt, h * VC:h * VC + VC], Pr[:, HG * r + j, f:f + sh.CP],
                                        start=(tt == 0), stop=(tt == sh.NT - 1), tile_position=(0, VW * j))
                            mm.then_inc(self.s["pv_done"], 1)
                        if what == "norm":
                            ug = u0 + i
                            pe.wait_ge(self.s["ot_out"], ug + 1)
                            for q in range(0, sh.SQ, sh.CP):
                                mm = nc.tensor.matmul(psO[:, q // 512, 0:sh.CP], sel, self.OTs[:, q:q + sh.CP],
                                                      start=True, stop=True)
                            mm.then_inc(self.s["den_full"], 1)

            def act(self, act):
                sh = self.sh
                act.wait_ge(self.s["zeroed"], 3)
                mi = 0

                def misc():
                    nonlocal mi
                    mi += 1
                    return psM[:, mi % 2, :]

                for c in range(sh.NC):
                    u0 = c * UNITS
                    for i in range(sh.NQ):
                        m = c * sh.NQ + i
                        for t4 in range(0, sh.NT, sh.TP):
                            act.wait_ge(self.s["cntT_full"], m * (sh.NT // sh.TP) + t4 // sh.TP + 1)
                            if self.dense and c and i == 0 and t4 == 0:
                                act.wait_ge(self.s["w_ready"], B * c)
                            ct = self.CT[:, :].rearrange("p (t q) -> p t q", q=sh.SQ)
                            nc.scalar.copy(ct[:, t4:t4 + sh.TP, i * P:i * P + P],
                                           misc()[:, 0:sh.TP * P].rearrange("p (t q) -> p t q", q=P)).then_inc(self.s["cntT_out"], 1)
                    for what, i in self.due(c):
                        u = i // JOBS
                        if what == "guard_keys" and i % 2 == 0:
                            ug = u0 + i
                            half = ug // 2
                            if half >= 2:
                                act.wait_ge(self.s["g_scores"], JOBS * 2 * (half - 1))
                            for q4 in range(0, sh.NQ, sh.QP):
                                act.wait_ge(self.s["qg_full"], half * (sh.NQ // sh.QP) + q4 // sh.QP + 1)
                                nc.scalar.copy(self.QG[:, half % 2, q4 * P:(q4 + sh.QP) * P],
                                               misc()[:, 0:sh.QP * P]).then_inc(self.s["qg_out"], 1)
                            if ug:
                                act.wait_ge(self.s["kg_ready"], ug)
                            for t4 in range(0, sh.NT, sh.TP):
                                act.wait_ge(self.s["kt_full"], half * (sh.NT // sh.TP) + t4 // sh.TP + 1)
                                nc.scalar.copy(self.KT[:, t4 * P:(t4 + sh.TP) * P],
                                               misc()[:, 0:sh.TP * P]).then_inc(self.s["kt_out"], 1)
                        if what == "score_keys":
                            ug = u0 + i
                            if ug >= sh.NB:
                                act.wait_ge(self.s["s_scores"], JOBS * (ug - sh.NB + 1))
                            for tt in range(sh.NT):
                                act.wait_ge(self.s["ka_full"], ug * sh.NT + tt + 1)
                                ps = misc()[:, 0:2 * P].rearrange("p (a t) -> p a t", t=P)
                                kp = self.KP[:, ug % sh.NB, :, tt * P:tt * P + P]
                                nc.scalar.copy(kp[0:AUG, 0::2, :], ps[0:AUG, :, :])
                                nc.scalar.copy(kp[AUG:P, 1::2, :], ps[AUG:P, :, :]).then_inc(self.s["kp_out"], 1)
                        if what == "query_rows":
                            m = u0 * sh.NQ + i
                            ug, st = divmod(m, sh.NQ)
                            act.wait_ge(self.s["qa_full"], m + 1)
                            if ug >= 2 and st == 0:
                                act.wait_ge(self.s["s_scores"], JOBS * (ug - 1))
                            ps = misc()[:, 0:2 * P].rearrange("p (a t) -> p a t", t=P)
                            nc.scalar.copy(self.QAT[:, ug % 2, :, st * P:st * P + P], ps).then_inc(self.s["qat_out"], 1)
                        if what == "score":
                            n = u0 * JOBS + i
                            if self.dense and i % (GROUPS * JOBS) == 0:
                                b = i // (GROUPS * JOBS)
                                k = c * B + b
                                act.wait_ge(L["mask"], 16 * (c + 1))
                                act.wait_ge(s["idx_ready"], 1)
                                if k:
                                    act.wait_ge(self.s["s_prob"], k * GROUPS * JOBS)
                                nc.scalar.activation(W[:, :], self.maskT[:, :].bitcast(U8), ACT.Exp, bias=lam[:, 4, b:b + 1],
                                                     scale=lam[:, 3, b:b + 1]).then_inc(self.s["bias_exp"], 1)
                            act.wait_ge(self.s["s_scores"], n + 1)
                            if n >= JOBS:
                                act.wait_ge(self.s["pv_done"], (n - JOBS) // HG + 1)
                            nc.scalar.activation(Pr[:, n % JOBS, :], psS[:, :, :].rearrange("p a b -> p (a b)"),
                                                 ACT.Exp, scale=SCALE).then_inc(self.s["s_exp"], 1)
                        if what == "norm":
                            ug = u0 + i
                            act.wait_ge(self.s["pv_done"], 2 * (ug + 1))
                            if ug:
                                act.wait_ge(self.s["att_ready"], ug)
                            nc.scalar.copy(self.OTs[:, 0:sh.SQ], psO[:, :, :].rearrange("p a b -> p (a b)")[:, 0:sh.SQ]
                                           ).then_inc(self.s["ot_out"], 1)

            def vector(self, dve):
                sh = self.sh
                nc.vector.memset(self.KP[:, :, :, :].bitcast(F32), 0.0).then_inc(self.s["zeroed"], 1)
                va = self.VA[:, :, :, :].rearrange("p b t (h w) -> p (b t) h w", w=VC)
                nc.vector.memset(va[:, :, :, DH:VC], 1.0).then_inc(self.s["zeroed"], 1)
                nc.vector.memset(psO[:, :, :], 0.0).then_inc(self.s["zeroed"], 1)
                for m in range(B * sh.NT):
                    b, tt = divmod(m, sh.NT)
                    dve.wait_ge(self.s["kv_full"], m + 1)
                    nc.vector.tensor_tensor(self.Kn[:, b, tt, :], RING[m % 4][:, 0:D], bqkv[:, D:2 * D], ALU.add)
                    nc.vector.tensor_tensor(va[:, m, :, 0:DH],
                                            RING[m % 4][:, D:2 * D].rearrange("p (h d) -> p h d", d=DH),
                                            bqkv[:, 2 * D:3 * D].rearrange("p (h d) -> p h d", d=DH),
                                            ALU.add).then_inc(self.s["kv_out"], 1)
                for c in range(sh.NC):
                    u0 = c * UNITS
                    for i in range(B * sh.NQ):
                        m = c * B * sh.NQ + i
                        b, st = divmod(i, sh.NQ)
                        dve.wait_ge(self.s["q_full"], m + 1)
                        if c and i == 0:
                            dve.wait_ge(self.s["qa_split"], u0 * sh.NQ)
                            dve.wait_ge(self.s["qg_full"], u0 // 2 * (sh.NQ // sh.QP))
                        nc.vector.tensor_tensor(self.Qn[:, b, st, :], RING[i % 4][:, 0:D], bqkv[:, 0:D],
                                                ALU.add).then_inc(self.s["q_out"], 1)
                    for i in range(sh.NQ):
                        m = c * sh.NQ + i
                        for k in range(K_SPARSE):
                            e = m * K_SPARSE + k
                            if e >= self.NE:
                                dve.wait_ge(self.s["eq_used"], e - self.NE + 1)
                            nc.vector.tensor_scalar(self.EQ[:, e % self.NE, :], iota16[:, 0:sh.T], idx1[:, m, k:k + 1], None,
                                                    ALU.is_equal).then_inc(self.s["eq_ready"], 1)
                        dve.wait_ge(self.s["eq_used"], (m + 1) * K_SPARSE)
                        if m:
                            dve.wait_ge(self.s["cntT_full"], m * (sh.NT // sh.TP))
                        cnt = psO[:, :, :].rearrange("p a b -> p (a b)")[:, 0:sh.T]
                        nc.vector.tensor_copy(self.Cn[:, :], cnt).then_inc(self.s["cnt_out"], 1)
                        nc.vector.tensor_scalar(Mneg[:, i * sh.T:(i + 1) * sh.T], cnt, 0.0, -BIG, ALU.is_equal,
                                                ALU.mult).then_inc(self.s["cnt_out"], 1)
                    for what, i in self.due(c):
                        u = i // JOBS
                        if what == "guard":
                            gj = u0 * JOBS + i
                            st_, blk = divmod(gj, sh.NBK)
                            dve.wait_ge(self.s["g_scores"], gj + 1)
                            src = psG[:, :, :].rearrange("p a (h t) -> p (a h) t", h=2)
                            last = blk == sh.NBK - 1
                            if sh.NBK == 1:
                                dst = shift[:, st_ % 2, :]
                            else:
                                dst = shiftb[:, :, blk]
                            nc.vector.tensor_reduce(dst, src, AX.X, ALU.max, negate=True).then_inc(self.s["g_max"], 1)
                            if last:
                                dve.wait_ge(self.s["g_max"], gj + 1)
                                if sh.NBK > 1:
                                    nc.vector.tensor_reduce(shift[:, st_ % 2, :], shiftb[:, :, :], AX.X,
                                                            ALU.min).then_inc(self.s["self_dve"], 1)
                                    self.nd += 1
                                    dve.wait_ge(self.s["self_dve"], self.nd)
                                if st_ >= 2:
                                    dve.wait_ge(self.s["qa_full"], st_ - 1)
                                if st_ < 2:
                                    dve.wait_ge(s["cleared"], 3)
                                qa = Qa[:, st_ % 2, :, :]
                                nc.vector.tensor_copy(qa[:, :, 48], shift[:, st_ % 2, :]).then_inc(self.s["self_dve"], 1)
                                self.nd += 1
                                dve.wait_ge(self.s["self_dve"], self.nd)
                                nc.vector.tensor_tensor(qa[:, :, 49], shift[:, st_ % 2, :],
                                                        qa[:, :, 48].bitcast(F32), ALU.subtract).then_inc(self.s["qa_shift"], 1)
                        if what == "score":
                            n = u0 * JOBS + i
                            r = (n % JOBS) // HG
                            if i % (GROUPS * JOBS) == 0:
                                dve.wait_ge(self.s["cntT_out"], (c + 1) * sh.NQ * (sh.NT // sh.TP))
                                if self.dense:
                                    b = i // (GROUPS * JOBS)
                                    dve.wait_ge(self.s["bias_exp"], c * B + b + 1)
                                    nc.vector.tensor_scalar(W[:, :], W[:, :], lam[:, 5, b:b + 1], None,
                                                            ALU.mult).then_inc(self.s["self_dve"], 1)
                                    self.nd += 1
                                    dve.wait_ge(self.s["self_dve"], self.nd)
                                    nc.vector.scalar_tensor_tensor(W[:, :], self.CT[:, :], lam[:, 2, b:b + 1], W[:, :],
                                                                   ALU.mult, ALU.add).then_inc(self.s["w_ready"], 1)
                                    dve.wait_ge(self.s["w_ready"], c * B + b + 1)
                            dve.wait_ge(self.s["s_exp"], n + 1)
                            pr = Pr[:, n % JOBS, :]
                            nc.vector.scalar_tensor_tensor(pr, pr, FMAX, W[:, r * 1024:r * 1024 + 1024], ALU.min,
                                                           ALU.mult).then_inc(self.s["s_prob"], 1)
                        if what == "norm":
                            ug = u0 + i
                            b, g = divmod(i, GROUPS)
                            dve.wait_ge(self.s["den_full"], ug + 1)
                            den = psO[:, :, :].rearrange("p a b -> p (a b)")[:, 0:sh.SQ]
                            nc.vector.reciprocal(self.Rr[:, :], den).then_inc(self.s["recip"], 1)
                            dve.wait_ge(self.s["recip"], ug + 1)
                            t0 = b * S + c * sh.SQ
                            nc.vector.tensor_tensor(attT[:, g, t0:t0 + sh.SQ], self.OTs[:, :], self.Rr[:, :],
                                                    ALU.mult).then_inc(
                                                        *((self.s["att_ready"], 1) if ug < sh.NC * UNITS - 1
                                                          else (s["attention_done"], 1)))

        atts = []
        for n_, sh in enumerate(shapes):
            at = ExitStack()
            atts.append(Attention(sh, f"_{sh.T}", at))
            at.close()
        actx.close()

        WoT = sb("WoT", [P, GROUPS, D], F32)
        w1 = sb("w1", [P, KD, WIDTH], F32)
        w2 = sb("w2", [P, KW, D], F32)
        fc1 = sb("fc1", [P, KD, WIDTH], F32)
        Wc = sb("Wc", [P, B, KW, D], F32)
        rw = sb("rw", [P, KD, NE], F32)
        ew = sb("ew", [P, KD, NE * D], F32)
        aoT = sb("aoT", [P, 2, KD, QC], F32)
        hT = sb("hT", [P, 2, KW, QC], F32)
        x1T = sb("x1T", [P, 2, KD, QC], F32)
        cT = sb("cT", [P, 2, KD, QC], F32)
        top = sb("top", [P, 4, 8], F32)
        topi = sb("topi", [P, 4, 8], U32)
        rt = sb("rt", [P, 12, 4], F32)
        lg = sb("lg", [P, 4, 8], F32)
        dl = sb("dl", [P, 4, 8], F32)
        oh = sb("oh", [P, 2, 4, 8], F32)
        gate = sb("gate", [P, 2, 4, 8], F32)
        pw = sb("pw", [P, 2, 4], F32)
        y = sb("y", [P, 2, D], F32)
        LD = {k: sem("ld_" + k) for k in ("w2", "fc1", "wc", "rw", "ew")}
        d = {k: sem(k) for k in (
            "a_full", "a_out", "v_full", "v_out", "ao_out", "x1_out", "ct_out", "xn_full",
            "rt_full", "rt_out", "rt_exp", "rt_sub", "gate_ready", "ex_full", "ex_out", "self_dense", "stored0", "stored1")}
        TT = QC // P
        ABANK = RING
        VBANK = [psO[:, 0, :], psO[:, 1, :], psM[:, 0, :], psM[:, 1, :]]
        bo, b1, b2, f1b = cols[:, 0:2], cols[:, 2:10], cols[:, 10:12], cols[:, 12:20]
        STAGES = ("ao", "h", "y", "gelu", "c", "router", "experts")

        def dense_order():
            for pair in range(CHUNKS // 2):
                for stage in STAGES:
                    for c in (2 * pair, 2 * pair + 1):
                        yield stage, c

        def dense_jobs():
            na = nv = 0
            for stage, c in dense_order():
                if stage == "ao":
                    js = ["act"] * KD
                elif stage == "h":
                    js = ["act", "dve"] * (KW // 2)
                elif stage == "y":
                    js = ["dve"] * KD
                elif stage == "gelu":
                    js = ["act"] * KW
                elif stage == "c":
                    js = ["act"] * KD
                elif stage == "router":
                    js = ["dve"]
                else:
                    js = ["dve"] * (TT * 5)
                for i, e in enumerate(js):
                    if e == "act":
                        yield stage, c, i, e, na
                        na += 1
                    else:
                        yield stage, c, i, e, nv
                        nv += 1

        jobs = list(dense_jobs())
        upto = {}
        for stage, c, i, e, n in jobs:
            key = (stage, c, e)
            upto[key] = max(upto.get(key, 0), n + 1)

        def dense_tensor(pe):
            pe.wait_ge(s["attention_done"], 1)
            pe.wait_ge(L["wo"], 16)

            def bank(e, n):
                if n >= 4:
                    pe.wait_ge(d["a_out" if e == "act" else "v_out"], n - 3)
                return (ABANK if e == "act" else VBANK)[n % 4]

            def full(mm, e):
                mm.then_inc(d["a_full" if e == "act" else "v_full"], 1)

            def done(stage, c):
                for e, q in (("act", "a_out"), ("dve", "v_out")):
                    if (stage, c, e) in upto:
                        pe.wait_ge(d[q], upto[(stage, c, e)])

            loaded = set()

            def need(k, sm, v):
                if k not in loaded:
                    loaded.add(k)
                    pe.wait_ge(sm, v)

            for stage, c, i, e, n in jobs:
                q = c % 2
                ps = bank(e, n)
                if stage == "ao":
                    for g in range(GROUPS):
                        mm = nc.tensor.matmul(ps, WoT[:, g, i * P:i * P + P], attT[:, g, c * QC:(c + 1) * QC],
                                              start=(g == 0), stop=(g == GROUPS - 1))
                if stage == "h":
                    need("w1", L["w1"], 16)
                    if i == 0:
                        done("ao", c)
                    for k in range(KD):
                        mm = nc.tensor.matmul(ps, w1[:, k, i * P:i * P + P], aoT[:, q, k, :],
                                              start=(k == 0), stop=(k == KD - 1))
                if stage == "y":
                    need("w2", LD["w2"], 16)
                    if i == 0:
                        done("h", c)
                    for k in range(KW):
                        mm = nc.tensor.matmul(ps, w2[:, k, i * P:i * P + P], hT[:, q, k, :],
                                              start=(k == 0), stop=(k == KW - 1))
                if stage == "gelu":
                    need("fc1", LD["fc1"], 16)
                    if i == 0:
                        done("y", c)
                    for k in range(KD):
                        mm = nc.tensor.matmul(ps, fc1[:, k, i * P:i * P + P], x1T[:, q, k, :],
                                              start=(k == 0), stop=(k == KD - 1))
                if stage == "c":
                    need("wc", LD["wc"], 16 * 2 * B)
                    if i == 0:
                        done("gelu", c)
                    for k in range(KW):
                        mm = nc.tensor.matmul(ps, Wc[:, c * QC // S, k, i * P:i * P + P], hT[:, q, k, :],
                                              start=(k == 0), stop=(k == KW - 1))
                if stage == "router":
                    need("rw", LD["rw"], 16)
                    done("c", c)
                    for t in range(TT):
                        for k in range(KD):
                            mm = nc.tensor.matmul(ps[:, t * NE:(t + 1) * NE], cT[:, q, k, t * P:t * P + P], rw[:, k, :],
                                                  start=(k == 0), stop=(k == KD - 1))
                if stage == "experts":
                    need("ew", LD["ew"], 16)
                    t, j = divmod(i, 5)
                    if j == 0:
                        for k in range(KD):
                            mm = nc.tensor.transpose(ps[:, k * P:k * P + P], x1T[:, q, k, t * P:t * P + P], ident)
                    else:
                        for k in range(KD):
                            mm = nc.tensor.matmul(ps, cT[:, q, k, t * P:t * P + P], ew[:, k, (j - 1) * 512:j * 512],
                                                  start=(k == 0), stop=(k == KD - 1))
                full(mm, e)

        def dense_act(act):
            act.wait_ge(L["cols"], 16)
            first_c = True
            for stage, c, i, e, n in jobs:
                q = c % 2
                ps = ABANK[n % 4]
                if stage == "router":
                    act.wait_ge(d["rt_sub"], c + 1)
                    nc.scalar.activation(dl[:, :, :], dl[:, :, :], ACT.Exp).then_inc(d["rt_exp"], 1)
                if e != "act":
                    continue
                act.wait_ge(d["a_full"], n + 1)
                if stage == "ao":
                    nc.scalar.activation(aoT[:, q, i, :], ps, ACT.Identity, bias=bo[:, i:i + 1]).then_inc(d["a_out"], 1)
                if stage == "h":
                    nc.scalar.activation(hT[:, q, i, :], ps, ACT.Relu, bias=b1[:, i:i + 1]).then_inc(d["a_out"], 1)
                if stage == "gelu":
                    nc.scalar.activation(hT[:, q, i, :], ps, ACT.Gelu, bias=f1b[:, i:i + 1]).then_inc(d["a_out"], 1)
                if stage == "c":
                    if first_c:
                        act.wait_ge(L["small"], 16 * 6)
                        first_c = False
                    nc.scalar.activation(cT[:, q, i, :], ps, ACT.Identity,
                                         bias=cbias[:, c * QC // S, i:i + 1]).then_inc(d["a_out"], 1)

        def dense_vector(dve):
            dve.wait_ge(L["cols"], 16)
            nd = [0]

            def link(ins):
                nd[0] += 1
                ins.then_inc(d["self_dense"], 1)

            def settle():
                dve.wait_ge(d["self_dense"], nd[0])

            for stage, c, i, e, n in jobs:
                if e != "dve":
                    continue
                q = c % 2
                ps = VBANK[n % 4]
                dve.wait_ge(d["v_full"], n + 1)
                if stage == "h":
                    nc.vector.tensor_scalar(hT[:, q, i, :], ps, b1[:, i:i + 1], 0.0, ALU.add, ALU.max).then_inc(d["v_out"], 1)
                if stage == "y":
                    nc.vector.scalar_tensor_tensor(x1T[:, q, i, :], ps, b2[:, i:i + 1], xT[:, i, c * QC:(c + 1) * QC],
                                                   ALU.add, ALU.add).then_inc(d["v_out"], 1)
                if stage == "router":
                    if c:
                        dve.wait_ge(d["rt_exp"], c)
                    nc.vector.tensor_copy(lg[:, :, :], ps[:, 0:TT * NE].rearrange("p (t e) -> p t e", e=NE)).then_inc(d["v_out"], 1)
                    dve.wait_ge(d["v_out"], n + 1)
                    for t in range(TT):
                        link(nc.vector.max(top[:, t, :], lg[:, t, :]))
                    settle()
                    for t in range(TT):
                        link(nc.vector.max_index(topi[:, t, :], top[:, t, :], lg[:, t, :]))
                    nc.vector.tensor_tensor(dl[:, :, :], lg[:, :, :], top[:, :, 0:1].to_broadcast([P, TT, NE]),
                                            ALU.subtract).then_inc(d["rt_sub"], 1)
                    settle()
                    link(nc.vector.tensor_copy(rt[:, 0:2, :].rearrange("p k t -> p t k"), topi[:, :, 0:2]))
                    settle()
                    for k in range(2):
                        link(nc.vector.tensor_tensor(oh[:, k, :, :], iota8[:, None, :].to_broadcast([P, TT, NE]),
                                                     rt[:, k, :, None].to_broadcast([P, TT, NE]), ALU.is_equal))
                    dve.wait_ge(d["rt_exp"], c + 1)
                    link(nc.vector.tensor_reduce(rt[:, 2, :], dl[:, :, :], AX.X, ALU.add))
                    settle()
                    link(nc.vector.reciprocal(rt[:, 3, :], rt[:, 2, :]))
                    settle()
                    link(nc.vector.tensor_tensor(dl[:, :, :], dl[:, :, :], rt[:, 3, :, None].to_broadcast([P, TT, NE]), ALU.mult))
                    settle()
                    for k in range(2):
                        link(nc.vector.tensor_tensor(lg[:, :, :], dl[:, :, :], oh[:, k, :, :], ALU.mult))
                        settle()
                        link(nc.vector.tensor_reduce(rt[:, 4 + k, :], lg[:, :, :], AX.X, ALU.add))
                        settle()
                    link(nc.vector.scalar_tensor_tensor(rt[:, 6, :], rt[:, 4, :], 1e-6, rt[:, 5, :], ALU.add, ALU.add))
                    settle()
                    link(nc.vector.reciprocal(rt[:, 7, :], rt[:, 6, :]))
                    settle()
                    for k in range(2):
                        link(nc.vector.tensor_tensor(rt[:, 8 + k, :], rt[:, 4 + k, :], rt[:, 7, :], ALU.mult))
                    settle()
                    for k in range(2):
                        link(nc.vector.tensor_tensor(rt[:, 10 + k, :], rt[:, 4 + k, :], rt[:, 8 + k, :], ALU.mult))
                        link(nc.vector.tensor_tensor(oh[:, k, :, :], oh[:, k, :, :],
                                                     rt[:, 8 + k, :, None].to_broadcast([P, TT, NE]), ALU.mult))
                    settle()
                    link(nc.vector.tensor_tensor(pw[:, q, :], rt[:, 10, :], rt[:, 11, :], ALU.add))
                    link(nc.vector.tensor_tensor(gate[:, q, :, :], oh[:, 0, :, :], oh[:, 1, :, :], ALU.add))
                    settle()
                if stage == "experts":
                    t, j = divmod(i, 5)
                    k = c * TT + t
                    if j == 0:
                        if k >= 2:
                            dve.wait_ge(d[f"stored{k % 2}"], 16 * (k // 2))
                        ins = nc.vector.tensor_scalar(y[:, k % 2, :], ps[:, 0:D], pw[:, q, t:t + 1], None, ALU.add)
                        ins.then_inc(d["v_out"], 1)
                        dve.wait_ge(d["v_out"], n + 1)
                    else:
                        e0 = 2 * (j - 1)
                        link(nc.vector.scalar_tensor_tensor(y[:, k % 2, :], ps[:, 0:D], gate[:, q, t, e0:e0 + 1],
                                                            y[:, k % 2, :], ALU.mult, ALU.add))
                        settle()
                        nc.vector.scalar_tensor_tensor(y[:, k % 2, :], ps[:, D:2 * D], gate[:, q, t, e0 + 1:e0 + 2],
                                                       y[:, k % 2, :], ALU.mult, ALU.add).then_inc(d["v_out"], 1)
                        dve.wait_ge(d["v_out"], n + 1)
                        if j == 4:
                            pass

        block = ctx.enter_context(nc.Block())

        @block.sync
        def _(sp):
            sp.dma_start(cst[:, :], io["consts"]).then_inc(L["cst"], 16)
            sp.dma_start(ramp, io["ramp"]).then_inc(L["cst"], 16)
            sp.dma_start(wqkv[:, :, :], io["wqkv"]).then_inc(L["wqkv"], 16)
            sp.dma_start(bqkv[:, :], io["bqkv"]).then_inc(L["wqkv"], 16)
            sp.dma_start(xT[:, :, :], io["xT"]).then_inc(L["x"], 16)
            sp.dma_start(idx, io["idx"]).then_inc(L["idx"], 16)
            sp.dma_start(idm[:, :, :], io["idm"]).then_inc(L["idx"], 16)
            sp.dma_start(lam[:, 0, :], io["u"]).then_inc(L["u"], 16)
            sp.dma_start(small[:, 0:2], io["expert_id"]).then_inc(L["small"], 16)
            sp.dma_start(cols[:, :], io["cols"]).then_inc(L["cols"], 16)
            sp.wait_ge(L["small"], 16)
            eid = [sp.value_load(small[0:1, b:b + 1], min_val=0, max_val=15) for b in range(B)]
            for b in range(B):
                sp.dma_start(cbias[:, b, 0:1], io["cshared"][:, 0:1], allow_slow_non_contiguous=True).then_inc(L["small"], 16)
                sp.dma_start(cbias[0:64, b, 1:2], io["cshared"][0:64, 1:2], allow_slow_non_contiguous=True).then_inc(L["small"], 16)
            for b in range(B):
                sp.dma_start(cbias[64:128, b, 1:2],
                             io["eb"][bass.ds(eid[b], 1), :].rearrange("a p -> p a"), allow_slow_non_contiguous=True).then_inc(L["small"], 16)
            def load_masks(att):
                for c in range(att.sh.NC if att.dense else 0):
                    if c:
                        sp.wait_ge(att.s["bias_exp"], B * c)
                    sp.dma_start(att.maskT[:, :].rearrange("p (t q) -> p t q", q=att.sh.SQ // 4),
                                 io["maskT"][:, :, c * att.sh.SQ // 4:(c + 1) * att.sh.SQ // 4]).then_inc(L["mask"], 16)
            either(sp, load_masks)
            sp.wait_ge(s["attention_done"], 1)
            sp.dma_start(WoT[:, :, :], io["WoT"]).then_inc(L["wo"], 16)
            sp.dma_start(w1[:, :, :], io["w1"]).then_inc(L["w1"], 16)
            sp.dma_start(w2[:, :, :], io["w2"]).then_inc(LD["w2"], 16)
            sp.dma_start(fc1[:, :, :], io["fc1"]).then_inc(LD["fc1"], 16)
            for b in range(B):
                sp.dma_start(Wc[:, b, :, 0:SHARED], io["fc2"]).then_inc(LD["wc"], 16)
                sp.dma_start(Wc[:, b, :, SHARED:D], io["experts"][:, bass.ds(eid[b], 1), :, :].rearrange(
                    "p a k o -> p (a k) o")).then_inc(LD["wc"], 16)
            sp.dma_start(rw[:, :, :], io["rw"]).then_inc(LD["rw"], 16)
            sp.dma_start(ew[:, :, :], io["ew"]).then_inc(LD["ew"], 16)
            k = 0
            for stage, c, i, e, n in jobs:
                if stage == "experts" and i % 5 == 4:
                    sp.wait_ge(d["v_out"], n + 1)
                    t0 = (c * TT + i // 5) * P
                    sp.dma_start(out[t0:t0 + P, :], y[:, k % 2, :]).then_inc(d[f"stored{k % 2}"], 16)
                    k += 1
            for i in range(2):
                sp.wait_ge(d[f"stored{i}"], 16 * (k // 2))

        @block.gpsimd
        def _(pool):
            setup_pool(pool)
            either(pool, lambda att: att.pool(pool))

        @block.tensor
        def _(pe):
            setup_tensor(pe)
            either(pe, lambda att: att.tensor(pe))
            dense_tensor(pe)

        @block.scalar
        def _(act):
            setup_act(act)
            either(act, lambda att: att.act(act))
            dense_act(act)

        @block.vector
        def _(dve):
            setup_dve(dve)
            dve.wait_ge(L["wqkv"], 32)
            either(dve, lambda att: att.vector(dve))
            dense_vector(dve)


_OUT = "out_dram"


def _consts():
    c = np.zeros((P, C_END), np.float32)
    p = np.arange(P)
    c[:, C_ID:C_ID + P] = np.eye(P, dtype=np.float32)
    c[:, C_HM:C_HM + 8] = (p[:, None] // DH == np.arange(8)[None, :])
    c[:, C_SEL:C_SEL + P] = (p[:, None] == VW * (p[None, :] // VW) + DH)
    c[:, C_E8:C_E8 + 8] = np.arange(8)
    return c


def kernel(x, itok_Sx32_0_1023, condB_uprev, itok_B_0_15, mask_SxS_bk0, mask_Sx32_bk1, L0_cond_Wq, L0_cond_bq,
           L0_cond_Wk, L0_cond_bk, L0_cond_Wv, L0_cond_bv, L0_cond_Wo, L0_cond_bo, L0_ffn_w1, L0_ffn_b1, L0_ffn_w2,
           L0_ffn_b2, L1_cond_fc1_w, L1_cond_fc1_b, L1_cond_fc2_w, L1_cond_fc2_b, L1_cond_experts_w,
           L1_cond_experts_b, L1_ffn_router_w, L1_ffn_expert_weights):
    import concourse.bacc as bacc
    from concourse.bass_utils import run_bass_kernel_spmd

    def rows(a):
        a = np.asarray(a)
        return np.ascontiguousarray(a.reshape(a.shape[0] // P, P, -1).transpose(1, 0, 2))

    def spread(*vs):
        return np.ascontiguousarray(np.broadcast_to(np.concatenate([np.asarray(v) for v in vs])[None, :],
                                                    (P, sum(v.shape[0] for v in vs))))

    def column(v):
        return np.asarray(v).reshape(-1, P).T

    A = np.asarray
    wo = np.zeros((H, VW, D), np.float32)
    wo[:, 0:DH, :] = A(L0_cond_Wo).T.reshape(H, DH, D)
    fc2b = np.zeros((2, P), np.float32)
    fc2b.reshape(-1)[0:SHARED] = A(L1_cond_fc2_b)
    arrays = {
        "consts": _consts(),
        "ramp": np.ascontiguousarray(np.broadcast_to(np.arange(1, S + 1, dtype=np.float32), (P, S))),
        "xT": rows(A(x).reshape(N, D).T),
        "wqkv": rows(np.concatenate([A(L0_cond_Wq).T, A(L0_cond_Wk).T, A(L0_cond_Wv).T], axis=1)),
        "bqkv": spread(L0_cond_bq, L0_cond_bk, L0_cond_bv),
        "idx": np.ascontiguousarray(A(itok_Sx32_0_1023).reshape(S // P, P, K_SPARSE).transpose(1, 0, 2)),
        "idm": np.ascontiguousarray(A(mask_Sx32_bk1).view(np.int32).reshape(S // P, P, K_SPARSE // 4).transpose(1, 0, 2)),
        "u": spread(condB_uprev),
        "expert_id": np.ascontiguousarray(A(itok_B_0_15).reshape(1, B)),
        "cols": np.ascontiguousarray(np.concatenate(
            [column(L0_cond_bo), column(L0_ffn_b1), column(L0_ffn_b2), column(L1_cond_fc1_b)], axis=1)),
        "cshared": np.ascontiguousarray(fc2b.T),
        "eb": A(L1_cond_experts_b),
        "WoT": rows(wo.reshape(H * VW, D)),
        "w1": rows(L0_ffn_w1),
        "maskT": rows(np.ascontiguousarray(A(mask_SxS_bk0).T).view(np.int32)),
        "w2": rows(L0_ffn_w2),
        "fc1": rows(A(L1_cond_fc1_w).T),
        "fc2": rows(A(L1_cond_fc2_w).T),
        "experts": np.ascontiguousarray(A(L1_cond_experts_w).transpose(2, 0, 1).reshape(KW, P, 16, PART).transpose(1, 2, 0, 3)),
        "rw": rows(A(L1_ffn_router_w).T),
        "ew": rows(A(L1_ffn_expert_weights).transpose(1, 0, 2).reshape(D, NE * D)),
    }
    nc = bacc.Bacc("TRN2", target_bir_lowering=False, num_devices=1)
    io = {k: nc.dram_tensor(k + "_dram", v.shape, mybir.dt.from_np(v.dtype), kind="ExternalInput").ap()
          for k, v in arrays.items()}
    out = nc.dram_tensor(_OUT, (N, D), F32, kind="ExternalOutput").ap()
    bass_adaln_ffn(nc, io, out, **OPTIONS)
    r = run_bass_kernel_spmd(nc, [{k + "_dram": v for k, v in arrays.items()}], core_ids=[0])
    return r.results[0][_OUT].reshape(B, S, D)


OPTIONS = dict()
```

```python
import concourse.bass as bass
from concourse import mybir
from contextlib import ExitStack
import numpy as np

F32 = mybir.dt.float32
F32R = mybir.dt.float32r
F16 = mybir.dt.float16
BF16 = mybir.dt.bfloat16
I32 = mybir.dt.int32
U8 = mybir.dt.uint8
U32 = mybir.dt.uint32
ALU = mybir.AluOpType
ACT = mybir.ActivationFunctionType
AX = mybir.AxisListType

P = 128
B, S, D, H = 2, 1024, 256, 16
DH = D // H
K_SPARSE = 32
N = B * S
KD = D // P
WIDTH = 1024
KW = WIDTH // P
SHARED = 192
PART = D - SHARED
NE = 8
HG = 4
GROUPS = H // HG
AUG = 64
QB = 4
VW = 32
VC = DH + 1
FEW_KEYS = 256
LAMBDA_MAX, ALPHA = 10.0, 5.0
SCALE = 1.0 / 4.0
BIG = 1.0e30
FMAX = 3.0e38
QC = 512
CHUNKS = N // QC
UNITS = B * GROUPS
JOBS = 8
OF_POOL = (3, 8, 13, 18, 23, 28)
OF_ACT = (4, 10, 16, 22, 27)
NUMBER = {"_pool": len(OF_POOL), "_act": len(OF_ACT), "_dve": K_SPARSE - len(OF_POOL) - len(OF_ACT)}
AHEAD_AT = (1, 1, 4, 6)
LAG = 12

C_ID, C_HM, C_E8, C_END = 0, 128, 136, 144


class Shape:

    def __init__(self, keys):
        self.T = keys
        self.NT = keys // P
        self.SQ = 2048 * P // keys
        self.NQ = self.SQ // P
        self.NC = S // self.SQ
        self.NBK = keys // 256
        self.CP = min(512, self.SQ)
        self.NB = 2 if keys <= 256 else 1
        self.LEAD = 4 if self.NB == 2 else 0
        self.SPLIT = 6 if self.NB == 2 else 0
        self.TP = min(self.NT, 4)
        self.QP = min(self.NQ, 4)
        self.PROJECTED = B * self.NT + B * S // P
        self.EVERY = K_SPARSE * self.NQ // self.PROJECTED
        self.LATER = K_SPARSE * self.NQ // self.EVERY - self.PROJECTED


def bass_adaln_ffn(nc, io, out):
    ctx = ExitStack()
    with ctx:
        def sb(name, shape, dt, at=ctx):
            return at.enter_context(nc.sbuf_tensor(name, shape, dt))

        def sem(name):
            return ctx.enter_context(nc.semaphore(name))

        cst = sb("cst", [P, C_END], F32)
        ident, headmask, iota8 = cst[:, C_ID:C_ID + P], cst[:, C_HM:C_HM + 8], cst[:, C_E8:C_E8 + 8]
        attT = sb("attT", [P, KD, N], F32)
        cols = sb("cols", [P, 20], F32)
        cbias = sb("cbias", [P, B, KD], F32)
        small = sb("small", [1, 8], I32)
        flags = sb("flags", [P, 4], F32)
        few = sb("few", [1, 4], I32)

        psG = ctx.enter_context(nc.psum_tensor("psG", [P, 2, 512], F32))
        psS = ctx.enter_context(nc.psum_tensor("psS", [P, 2, 512], F32))
        psO = ctx.enter_context(nc.psum_tensor("psO", [P, 2, 512], F32))
        psM = ctx.enter_context(nc.psum_tensor("psM", [P, 2, 512], F32))
        RING = [psG[:, 0, :], psG[:, 1, :], psS[:, 0, :], psS[:, 1, :]]

        actx = ExitStack()
        shapes = [Shape(FEW_KEYS), Shape(S)]
        Qn = sb("Qn", [P, B, S // P, D], F32, actx)
        Mneg = sb("Mneg", [P, 2048], BF16, actx)
        iota16 = sb("iota16", [P, 1024], F16, actx)
        idm = sb("idm", [P, S // P, K_SPARSE // 4], I32, actx)
        idx1 = sb("idx1", [P, S // P, K_SPARSE], F32, actx)
        ident16 = sb("ident16", [P, P], F16, actx)
        identm = sb("identm", [P, B, P], BF16, actx)
        lam = sb("lam", [P, 6, B], F32, actx)
        Pr = sb("Pr", [P, 2 * HG, 1024], F32, actx)
        xT = Pr[:, 0:4, :].rearrange("p (k a) n -> p k (a n)", k=KD)
        wqkv = Pr[:, 4:6, 0:3 * D]
        bqkv = Pr[:, 6, 0:3 * D]
        W = sb("W", [P, 2048], F32, actx)
        idx = W[:, 1024:1280].bitcast(I32).rearrange("p (q k) -> p q k", k=K_SPARSE)
        idmf = W[:, 1280:1536].rearrange("p (q k) -> p q k", k=K_SPARSE)
        shift = sb("shift", [P, QB, HG], F32, actx)
        shiftb = sb("shiftb", [P, HG, 4], F32, actx)
        Qa = sb("Qa", [P, QB, HG, AUG], F32R, actx)
        Ka = sb("Ka", [P, 2, HG, AUG], F32R, actx)

        L = {k: sem("ld_" + k) for k in ("cst", "ramp", "x", "wqkv", "idx", "u", "small", "cols", "mask")}
        s = {k: sem(k) for k in ("consts_ready", "idx_ready", "lam_exp", "cleared", "self_setup", "greatest", "greatest_full",
                                 "flag_ready", "attention_done")}
        ATTENTION_SEMS = (
            "self_dve", "self_pool", "self_act", "zeroed", "zeroed_keys", "proj_full", "proj_out", "kv_out",
            "cnt_out", "cntT_full", "cntT_out", "bias_exp", "w_ready", "qg_full", "qg_out",
            "kt_full", "kt_out", "kg_ready", "ka_ready", "ka_full", "kp_out", "qa_split",
            "qa_shift", "qa_full", "qat_out", "g_scores", "g_max", "s_scores", "s_exp",
            "s_prob", "qa_copied",
            "pv_done", "ot_out", "on_full", "on_out", "recip", "at_full",
            "at_out", "shift_hi", "shift_ready", "eq_ready_dve", "eq_used_dve", "eq_ready_pool", "eq_used_pool",
            "eq_ready_act", "eq_used_act")

        def setup_pool(pool):
            nc.gpsimd.memset(Qa[:, :, :, :].bitcast(F32), 0.0).then_inc(s["cleared"], 1)
            nc.gpsimd.memset(Ka[:, :, :, :].bitcast(F32), 0.0).then_inc(s["cleared"], 1)
            pool.wait_ge(s["cleared"], 2)
            nc.gpsimd.memset(Ka[:, :, :, 48:50].bitcast(F32), 1.0).then_inc(s["cleared"], 1)

        def setup_dve(dve):
            dve.wait_ge(L["idx"], 32)
            nc.vector.tensor_copy(idmf, idm[:, :, :].bitcast(U8)).then_inc(s["self_setup"], 1)
            nc.vector.tensor_copy(idx1[:, :, :], idx).then_inc(s["self_setup"], 1)
            dve.wait_ge(s["self_setup"], 2)
            nc.vector.scalar_tensor_tensor(idx1[:, :, :], idx1[:, :, :], 1.0, idmf,
                                           ALU.add, ALU.mult).then_inc(s["idx_ready"], 1)
            dve.wait_ge(s["idx_ready"], 1)
            nc.vector.tensor_reduce(flags[:, 0:1], idx1[:, :, :], AX.XY, ALU.max).then_inc(s["greatest"], 1)
            dve.wait_ge(s["lam_exp"], 1)
            nc.vector.tensor_scalar(lam[:, 1, :], lam[:, 1, :], LAMBDA_MAX, None, ALU.mult).then_inc(s["self_setup"], 1)
            dve.wait_ge(s["self_setup"], 3)
            nc.vector.tensor_scalar(lam[:, 2, :], lam[:, 1, :], 1.0, None, ALU.is_ge).then_inc(s["self_setup"], 1)
            nc.vector.tensor_scalar(lam[:, 3, :], lam[:, 1, :], 1.0, None, ALU.min).then_inc(s["self_setup"], 1)
            nc.vector.tensor_scalar(lam[:, 4, :], lam[:, 1, :], 1.0, -1.0, ALU.min, ALU.mult).then_inc(s["self_setup"], 1)
            dve.wait_ge(s["self_setup"], 6)
            nc.vector.tensor_scalar(lam[:, 5, :], lam[:, 2, :], -1.0, 1.0, ALU.mult, ALU.add).then_inc(s["self_setup"], 1)
            dve.wait_ge(L["cst"], 16)
            nc.vector.tensor_copy(ident16[:, :], ident).then_inc(s["consts_ready"], 1)
            for b in range(B):
                nc.vector.tensor_scalar(identm[:, b, :], ident, lam[:, 2, b:b + 1], None,
                                        ALU.mult).then_inc(s["consts_ready"], 1)
            dve.wait_ge(s["greatest_full"], 1)
            nc.vector.tensor_reduce(flags[0:1, 1:2], psM[0:1, 0, 0:P], AX.X, ALU.max).then_inc(s["self_setup"], 1)
            dve.wait_ge(s["self_setup"], 8)
            nc.vector.scalar_tensor_tensor(flags[0:1, 2:3], flags[0:1, 1:2], float(FEW_KEYS), lam[0:1, 2, 0:1],
                                           ALU.is_le, ALU.mult).then_inc(s["self_setup"], 1)
            dve.wait_ge(s["self_setup"], 9)
            nc.vector.tensor_tensor(few[0:1, 0:1], flags[0:1, 2:3], lam[0:1, 2, 1:2],
                                    ALU.mult).then_inc(s["flag_ready"], 1)

        def setup_tensor(pe):
            pe.wait_ge(s["greatest"], 1)
            pe.wait_ge(L["cst"], 16)
            nc.tensor.transpose(psM[0:1, 0, 0:P], flags[:, 0:1], ident).then_inc(s["greatest_full"], 1)

        def either(eng, run):
            eng.wait_ge(s["flag_ready"], 1)
            flag = eng.value_load(few[0:1, 0:1], min_val=0, max_val=1)
            with eng.If(flag == 1):
                run(atts[0])
            with eng.Else():
                run(atts[1])

        def setup_act(act):
            act.wait_ge(L["u"], 16)
            nc.scalar.activation(lam[:, 1, :], lam[:, 0, :], ACT.Exp, scale=-ALPHA).then_inc(s["lam_exp"], 1)

        class Attention:

            def __init__(self, sh, tag, at):
                self.sh = sh
                self.s = {k: sem(k + tag) for k in ATTENTION_SEMS}
                self.nd = self.np = self.na = 0
                self.Kn = sb("Kn" + tag, [P, B, sh.NT, D], F32, at)
                self.VA = sb("VA" + tag, [P, B, sh.NT, H * VC], F32, at)
                self.QG = sb("QG" + tag, [P, 2, sh.SQ], F32R, at)
                self.KT = sb("KT" + tag, [P, sh.T], F32, at)
                if sh.NB == 1:
                    self.compared(tag)
                self.KG = sb("KG" + tag, [P, sh.NB, HG, sh.T], F32R, at)
                self.KP = sb("KP" + tag, [P, sh.NB, HG, sh.T], F32R, at)
                if sh.NB == 2:
                    self.compared(tag)
                self.QAT = sb("QAT" + tag, [P, 2, 2, sh.SQ], F32R, at)
                self.OTs = sb("OTs" + tag, [P, sh.SQ], F32, at)
                self.An = sb("An" + tag, [P, sh.NQ, P], F32, at)
                self.rden = sb("rden" + tag, [P, sh.NQ, HG], F32, at)
                self.Cn = sb("Cn" + tag, [P, sh.T], F32, at)
                self.dense = sh.T == S
                if self.dense:
                    self.CT = sb("CT" + tag, [P, 2048], BF16, at)
                    self.maskT = sb("maskT" + tag, [P, 512], I32, at)
                else:
                    self.CT = W

            def compared(self, tag):
                sh = self.sh
                self.RINGS = {"_dve": 12, "_pool": 6, "_act": 6} if sh.NB == 2 else {"_dve": 3, "_pool": 2, "_act": 2}
                self.NA = 2 if sh.NB == 2 else 1
                with ExitStack() as place:
                    self.EQ = {who: sb("EQ" + who + tag, [P, n, sh.T], F16, place) for who, n in self.RINGS.items()}
                    self.apart = sb("apart" + tag, [P, self.NA, sh.T], F16, place)

            def lister(self, k):
                return "_pool" if k in OF_POOL else "_act" if k in OF_ACT else "_dve"

            def counting(self, c):
                tiles = range(c * self.sh.NQ, (c + 1) * self.sh.NQ)
                behind = not self.dense
                for m in tiles:
                    for k in range(K_SPARSE):
                        yield "entry", m, k
                        if behind and m > tiles[0] and k == 10:
                            yield "counts", m - 1, 0
                        if behind and m > tiles[0] and k == 18:
                            yield "turn_counts", m - 1, 0
                        if behind and m > tiles[0] and k == 30:
                            yield "turned_counts", m - 1, 0
                    if not behind or m == tiles[-1]:
                        yield "counts", m, 0
                        yield "turn_counts", m, 0
                        yield "turned_counts", m, 0

            def guard_bank(self, i):
                if self.dense or i > LAG:
                    return psG, i - 1
                return (psS if i % 2 else psG), i - 2

            def bank_of_counts(self, m):
                if self.dense:
                    return psO[:, :, :].rearrange("p a b -> p (a b)")
                return psO[:, m % 2, 0:self.sh.T]

            def compare(self, eng, who, m, k, op):
                mine = [j for j in range(K_SPARSE) if self.lister(j) == who]
                e, n = m * len(mine) + mine.index(k), self.RINGS[who]
                if e == 0:
                    eng.wait_ge(L["ramp"], 16)
                    eng.wait_ge(s["idx_ready"], 1)
                if self.dense and m % self.sh.NQ == 0 and k == mine[0] and m:
                    eng.wait_ge(self.s["g_scores"], 2 * JOBS * UNITS * (m // self.sh.NQ))
                if e >= n:
                    eng.wait_ge(self.s["eq_used" + who], e - n + 1)
                op(self.EQ[who][:, e % n, :], idx1[:, m, k:k + 1]).then_inc(self.s["eq_ready" + who], 1)

            def compare_on(self, eng, nceng, who, m, k):
                self.compare(eng, who, m, k, lambda eq, one: nceng.tensor_scalar(
                    eq, iota16[:, 0:self.sh.T], one, None, ALU.is_equal))

            def compare_act(self, act, m, k):
                def op(eq, one):
                    apart = self.apart[:, self.na % self.NA, :]
                    if self.na >= self.NA:
                        act.wait_ge(self.s["eq_ready_act"], self.na - self.NA + 1)
                    self.na += 1
                    nc.scalar.activation(apart, iota16[:, 0:self.sh.T], ACT.Abs, bias=one,
                                         scale=-1.0).then_inc(self.s["self_act"], 1)
                    act.wait_ge(self.s["self_act"], self.na)
                    return nc.scalar.activation(eq, apart, ACT.Relu, bias=1.0, scale=-1.0)
                self.compare(act, "_act", m, k, op)

            def query_tile(self, c, m, b, g):
                q = Qn[:, b, c * self.sh.NQ + m % self.sh.NQ, g * HG * DH:(g + 1) * HG * DH]
                return q.rearrange("p (h d) -> p h d", d=DH), Qa[:, m % QB, :, :]

            def due(self, c):
                sh = self.sh
                n_jobs = UNITS * JOBS
                for t in range(-sh.LEAD, n_jobs + LAG + 20):
                    n = t - LAG
                    if (t + sh.LEAD) % JOBS == 0 and 0 <= (t + sh.LEAD) // JOBS < UNITS:
                        yield "guard_keys", (t + sh.LEAD) // JOBS
                    if (n + sh.SPLIT) % JOBS == 0 and 0 <= (n + sh.SPLIT) // JOBS < UNITS:
                        yield "split_keys", (n + sh.SPLIT) // JOBS
                    for tt in range(sh.NT):
                        ahead = n + sh.LEAD - (tt if sh.NB == 2 else 0)
                        if ahead % JOBS == 0 and 0 <= ahead // JOBS < UNITS:
                            yield "score_keys", ahead // JOBS * sh.NT + tt
                    if 0 <= n < n_jobs:
                        yield "score", n
                    if 0 <= t < n_jobs:
                        yield "guard", t
                    if 1 <= n <= n_jobs:
                        yield "weigh", n - 1
                    if t >= 3 and (t - 2) % sh.NBK == 0 and (t - 2) // sh.NBK - 1 < n_jobs // sh.NBK:
                        yield "query_rows", (t - 2) // sh.NBK - 1
                    for half in range(2):
                        after = n - 6 - half
                        if after >= 0 and after % HG == 0 and after // HG < 2 * UNITS:
                            yield f"values{half}", after // HG
                    if n >= 11 and (n - 11) % JOBS == 0 and (n - 11) // JOBS < UNITS:
                        yield "take", (n - 11) // JOBS
                    if n >= 13 and (n - 13) % JOBS == 0 and (n - 13) // JOBS < UNITS:
                        yield "norm", (n - 13) // JOBS
                    if n >= 23 and (n - 23) % (2 * JOBS) == 0 and (n - 23) // (2 * JOBS) < UNITS // 2:
                        yield "turn", (n - 23) // (2 * JOBS)
                    if not self.dense and t == n_jobs - 4:
                        yield "first_input", 0
                    for j, after in enumerate(AHEAD_AT):
                        if not self.dense and n - n_jobs == after:
                            yield "ahead", j

            def pool(self, pool):
                sh = self.sh
                for c in range(sh.NC):
                    for m in range(c * sh.NQ, (c + 1) * sh.NQ):
                        for k in OF_POOL:
                            self.compare_on(pool, nc.gpsimd, "_pool", m, k)
                    if c == 0:
                        nc.gpsimd.memset(self.KP[:, :, :, :].bitcast(F32), 0.0).then_inc(self.s["zeroed_keys"], 1)
                    pool.wait_ge(self.s["kv_out"], B * sh.NT)
                    if self.dense:
                        pool.wait_ge(self.s["cnt_out"], 2 * (c + 1) * sh.NQ)
                    for what, i in self.due(c):
                        if what == "guard" and not self.dense and i % JOBS == 6 and i // JOBS < len(EARLY):
                            split_lo(nc.gpsimd, pool, EARLY[i // JOBS:i // JOBS + 1])
                        if what == "first_input":
                            attention_lo(pool, 0)
                        if what == "guard_keys":
                            g = i % GROUPS
                            ug = c * UNITS + i
                            pool.wait_ge(self.s["kt_out"], (ug // 2 + 1) * (sh.NT // sh.TP))
                            if ug >= sh.NB and not (self.dense and i == 0):
                                pool.wait_ge(self.s["g_scores"], 2 * JOBS * (ug - sh.NB + 1))
                            hm = headmask[:, HG * (g % 2):HG * (g % 2) + HG]
                            nc.gpsimd.tensor_tensor(
                                self.KG[:, ug % sh.NB, :, :],
                                self.KT[:, None, :].to_broadcast([P, HG, sh.T]),
                                hm[:, :, None].to_broadcast([P, HG, sh.T]), ALU.mult).then_inc(self.s["kg_ready"], 1)
                        if what == "split_keys":
                            b, g = divmod(i, GROUPS)
                            ug = c * UNITS + i
                            for tt in range(sh.NT):
                                m = ug * sh.NT + tt
                                if m >= 2:
                                    pool.wait_ge(self.s["ka_full"], m - 1)
                                k = self.Kn[:, b, tt, g * HG * DH:(g + 1) * HG * DH].rearrange("p (h d) -> p h d", d=DH)
                                ka = Ka[:, m % 2, :, :]
                                nc.gpsimd.tensor_copy(ka[:, :, 0:16], k).then_inc(self.s["self_pool"], 1)
                                nc.gpsimd.tensor_copy(ka[:, :, 32:48], k)
                                self.np += 1
                                pool.wait_ge(self.s["self_pool"], self.np)
                                nc.gpsimd.tensor_tensor(ka[:, :, 16:32], k, ka[:, :, 0:16].bitcast(F32),
                                                        ALU.subtract).then_inc(self.s["ka_ready"], 1)
                        if what == "guard" and i % sh.NBK == 0:
                            u = i // JOBS
                            b, g = divmod(u, GROUPS)
                            m = c * UNITS * sh.NQ + i // sh.NBK
                            pool.wait_ge(self.s["qa_copied"], m + 1)
                            q, qa = self.query_tile(c, m, b, g)
                            nc.gpsimd.tensor_tensor(qa[:, :, 32:48], q, qa[:, :, 0:16].bitcast(F32),
                                                    ALU.subtract).then_inc(self.s["qa_split"], 1)
                        if what == "guard" and i % sh.NBK == sh.NBK - 1:
                            m = c * UNITS * sh.NQ + i // sh.NBK
                            qa = Qa[:, m % QB, :, :]
                            if sh.NBK > 1:
                                pool.wait_ge(self.s["shift_ready"], m + 1)
                            else:
                                pool.wait_ge(self.s["g_max"], 2 * (m + 1))
                            nc.gpsimd.tensor_copy(qa[:, :, 48], shift[:, m % QB, :]).then_inc(self.s["shift_hi"], 1)
                            pool.wait_ge(self.s["shift_hi"], m + 1)
                            nc.gpsimd.tensor_tensor(qa[:, :, 49], shift[:, m % QB, :], qa[:, :, 48].bitcast(F32),
                                                    ALU.subtract).then_inc(self.s["qa_shift"], 1)

            def tensor(self, pe):
                sh = self.sh
                log = []

                def misc(kind, n):
                    if len(log) >= 2:
                        pe.wait_ge(self.s[log[-2][0]], log[-2][1] + 1)
                    log.append((kind, n))
                    return psM[:, len(log) % 2, :]

                pe.wait_ge(L["cst"], 16)
                def project(n):
                    if n >= 4:
                        pe.wait_ge(self.s["proj_out"], n - 3)
                    if n < B * sh.NT:
                        b, tt = divmod(n, sh.NT)
                        w0, w1 = D, 3 * D
                    else:
                        b, tt = divmod(n - B * sh.NT, S // P)
                        w0, w1 = 0, D
                    for kk in range(KD):
                        mm = nc.tensor.matmul(RING[n % 4][:, 0:w1 - w0], xT[:, kk, b * S + tt * P:b * S + tt * P + P],
                                              wqkv[:, kk, w0:w1], start=(kk == 0), stop=(kk == KD - 1))
                    mm.then_inc(self.s["proj_full"], 1)

                pe.wait_ge(s["consts_ready"], 1 + B)
                pe.wait_ge(self.s["zeroed"], 2)
                for c in range(sh.NC):
                    u0 = c * UNITS
                    if c:
                        pe.wait_ge(self.s["ot_out"], u0)
                    for what, m, k in self.counting(c):
                        if what == "entry":
                            k0 = m * K_SPARSE + k
                            tile = k0 // sh.EVERY - sh.LATER
                            if c == 0 and k0 % sh.EVERY == sh.EVERY - 1 and 0 <= tile < sh.PROJECTED:
                                if tile == 0:
                                    pe.wait_ge(L["x"], 16)
                                    pe.wait_ge(L["wqkv"], 32)
                                project(tile)
                            banks = 1 if self.dense else 2
                            if k == 0 and m >= banks:
                                pe.wait_ge(self.s["cnt_out"], 2 * (m - banks + 1))
                            who = self.lister(k)
                            e = m * NUMBER[who] + sum(self.lister(j) == who for j in range(k))
                            pe.wait_ge(self.s["eq_ready" + who], e + 1)
                            eq = self.EQ[who][:, e % self.RINGS[who], :]
                            for f in range(0, sh.T, 512):
                                w = min(512, sh.T)
                                mm = nc.tensor.matmul(self.bank_of_counts(m)[:, f:f + w], ident16[:, :], eq[:, f:f + w],
                                                      start=(k == 0), stop=(k == K_SPARSE - 1))
                            mm.then_inc(self.s["eq_used" + who], 1)
                        if what == "turn_counts":
                            pe.wait_ge(self.s["cnt_out"], 2 * (m + 1))
                            for t4 in range(0, sh.NT, sh.TP):
                                ps = misc("cntT_out", m * (sh.NT // sh.TP) + t4 // sh.TP)
                                for j in range(sh.TP):
                                    mm = nc.tensor.transpose(ps[:, j * P:j * P + P],
                                                             self.Cn[:, (t4 + j) * P:(t4 + j + 1) * P], ident)
                                mm.then_inc(self.s["cntT_full"], 1)
                    pe.wait_ge(self.s["proj_out"], sh.PROJECTED)
                    for what, i in self.due(c):
                        u = i // JOBS
                        if what == "ahead":
                            if i == 0:
                                pe.wait_ge(self.s["g_max"], 2 * JOBS * UNITS)
                                pe.wait_ge(self.s["s_exp"], 2 * JOBS * UNITS)
                            dense_tensor(pe, jobs[i:i + 1])
                        if what == "guard_keys":
                            b, g = divmod(i, GROUPS)
                            ug = u0 + i
                            half = ug // 2
                            if g % 2 == 0:
                                for q4 in range(0, sh.NQ, sh.QP):
                                    ps = misc("qg_out", half * (sh.NQ // sh.QP) + q4 // sh.QP)
                                    for j in range(sh.QP):
                                        mm = nc.tensor.transpose(ps[:, j * P:j * P + P],
                                                                 Qn[:, b, c * sh.NQ + q4 + j, (g // 2) * P:(g // 2) * P + P], ident)
                                    mm.then_inc(self.s["qg_full"], 1)
                                for t4 in range(0, sh.NT, sh.TP):
                                    ps = misc("kt_out", half * (sh.NT // sh.TP) + t4 // sh.TP)
                                    for j in range(sh.TP):
                                        mm = nc.tensor.transpose(ps[:, j * P:j * P + P],
                                                                 self.Kn[:, b, t4 + j, (g // 2) * P:(g // 2) * P + P], ident)
                                    mm.then_inc(self.s["kt_full"], 1)
                        if what == "score_keys":
                            m = u0 * sh.NT + i
                            pe.wait_ge(self.s["ka_ready"], m + 1)
                            ps = misc("kp_out", m)
                            for p in range(2):
                                mm = nc.tensor.transpose(ps[:, p * P:p * P + P],
                                                         Ka[:, m % 2, 2 * p:2 * p + 2, :].rearrange("p h a -> p (h a)").bitcast(F32), ident)
                            mm.then_inc(self.s["ka_full"], 1)
                        if what == "query_rows":
                            m = u0 * sh.NQ + i
                            pe.wait_ge(self.s["qa_split"], m + 1)
                            pe.wait_ge(self.s["qa_shift"], m + 1)
                            ps = misc("qat_out", m)
                            for p in range(2):
                                mm = nc.tensor.transpose(ps[:, p * P:p * P + P],
                                                         Qa[:, m % QB, 2 * p:2 * p + 2, :].rearrange("p h a -> p (h a)").bitcast(F32), ident)
                            mm.then_inc(self.s["qa_full"], 1)
                        if what == "guard":
                            b, g = divmod(u, GROUPS)
                            ug = u0 + u
                            st, blk = divmod(i % JOBS, sh.NBK)
                            pe.wait_ge(self.s["kg_ready"], ug + 1)
                            pe.wait_ge(self.s["qg_out"], (ug // 2 + 1) * (sh.NQ // sh.QP))
                            for p in range(2):
                                banks, last = self.guard_bank(u0 * JOBS + i)
                                if last >= 0:
                                    pe.wait_ge(self.s["g_max"], 2 * last + p + 1)
                                o = banks[:, p, :].rearrange("p (h t) -> p h t", h=2)
                                nc.tensor.matmul(o, self.QG[:, (ug // 2) % 2, st * P:st * P + P],
                                                 self.KG[:, ug % sh.NB, 2 * p:2 * p + 2, blk * 256:blk * 256 + 256],
                                                 start=True, stop=False)
                                a = st * sh.T + blk * 256
                                mm = nc.tensor.matmul(o, identm[:, b, :],
                                                      Mneg[:, None, a:a + 256].to_broadcast([P, 2, 256]),
                                                      start=False, stop=True)
                                mm.then_inc(self.s["g_scores"], 1)
                        if what == "score":
                            ug = u0 + u
                            r, j = divmod(i % JOBS, HG)
                            pe.wait_ge(self.s["kp_out"], (ug + 1) * sh.NT)
                            pe.wait_ge(self.s["qat_out"], (ug + 1) * sh.NQ)
                            flat = psS[:, :, :].rearrange("p a b -> p (a b)")
                            for f in range(0, 1024, sh.CP):
                                if not self.dense and i == 0:
                                    pe.wait_ge(self.s["g_max"], 2 * LAG)
                                if f % 512 == 0 and u0 * JOBS + i >= 1:
                                    pe.wait_ge(self.s["s_exp"], 2 * (u0 * JOBS + i - 1) + f // 512 + 1)
                                tt, q = divmod(r * 1024 + f, sh.SQ)
                                mm = nc.tensor.matmul(flat[:, f:f + sh.CP],
                                                      self.KP[:, ug % sh.NB, j, tt * P:tt * P + P],
                                                      self.QAT[:, ug % 2, j // 2, q:q + sh.CP], start=True, stop=True)
                                if (f + sh.CP) % 512 == 0:
                                    mm.then_inc(self.s["s_scores"], 1)
                        if what in ("values0", "values1"):
                            v = 2 * u0 + i
                            ug, r = divmod(v, 2)
                            b, g = divmod(i // 2, GROUPS)
                            pe.wait_ge(self.s["s_prob"], HG * (v + 1))
                            if r == 0 and ug:
                                pe.wait_ge(self.s["ot_out"], ug)
                            part = int(what[-1])
                            for f in range(512 * part, 512 * part + 512, sh.CP):
                                tt, q = divmod(r * 1024 + f, sh.SQ)
                                for j in range(HG):
                                    h = g * HG + j
                                    mm = nc.tensor.matmul(
                                        psO[VW * j:VW * j + VC, q // 512, q % 512:q % 512 + sh.CP],
                                        self.VA[:, b, tt, h * VC:h * VC + VC], Pr[:, HG * r + j, f:f + sh.CP],
                                        start=(tt == 0), stop=(tt == sh.NT - 1), tile_position=(0, VW * j))
                            if part:
                                mm.then_inc(self.s["pv_done"], 1)
                        if what == "norm":
                            ug = u0 + i
                            pe.wait_ge(self.s["ot_out"], ug + 1)
                            for q4 in range(0, sh.NQ, sh.QP):
                                ps = misc("on_out", ug * (sh.NQ // sh.QP) + q4 // sh.QP)
                                for j in range(sh.QP):
                                    mm = nc.tensor.transpose(ps[:, j * P:j * P + P],
                                                             self.OTs[:, (q4 + j) * P:(q4 + j + 1) * P], ident)
                                mm.then_inc(self.s["on_full"], 1)
                        if what == "turn":
                            hg = u0 // 2 + i
                            pe.wait_ge(self.s["on_out"], (2 * hg + 2) * (sh.NQ // sh.QP))
                            for q4 in range(0, sh.NQ, sh.QP):
                                ps = misc("at_out", hg * (sh.NQ // sh.QP) + q4 // sh.QP)
                                for j in range(sh.QP):
                                    mm = nc.tensor.transpose(ps[:, j * P:j * P + P], self.An[:, q4 + j, :], ident)
                                mm.then_inc(self.s["at_full"], 1)

            def act(self, act):
                sh = self.sh
                mi = 0

                def misc():
                    nonlocal mi
                    mi += 1
                    return psM[:, mi % 2, :]

                for c in range(sh.NC):
                    u0 = c * UNITS
                    for what, m, k in self.counting(c):
                        if what == "entry" and self.lister(k) == "_act":
                            self.compare_act(act, m, k)
                        if what == "turned_counts":
                            i = m % sh.NQ
                            for t4 in range(0, sh.NT, sh.TP):
                                act.wait_ge(self.s["cntT_full"], m * (sh.NT // sh.TP) + t4 // sh.TP + 1)
                                if self.dense and c and i == 0 and t4 == 0:
                                    act.wait_ge(self.s["w_ready"], B * c)
                                ct = self.CT[:, :].rearrange("p (t q) -> p t q", q=sh.SQ)
                                nc.scalar.copy(ct[:, t4:t4 + sh.TP, i * P:i * P + P],
                                               misc()[:, 0:sh.TP * P].rearrange("p (t q) -> p t q", q=P)).then_inc(self.s["cntT_out"], 1)
                    for what, i in self.due(c):
                        u = i // JOBS
                        if what == "guard" and not self.dense and i % JOBS == 4 and i // JOBS < len(EARLY):
                            split_hi(act, EARLY[i // JOBS:i // JOBS + 1])
                        if what == "guard" and i % sh.NBK == 0:
                            b, g = divmod(i // JOBS, GROUPS)
                            m = c * UNITS * sh.NQ + i // sh.NBK
                            if m == 0:
                                act.wait_ge(s["cleared"], 3)
                                act.wait_ge(self.s["proj_out"], sh.PROJECTED)
                            if m >= QB:
                                act.wait_ge(self.s["qa_full"], m - QB + 1)
                            q, qa = self.query_tile(c, m, b, g)
                            nc.scalar.copy(qa[:, :, 0:32].rearrange("p h (r d) -> p h r d", d=DH),
                                           q[:, :, None, :].to_broadcast([P, HG, 2, DH])).then_inc(self.s["qa_copied"], 1)
                        if what == "first_input":
                            act.wait_ge(self.s["at_out"], 2 * sh.NQ // sh.QP)
                            act.wait_ge(self.s["qa_split"], GROUPS * sh.NQ)
                            attention_hi(act, 0)
                        if what == "ahead":
                            if i == 0:
                                act.wait_ge(self.s["g_scores"], 2 * JOBS * UNITS)
                                act.wait_ge(self.s["cnt_out"], 2 * sh.NQ)
                                act.wait_ge(L["cols"], 16)
                            dense_act(act, jobs[i:i + 1])
                        if what == "guard_keys" and i % 2 == 0:
                            ug = u0 + i
                            half = ug // 2
                            if half >= 2:
                                act.wait_ge(self.s["g_scores"], 2 * JOBS * 2 * (half - 1))
                            for q4 in range(0, sh.NQ, sh.QP):
                                act.wait_ge(self.s["qg_full"], half * (sh.NQ // sh.QP) + q4 // sh.QP + 1)
                                nc.scalar.copy(self.QG[:, half % 2, q4 * P:(q4 + sh.QP) * P],
                                               misc()[:, 0:sh.QP * P]).then_inc(self.s["qg_out"], 1)
                            if ug:
                                act.wait_ge(self.s["kg_ready"], ug)
                            for t4 in range(0, sh.NT, sh.TP):
                                act.wait_ge(self.s["kt_full"], half * (sh.NT // sh.TP) + t4 // sh.TP + 1)
                                nc.scalar.copy(self.KT[:, t4 * P:(t4 + sh.TP) * P],
                                               misc()[:, 0:sh.TP * P]).then_inc(self.s["kt_out"], 1)
                        if what == "score_keys":
                            ug, tt = divmod(u0 * sh.NT + i, sh.NT)
                            if ug == 0:
                                act.wait_ge(self.s["zeroed_keys"], 1)
                            if ug >= sh.NB:
                                act.wait_ge(self.s["s_scores"], 2 * JOBS * (ug - sh.NB + 1))
                            act.wait_ge(self.s["ka_full"], ug * sh.NT + tt + 1)
                            ps = misc()[:, 0:2 * P].rearrange("p (a t) -> p a t", t=P)
                            kp = self.KP[:, ug % sh.NB, :, tt * P:tt * P + P]
                            nc.scalar.copy(kp[0:AUG, 0::2, :], ps[0:AUG, :, :])
                            nc.scalar.copy(kp[AUG:P, 1::2, :], ps[AUG:P, :, :]).then_inc(self.s["kp_out"], 1)
                        if what == "query_rows":
                            m = u0 * sh.NQ + i
                            ug, st = divmod(m, sh.NQ)
                            act.wait_ge(self.s["qa_full"], m + 1)
                            if ug >= 2 and st == 0:
                                act.wait_ge(self.s["s_scores"], 2 * JOBS * (ug - 1))
                            ps = misc()[:, 0:2 * P].rearrange("p (a t) -> p a t", t=P)
                            nc.scalar.copy(self.QAT[:, ug % 2, :, st * P:st * P + P], ps).then_inc(self.s["qat_out"], 1)
                        if what == "score":
                            n = u0 * JOBS + i
                            if self.dense and i % (GROUPS * JOBS) == 0:
                                b = i // (GROUPS * JOBS)
                                k = c * B + b
                                act.wait_ge(L["mask"], 16 * (c + 1))
                                act.wait_ge(s["idx_ready"], 1)
                                if k:
                                    act.wait_ge(self.s["s_prob"], k * GROUPS * JOBS)
                                nc.scalar.activation(W[:, :], self.maskT[:, :].bitcast(U8), ACT.Exp, bias=lam[:, 4, b:b + 1],
                                                     scale=lam[:, 3, b:b + 1]).then_inc(self.s["bias_exp"], 1)
                            if n == 0:
                                act.wait_ge(self.s["proj_out"], sh.PROJECTED)
                            if n >= JOBS:
                                act.wait_ge(self.s["pv_done"], (n - JOBS) // HG + 1)
                            for f in range(2):
                                act.wait_ge(self.s["s_scores"], 2 * n + f + 1)
                                nc.scalar.activation(Pr[:, n % JOBS, 512 * f:512 * f + 512], psS[:, f, :],
                                                     ACT.Exp, scale=SCALE).then_inc(self.s["s_exp"], 1)
                        if what == "take":
                            ug = u0 + i
                            act.wait_ge(self.s["pv_done"], 2 * (ug + 1))
                            if ug:
                                act.wait_ge(self.s["on_full"], ug * (sh.NQ // sh.QP))
                            nc.scalar.copy(self.OTs[:, :], psO[:, :, :].rearrange("p a b -> p (a b)")[:, 0:sh.SQ]
                                           ).then_inc(self.s["ot_out"], 1)
                        if what == "norm":
                            for q4 in range(0, sh.NQ, sh.QP):
                                misc()
                        if what == "turn":
                            hg = u0 // 2 + i
                            b, half = divmod(i, GROUPS // 2)
                            for q4 in range(0, sh.NQ, sh.QP):
                                k = hg * (sh.NQ // sh.QP) + q4 // sh.QP
                                act.wait_ge(self.s["at_full"], k + 1)
                                t0 = b * S + c * sh.SQ + q4 * P
                                last = k == sh.NC * (UNITS // 2) * (sh.NQ // sh.QP) - 1
                                nc.scalar.copy(attT[:, half, t0:t0 + sh.QP * P], misc()[:, 0:sh.QP * P]).then_inc(
                                    *((s["attention_done"], 1) if last else (self.s["at_out"], 1)))

            def token_banks(self):
                sh, n, found = self.sh, 0, []
                for c in range(sh.NC):
                    n += sh.NQ * (sh.NT // sh.TP)
                    for what, i in self.due(c):
                        if what == "guard_keys" and i % 2 == 0:
                            n += sh.NQ // sh.QP + sh.NT // sh.TP
                        if what == "score_keys":
                            n += 1
                        if what == "query_rows":
                            n += 1
                        if what in ("norm", "turn"):
                            for _ in range(sh.NQ // sh.QP):
                                n += 1
                                if what == "norm":
                                    found.append(n)
                return found

            def vector(self, dve):
                sh = self.sh
                banks = self.token_banks()
                va = self.VA[:, :, :, :].rearrange("p b t (h w) -> p (b t) h w", w=VC)
                nc.vector.memset(psO[:, :, :], 0.0).then_inc(self.s["zeroed"], 1)
                nc.vector.memset(va[:, :, :, DH:VC], 1.0).then_inc(self.s["zeroed"], 1)

                def projected(n):
                    dve.wait_ge(self.s["proj_full"], n + 1)
                    if n == 0:
                        dve.wait_ge(L["wqkv"], 32)
                    ps = RING[n % 4]
                    if n < B * sh.NT:
                        b, tt = divmod(n, sh.NT)
                        nc.vector.tensor_tensor(self.Kn[:, b, tt, :], ps[:, 0:D], bqkv[:, D:2 * D],
                                                ALU.add).then_inc(self.s["kv_out"], 1)
                        nc.vector.tensor_tensor(va[:, n, :, 0:DH], ps[:, D:2 * D].rearrange("p (h d) -> p h d", d=DH),
                                                bqkv[:, 2 * D:3 * D].rearrange("p (h d) -> p h d", d=DH),
                                                ALU.add).then_inc(self.s["proj_out"], 1)
                    else:
                        b, st = divmod(n - B * sh.NT, S // P)
                        nc.vector.tensor_tensor(Qn[:, b, st, :], ps[:, 0:D], bqkv[:, 0:D],
                                                ALU.add).then_inc(self.s["proj_out"], 1)

                for c in range(sh.NC):
                    u0 = c * UNITS
                    for what, m, k in self.counting(c):
                        if what == "entry":
                            if self.lister(k) == "_dve":
                                self.compare_on(dve, nc.vector, "_dve", m, k)
                            k0 = m * K_SPARSE + k
                            tile = k0 // sh.EVERY - sh.LATER - 1
                            if c == 0 and k0 % sh.EVERY == sh.EVERY // 2 and 0 <= tile < sh.PROJECTED - 1:
                                projected(tile)
                            if c == 0 and k0 == K_SPARSE * sh.NQ - 1:
                                projected(sh.PROJECTED - 1)
                        if what == "counts":
                            i = m % sh.NQ
                            for who in NUMBER:
                                dve.wait_ge(self.s["eq_used" + who], (m + 1) * NUMBER[who])
                            if m:
                                dve.wait_ge(self.s["cntT_full"], m * (sh.NT // sh.TP))
                            cnt = self.bank_of_counts(m)
                            nc.vector.tensor_copy(self.Cn[:, :], cnt).then_inc(self.s["cnt_out"], 1)
                            nc.vector.tensor_scalar(Mneg[:, i * sh.T:(i + 1) * sh.T], cnt, 0.0, -BIG, ALU.is_equal,
                                                    ALU.mult).then_inc(self.s["cnt_out"], 1)
                    for what, i in self.due(c):
                        u = i // JOBS
                        if what == "ahead" and i < KD:
                            if i == 0:
                                dve.wait_ge(self.s["qa_split"], UNITS * sh.NQ)
                            dense_vector(dve, jobs[i:i + 1], i)
                        if what == "guard":
                            gj = u0 * JOBS + i
                            st_, blk = divmod(gj, sh.NBK)
                            if blk == 0 and st_ >= QB:
                                dve.wait_ge(self.s["qa_shift"], st_ - QB + 1)
                            if sh.NBK > 1 and blk == 0 and st_:
                                dve.wait_ge(self.s["shift_ready"], st_)
                            for p in range(2):
                                dve.wait_ge(self.s["g_scores"], 2 * gj + p + 1)
                                dst = shift[:, st_ % QB, 2 * p:2 * p + 2] if sh.NBK == 1 else shiftb[:, 2 * p:2 * p + 2, blk]
                                nc.vector.tensor_reduce(dst, self.guard_bank(gj)[0][:, p, :].rearrange("p (h t) -> p h t", h=2), AX.X,
                                                        ALU.max, negate=True).then_inc(self.s["g_max"], 1)
                            if sh.NBK > 1 and blk == sh.NBK - 1:
                                dve.wait_ge(self.s["g_max"], 2 * (gj + 1))
                                nc.vector.tensor_reduce(shift[:, st_ % QB, :], shiftb[:, :, :], AX.X,
                                                        ALU.min).then_inc(self.s["shift_ready"], 1)
                        if what == "weigh":
                            n = u0 * JOBS + i
                            r = (n % JOBS) // HG
                            if i % (GROUPS * JOBS) == 0:
                                dve.wait_ge(self.s["cntT_out"], (c + 1) * sh.NQ * (sh.NT // sh.TP))
                                if self.dense:
                                    b = i // (GROUPS * JOBS)
                                    dve.wait_ge(self.s["bias_exp"], c * B + b + 1)
                                    nc.vector.tensor_scalar(W[:, :], W[:, :], lam[:, 5, b:b + 1], None,
                                                            ALU.mult).then_inc(self.s["self_dve"], 1)
                                    self.nd += 1
                                    dve.wait_ge(self.s["self_dve"], self.nd)
                                    nc.vector.scalar_tensor_tensor(W[:, :], self.CT[:, :], lam[:, 2, b:b + 1], W[:, :],
                                                                   ALU.mult, ALU.add).then_inc(self.s["w_ready"], 1)
                                    dve.wait_ge(self.s["w_ready"], c * B + b + 1)
                            dve.wait_ge(self.s["s_exp"], 2 * (n + 1))
                            pr = Pr[:, n % JOBS, :]
                            nc.vector.scalar_tensor_tensor(pr, pr, FMAX, W[:, r * 1024:r * 1024 + 1024], ALU.min,
                                                           ALU.mult).then_inc(self.s["s_prob"], 1)
                        if what == "norm":
                            ug = u0 + i
                            if ug >= 2 and ug % 2 == 0:
                                dve.wait_ge(self.s["at_full"], ug // 2 * (sh.NQ // sh.QP))
                            for q4 in range(0, sh.NQ, sh.QP):
                                k = ug * (sh.NQ // sh.QP) + q4 // sh.QP
                                dve.wait_ge(self.s["on_full"], k + 1)
                                ps = psM[:, banks[k] % 2, :][:, 0:sh.QP * P].rearrange("p (q h w) -> p q h w", h=HG, w=VW)
                                rd = self.rden[:, q4:q4 + sh.QP, :]
                                nc.vector.reciprocal(rd, ps[:, :, :, DH]).then_inc(self.s["recip"], 1)
                                dve.wait_ge(self.s["recip"], k + 1)
                                o = self.An[:, q4:q4 + sh.QP, (ug % 2) * 64:(ug % 2) * 64 + 64]
                                nc.vector.tensor_tensor(o.rearrange("p q (h d) -> p q h d", d=DH), ps[:, :, :, 0:DH],
                                                        rd[:, :, :, None].to_broadcast([P, sh.QP, HG, DH]),
                                                        ALU.mult).then_inc(self.s["on_out"], 1)

        atts = []
        attention_end = nc.sbuf_base
        for sh in shapes:
            at = ExitStack()
            atts.append(Attention(sh, f"_{sh.T}", at))
            if sh is shapes[0]:
                attention_end = nc.sbuf_base
            at.close()
        actx.close()

        class Split:
            def __init__(self, name, shape, at=ctx):
                self.hi = sb(name + "_hi", [P] + shape, F32R, at)
                self.lo = sb(name + "_lo", [P] + shape, F32R, at)

        cT = Split("cT", [KD, QC])
        aoT = Split("aoT", [KD, QC])
        V = sb("V", [P, 3, QC], F32)
        WcB = Split("WcB", [B, KW, P])
        ew = Split("ew", [KD, NE * D])
        WcA = Split("WcA", [KW, P])
        hT = Split("hT", [KW, QC])
        x1 = Split("x1", [KD, QC])
        rw = sb("rw", [P, KD, 2, NE], F32R)
        rw_in = sb("rw_in", [P, KD, NE], F32)
        x1T = sb("x1T", [P, KD, QC], F32)
        top = sb("top", [P, 4, 8], F32)
        topi = sb("topi", [P, 4, 8], U32)
        rt = sb("rt", [P, 12, 4], F32)
        lg = sb("lg", [P, 4, 8], F32)
        dl = sb("dl", [P, 4, 8], F32)
        oh = sb("oh", [P, 2, 4, 8], F32)
        gate = sb("gate", [P, 4, 8], F32)
        pw = sb("pw", [P, 4], F32)
        y = sb("y", [P, 2, D], F32)
        if nc.sbuf_base < attention_end:
            sb("gap", [P, (attention_end - nc.sbuf_base + 3) // 4], F32)
        Wo = Split("Wo", [KD, D])
        w1 = Split("w1", [KD, WIDTH])
        w2 = Split("w2", [KW, D])
        fc1 = Split("fc1", [KD, WIDTH])
        staged = sb("staged", [P, 2, 1024], F32)

        def flat(w, n0, n):
            out = []
            for part in (w.hi, w.lo):
                a = part[:]
                if len(a.shape) == 3:
                    a = a.rearrange("p a b -> p (a b)")
                elif len(a.shape) == 4:
                    a = a.rearrange("p a b c -> p (a b c)")
                out.append(a[:, n0:n0 + n])
            return out

        early, late = [], []
        early.append(("Wo", flat(Wo, 0, 512), [("WoT", 0, 512)]))
        for name, w in (("w1", w1), ("w2", w2), ("fc1", fc1)):
            for h in range(2):
                early.append((name, flat(w, h * 1024, 1024), [(name, h * 1024, 1024)]))
        late.append(("Wc", flat(WcA, 0, 1024), [("fc2a", 0, 1024)]))
        for b in range(B):
            late.append(("Wc", flat(WcB, b * 1024, 1024), [("fc2b", b)]))
        for h in range(KD * NE * D // 1024):
            late.append(("ew", flat(ew, h * 1024, 1024), [("ew", h * 1024, 1024)]))
        pieces = early + late
        ready_at = {name: i + 1 for i, (name, _, _) in enumerate(pieces)}
        LD = {k: sem(k) for k in ("ld_stage0", "ld_stage1", "w_hi", "w_lo0", "w_lo1", "ld_rw", "ld_residual")}
        stage_loads = [0, 0]
        load_values = []
        for i, (_, _, loads) in enumerate(pieces):
            stage_loads[i % 2] += 16 * (2 if loads[0][0] == "fc2b" else 1)
            load_values.append(stage_loads[i % 2])

        def load_pieces(sp, which, eid):
            for i in which:
                if i >= 2:
                    sp.wait_ge(LD[f"w_lo{i % 2}"], i // 2)
                st = staged[:, i % 2, :]
                name, loads = pieces[i][0], pieces[i][2][0]
                if loads[0] == "fc2b":
                    st = st.rearrange("p (k o) -> p k o", o=P)
                    sp.dma_start(st[:, :, 0:P - PART], io["fc2b"]).then_inc(LD[f"ld_stage{i % 2}"], 16)
                    sp.dma_start(st[:, :, P - PART:P], io["experts"][:, bass.ds(eid[loads[1]], 1), :, :].rearrange(
                        "p a k o -> p (a k) o")).then_inc(LD[f"ld_stage{i % 2}"], 16)
                else:
                    sp.dma_start(st[:, 0:loads[2]], io[loads[0]][:, loads[1]:loads[1] + loads[2]]).then_inc(
                        LD[f"ld_stage{i % 2}"], 16)

        def split_hi(act, which):
            for i in which:
                act.wait_ge(LD[f"ld_stage{i % 2}"], load_values[i])
                hi = pieces[i][1][0]
                nc.scalar.copy(hi, staged[:, i % 2, 0:hi.shape[1]]).then_inc(LD["w_hi"], 1)

        def split_lo(engine, eng, which):
            for i in which:
                eng.wait_ge(LD["w_hi"], i + 1)
                hi, lo = pieces[i][1]
                engine.tensor_tensor(lo, staged[:, i % 2, 0:hi.shape[1]], hi.bitcast(F32),
                                     ALU.subtract).then_inc(LD[f"w_lo{i % 2}"], 1)

        EARLY, LATE = range(len(early)), range(len(early), len(pieces))

        d = {k: sem(k) for k in (
            "a_full", "a_out", "v_full", "v_out", "parts", "at_hi", "at_lo",
            "rt_exp", "rt_sub", "self_dense", "stored0", "stored1")}
        TT = QC // P
        ABANK = RING
        VBANK = [psO[:, 0, :], psO[:, 1, :], psM[:, 0, :], psM[:, 1, :]]
        bo, b1, b2, f1b = cols[:, 0:2], cols[:, 2:10], cols[:, 10:12], cols[:, 12:20]

        def dense_jobs():
            n = {"act": 0, "dve": 0}

            def jobs_of(stage, c, which, eng):
                for i in which:
                    yield stage, c, i, eng, n[eng]
                    n[eng] += 1

            yield from jobs_of("ao", 0, range(KD), "act")
            behind = TT * 5 - 4
            for c in range(CHUNKS + 1):
                if c < CHUNKS:
                    yield from jobs_of("h", c, range(KW // 2), "act")
                if c:
                    yield from jobs_of("router", c - 1, range(1), "dve")
                if c < CHUNKS:
                    yield from jobs_of("h", c, range(KW // 2, KW), "act")
                if c:
                    yield from jobs_of("experts", c - 1, range(behind), "dve")
                if c < CHUNKS:
                    yield from jobs_of("y", c, range(KD), "dve")
                now = TT * 5 if c + 1 < CHUNKS or c == CHUNKS else behind + 2
                if c:
                    yield from jobs_of("experts", c - 1, range(behind, now), "dve")
                if c == 0:
                    yield from jobs_of("ao", 1, range(1), "act")
                if c < CHUNKS:
                    yield from jobs_of("gelu", c, range(KW), "act")
                    if c:
                        yield from jobs_of("experts", c - 1, range(now, TT * 5), "dve")
                    if c + 1 < CHUNKS:
                        yield from jobs_of("ao", c + 1, range(c == 0, KD), "act")
                    yield from jobs_of("c", c, range(KD), "act")

        jobs = list(dense_jobs())
        split_no = {}
        for stage, c, i, e, n in jobs:
            if stage in ("ao", "h", "y", "gelu", "c"):
                split_no[stage, c, i] = len(split_no) + 1
        number = {(stage, c, i): n for stage, c, i, e, n in jobs}

        def mm3(ps, w, a, start, stop):
            nc.tensor.matmul(ps, w[0], a[1], start=start, stop=False)
            nc.tensor.matmul(ps, w[1], a[0], start=False, stop=False)
            return nc.tensor.matmul(ps, w[0], a[0], start=False, stop=stop)

        def parts(t, *at):
            return t.hi[at], t.lo[at]

        ALL = slice(None)

        def dense_tensor(pe, part):
            def bank(e, n):
                if n >= 4:
                    pe.wait_ge(d["a_out" if e == "act" else "v_out"], n - 3)
                return (ABANK if e == "act" else VBANK)[n % 4]

            whole = set()

            def weights(name):
                if name not in whole:
                    whole.add(name)
                    for st in range(2):
                        pe.wait_ge(LD[f"w_lo{st}"], (ready_at[name] + 1 - st) // 2)

            for stage, c, i, e, n in part:
                ps = bank(e, n)
                cols_ = slice(i * P, i * P + P)
                if stage == "ao":
                    weights("Wo")
                    pe.wait_ge(d["at_lo"], c + 1)
                    for k in range(KD):
                        mm = mm3(ps, parts(Wo, ALL, k, cols_), parts(cT, ALL, k, ALL), k == 0, k == KD - 1)
                if stage == "h":
                    weights("w1")
                    pe.wait_ge(d["parts"], split_no["ao", c, KD - 1])
                    for k in range(KD):
                        mm = mm3(ps, parts(w1, ALL, k, cols_), parts(aoT, ALL, k, ALL), k == 0, k == KD - 1)
                if stage == "y":
                    weights("w2")
                    for k in range(KW):
                        pe.wait_ge(d["parts"], split_no["h", c, k])
                        mm = mm3(ps, parts(w2, ALL, k, cols_), parts(hT, ALL, k, ALL), k == 0, k == KW - 1)
                if stage == "gelu":
                    weights("fc1")
                    pe.wait_ge(d["parts"], split_no["y", c, KD - 1])
                    for k in range(KD):
                        mm = mm3(ps, parts(fc1, ALL, k, cols_), parts(x1, ALL, k, ALL), k == 0, k == KD - 1)
                if stage == "c":
                    weights("Wc")
                    for k in range(KW):
                        pe.wait_ge(d["parts"], split_no["gelu", c, k])
                        w = parts(WcA, ALL, k, ALL) if i == 0 else parts(WcB, ALL, c * QC // S, k, ALL)
                        mm = mm3(ps, w, parts(hT, ALL, k, ALL), k == 0, k == KW - 1)
                if stage == "router":
                    if c == 0:
                        pe.wait_ge(d["parts"], split_no["h", 0, 0])
                    pe.wait_ge(d["parts"], split_no["c", c, KD - 1])
                    for t in range(TT):
                        o = ps[:, t * 2 * NE:(t + 1) * 2 * NE]
                        for k in range(KD):
                            hi, lo = parts(cT, ALL, k, slice(t * P, t * P + P))
                            nc.tensor.matmul(o, hi, rw[:, k, :, :].rearrange("p a e -> p (a e)"), start=(k == 0), stop=False)
                            mm = nc.tensor.matmul(o[:, 0:NE], lo, rw[:, k, 0, :], start=False, stop=(k == KD - 1))
                if stage == "experts":
                    weights("ew")
                    t, j = divmod(i, 5)
                    if j == 0:
                        for k in range(KD):
                            mm = nc.tensor.transpose(ps[:, k * P:k * P + P], x1T[:, k, t * P:t * P + P], ident)
                    else:
                        for k in range(KD):
                            mm = mm3(ps, parts(cT, ALL, k, slice(t * P, t * P + P)),
                                     parts(ew, ALL, k, slice((j - 1) * 512, j * 512)), k == 0, k == KD - 1)
                mm.then_inc(d["a_full" if e == "act" else "v_full"], 1)

        LATE_AT = (("h", 2), ("h", 5), ("y", 0), ("y", 0), ("gelu", 1), ("gelu", 4), ("c", 0))

        def late_at(stage, c, i):
            return [LATE[k] for k, at in enumerate(LATE_AT) if c == 0 and at == (stage, i)]

        def attention_hi(act, c):
            if c >= 2:
                act.wait_ge(d["v_full"], number["experts", c - 2, TT * 5 - 1] + 1)
            nc.scalar.copy(cT.hi[:, :, :], attT[:, :, c * QC:(c + 1) * QC]).then_inc(d["at_hi"], 1)

        def dense_act(act, part):
            for stage, c, i, e, n in part:
                ps = ABANK[n % 4]
                if stage == "y":
                    split_hi(act, late_at(stage, c, i))
                if (stage, c, i) == ("y", 0, 0) or stage == "gelu" and i == 2 and 0 < c < CHUNKS - 1:
                    attention_hi(act, c + 1)
                if stage == "router":
                    act.wait_ge(d["rt_sub"], c + 1)
                    nc.scalar.activation(dl[:, :, :], dl[:, :, :], ACT.Exp).then_inc(d["rt_exp"], 1)
                if e != "act":
                    continue
                act.wait_ge(d["a_full"], n + 1)
                if n >= 3:
                    act.wait_ge(d["parts"], split_of_act[n - 3])
                v = V[:, n % 3, :]
                if stage == "ao":
                    nc.scalar.activation(v, ps, ACT.Identity, bias=bo[:, i:i + 1]).then_inc(d["a_out"], 1)
                if stage == "h":
                    nc.scalar.activation(v, ps, ACT.Relu, bias=b1[:, i:i + 1]).then_inc(d["a_out"], 1)
                    split_hi(act, late_at(stage, c, i))
                if stage == "gelu":
                    nc.scalar.activation(v, ps, ACT.Gelu, bias=f1b[:, i:i + 1]).then_inc(d["a_out"], 1)
                    split_hi(act, late_at(stage, c, i))
                if stage == "c":
                    if c == 0 and i == 0:
                        act.wait_ge(L["small"], 16 * 6)
                    nc.scalar.activation(v, ps, ACT.Identity,
                                         bias=cbias[:, c * QC // S, i:i + 1]).then_inc(d["a_out"], 1)
                    split_hi(act, late_at(stage, c, i))

        split_of_act = [split_no[stage, c, i] for stage, c, i, e, n in jobs if e == "act"]

        def attention_lo(pool, c):
            pool.wait_ge(d["at_hi"], c + 1)
            nc.gpsimd.tensor_tensor(cT.lo[:, :, :], attT[:, :, c * QC:(c + 1) * QC], cT.hi[:, :, :].bitcast(F32),
                                    ALU.subtract).then_inc(d["at_lo"], 1)

        def dense_pool(pool):
            pool.wait_ge(s["attention_done"], 1)
            split_lo(nc.gpsimd, pool, [i for i, at in zip(LATE, LATE_AT) if i % 2 == 0 and at[0] in ("h", "y")])
            attention_lo(pool, 1)
            split_lo(nc.gpsimd, pool, [i for i, at in zip(LATE, LATE_AT) if i % 2 == 0 and at[0] in ("gelu", "c")])
            for c in range(2, CHUNKS):
                attention_lo(pool, c)

        def dense_vector(dve, part, links):
            nd = [links]

            def link(ins):
                nd[0] += 1
                ins.then_inc(d["self_dense"], 1)

            def settle():
                dve.wait_ge(d["self_dense"], nd[0])

            def split(tile, v, at):
                link(nc.vector.tensor_copy(tile.hi[at], v))
                settle()
                nc.vector.tensor_tensor(tile.lo[at], v, tile.hi[at].bitcast(F32), ALU.subtract).then_inc(d["parts"], 1)

            for stage, c, i, e, n in part:
                at = (ALL, i, ALL)
                if e == "act":
                    dve.wait_ge(d["a_out"], n + 1)
                    v = V[:, n % 3, :]
                    if stage == "ao":
                        if c and i == 0:
                            dve.wait_ge(d["a_full"], number["h", c - 1, KW - 1] + 1)
                        split(aoT, v, at)
                    if stage == "h":
                        if c and i == 0:
                            dve.wait_ge(d["a_full"], number["c", c - 1, KD - 1] + 1)
                        split(hT, v, at)
                    if stage == "gelu":
                        if i == 0:
                            dve.wait_ge(d["v_full"], number["y", c, KD - 1] + 1)
                        split(hT, v, at)
                    if stage == "c":
                        if i == 0:
                            dve.wait_ge(d["a_full"], number["ao", min(c + 1, CHUNKS - 1), KD - 1] + 1)
                            if c:
                                dve.wait_ge(d["v_full"], number["experts", c - 1, TT * 5 - 1] + 1)
                        split(cT, v, at)
                    split_lo(nc.vector, dve, [k for k in late_at(stage, c, i) if k % 2])
                    continue
                ps = VBANK[n % 4]
                split_lo(nc.vector, dve, [k for k in late_at(stage, c, i) if k % 2])
                dve.wait_ge(d["v_full"], n + 1)
                if stage == "y":
                    if i == 0:
                        dve.wait_ge(LD["ld_residual"], 16 * (c + 1))
                        if c:
                            dve.wait_ge(d["a_full"], number["gelu", c - 1, KW - 1] + 1)
                            dve.wait_ge(d["v_full"], number["experts", c - 1, TT * 5 - 5] + 1)
                    nc.vector.scalar_tensor_tensor(x1T[:, i, :], ps, b2[:, i:i + 1], x1T[:, i, :],
                                                   ALU.add, ALU.add).then_inc(d["v_out"], 1)
                    dve.wait_ge(d["v_out"], n + 1)
                    split(x1, x1T[:, i, :], at)
                if stage == "router":
                    if c:
                        dve.wait_ge(d["rt_exp"], c)
                    both = ps[:, 0:TT * 2 * NE].rearrange("p (t a e) -> p t a e", a=2, e=NE)
                    link(nc.vector.tensor_copy(lg[:, :, :], both[:, :, 1, :]))
                    settle()
                    nc.vector.tensor_tensor(lg[:, :, :], both[:, :, 0, :], lg[:, :, :], ALU.add).then_inc(d["v_out"], 1)
                    dve.wait_ge(d["v_out"], n + 1)
                    for t in range(TT):
                        link(nc.vector.max(top[:, t, :], lg[:, t, :]))
                    settle()
                    for t in range(TT):
                        link(nc.vector.max_index(topi[:, t, :], top[:, t, :], lg[:, t, :]))
                    nc.vector.tensor_tensor(dl[:, :, :], lg[:, :, :], top[:, :, 0:1].to_broadcast([P, TT, NE]),
                                            ALU.subtract).then_inc(d["rt_sub"], 1)
                    settle()
                    link(nc.vector.tensor_copy(rt[:, 0:2, :].rearrange("p k t -> p t k"), topi[:, :, 0:2]))
                    settle()
                    for k in range(2):
                        link(nc.vector.tensor_tensor(oh[:, k, :, :], iota8[:, None, :].to_broadcast([P, TT, NE]),
                                                     rt[:, k, :, None].to_broadcast([P, TT, NE]), ALU.is_equal))
                    dve.wait_ge(d["rt_exp"], c + 1)
                    link(nc.vector.tensor_reduce(rt[:, 2, :], dl[:, :, :], AX.X, ALU.add))
                    settle()
                    link(nc.vector.reciprocal(rt[:, 3, :], rt[:, 2, :]))
                    settle()
                    link(nc.vector.tensor_tensor(dl[:, :, :], dl[:, :, :], rt[:, 3, :, None].to_broadcast([P, TT, NE]), ALU.mult))
                    settle()
                    for k in range(2):
                        link(nc.vector.tensor_tensor(lg[:, :, :], dl[:, :, :], oh[:, k, :, :], ALU.mult))
                        settle()
                        link(nc.vector.tensor_reduce(rt[:, 4 + k, :], lg[:, :, :], AX.X, ALU.add))
                        settle()
                    link(nc.vector.scalar_tensor_tensor(rt[:, 6, :], rt[:, 4, :], 1e-6, rt[:, 5, :], ALU.add, ALU.add))
                    settle()
                    link(nc.vector.reciprocal(rt[:, 7, :], rt[:, 6, :]))
                    settle()
                    for k in range(2):
                        link(nc.vector.tensor_tensor(rt[:, 8 + k, :], rt[:, 4 + k, :], rt[:, 7, :], ALU.mult))
                    settle()
                    for k in range(2):
                        link(nc.vector.tensor_tensor(rt[:, 10 + k, :], rt[:, 4 + k, :], rt[:, 8 + k, :], ALU.mult))
                        link(nc.vector.tensor_tensor(oh[:, k, :, :], oh[:, k, :, :],
                                                     rt[:, 8 + k, :, None].to_broadcast([P, TT, NE]), ALU.mult))
                    settle()
                    link(nc.vector.tensor_tensor(pw[:, :], rt[:, 10, :], rt[:, 11, :], ALU.add))
                    link(nc.vector.tensor_tensor(gate[:, :, :], oh[:, 0, :, :], oh[:, 1, :, :], ALU.add))
                    settle()
                if stage == "experts":
                    t, j = divmod(i, 5)
                    k = c * TT + t
                    if j == 0:
                        if k >= 2:
                            dve.wait_ge(d[f"stored{k % 2}"], 16 * (k // 2))
                        ins = nc.vector.tensor_scalar(y[:, k % 2, :], ps[:, 0:D], pw[:, t:t + 1], None, ALU.add)
                        ins.then_inc(d["v_out"], 1)
                        dve.wait_ge(d["v_out"], n + 1)
                    else:
                        e0 = 2 * (j - 1)
                        link(nc.vector.scalar_tensor_tensor(y[:, k % 2, :], ps[:, 0:D], gate[:, t, e0:e0 + 1],
                                                            y[:, k % 2, :], ALU.mult, ALU.add))
                        settle()
                        nc.vector.scalar_tensor_tensor(y[:, k % 2, :], ps[:, D:2 * D], gate[:, t, e0 + 1:e0 + 2],
                                                       y[:, k % 2, :], ALU.mult, ALU.add).then_inc(d["v_out"], 1)
                        dve.wait_ge(d["v_out"], n + 1)

        block = ctx.enter_context(nc.Block())

        @block.sync
        def _(sp):
            sp.dma_start(idx, io["idx"]).then_inc(L["idx"], 16)
            sp.dma_start(idm[:, :, :], io["idm"]).then_inc(L["idx"], 16)
            sp.dma_start(lam[:, 0, :], io["u"]).then_inc(L["u"], 16)
            sp.dma_start(cst[:, :], io["consts"]).then_inc(L["cst"], 16)
            sp.dma_start(iota16[:, :], io["ramp"]).then_inc(L["ramp"], 16)
            sp.dma_start(wqkv, io["wqkv"]).then_inc(L["wqkv"], 16)
            sp.dma_start(bqkv, io["bqkv"]).then_inc(L["wqkv"], 16)
            sp.dma_start(xT, io["xT"]).then_inc(L["x"], 16)
            sp.dma_start(small[:, 0:2], io["expert_id"]).then_inc(L["small"], 16)
            sp.dma_start(cols[:, :], io["cols"]).then_inc(L["cols"], 16)
            sp.wait_ge(L["small"], 16)
            eid = [sp.value_load(small[0:1, b:b + 1], min_val=0, max_val=15) for b in range(B)]
            for b in range(B):
                sp.dma_start(cbias[:, b, 0:1], io["cshared"][:, 0:1], allow_slow_non_contiguous=True).then_inc(L["small"], 16)
                sp.dma_start(cbias[0:64, b, 1:2], io["cshared"][0:64, 1:2], allow_slow_non_contiguous=True).then_inc(L["small"], 16)
            for b in range(B):
                sp.dma_start(cbias[64:128, b, 1:2],
                             io["eb"][bass.ds(eid[b], 1), :].rearrange("a p -> p a"), allow_slow_non_contiguous=True).then_inc(L["small"], 16)

            def loads(att):
                if not att.dense:
                    load_pieces(sp, EARLY, eid)
                    return
                for c in range(att.sh.NC):
                    if c:
                        sp.wait_ge(att.s["bias_exp"], B * c)
                    sp.dma_start(att.maskT[:, :].rearrange("p (t q) -> p t q", q=att.sh.SQ // 4),
                                 io["maskT"][:, :, c * att.sh.SQ // 4:(c + 1) * att.sh.SQ // 4]).then_inc(L["mask"], 16)
                sp.wait_ge(s["attention_done"], 1)
                load_pieces(sp, EARLY, eid)
            either(sp, loads)
            load_pieces(sp, LATE[0:2], eid)
            sp.wait_ge(s["attention_done"], 1)
            sp.dma_start(rw_in[:, :, :], io["rw"]).then_inc(LD["ld_rw"], 16)
            sp.dma_start(x1T[:, :, :], io["xT"][:, :, 0:QC]).then_inc(LD["ld_residual"], 16)
            load_pieces(sp, LATE[2:], eid)
            k = 0
            for stage, c, i, e, n in jobs:
                if stage == "experts" and i == TT * 5 - 5 and c + 1 < CHUNKS:
                    sp.wait_ge(d["v_full"], n + 1)
                    sp.dma_start(x1T[:, :, :], io["xT"][:, :, (c + 1) * QC:(c + 2) * QC]).then_inc(LD["ld_residual"], 16)
                if stage == "experts" and i % 5 == 4:
                    sp.wait_ge(d["v_out"], n + 1)
                    t0 = (c * TT + i // 5) * P
                    sp.dma_start(out[t0:t0 + P, :], y[:, k % 2, :]).then_inc(d[f"stored{k % 2}"], 16)
                    k += 1
            for i in range(2):
                sp.wait_ge(d[f"stored{i}"], 16 * (k // 2))

        @block.gpsimd
        def _(pool):
            setup_pool(pool)

            def work(att):
                att.pool(pool)
                if att.dense:
                    pool.wait_ge(s["attention_done"], 1)
                    attention_lo(pool, 0)
                    split_lo(nc.gpsimd, pool, EARLY)
            either(pool, work)
            dense_pool(pool)

        @block.tensor
        def _(pe):
            setup_tensor(pe)

            def work(att):
                att.tensor(pe)
                pe.wait_ge(s["attention_done"], 1)
                if att.dense:
                    dense_tensor(pe, jobs[0:len(AHEAD_AT)])
            either(pe, work)
            dense_tensor(pe, jobs[len(AHEAD_AT):])

        @block.scalar
        def _(act):
            setup_act(act)

            def work(att):
                att.act(act)
                if att.dense:
                    act.wait_ge(s["attention_done"], 1)
                    attention_hi(act, 0)
                    split_hi(act, EARLY)
                    act.wait_ge(L["cols"], 16)
                    dense_act(act, jobs[0:len(AHEAD_AT)])
            either(act, work)
            act.wait_ge(s["attention_done"], 1)
            dense_act(act, jobs[len(AHEAD_AT):])

        @block.vector
        def _(dve):
            setup_dve(dve)

            def work(att):
                att.vector(dve)
                dve.wait_ge(s["attention_done"], 1)
                if att.dense:
                    for i in range(KD):
                        dense_vector(dve, jobs[i:i + 1], i)
            either(dve, work)
            dve.wait_ge(L["cols"], 16)
            dve.wait_ge(LD["ld_rw"], 16)
            nc.vector.tensor_copy(rw[:, :, 0, :], rw_in[:, :, :]).then_inc(d["self_dense"], 1)
            dve.wait_ge(d["self_dense"], KD + 1)
            nc.vector.tensor_tensor(rw[:, :, 1, :], rw_in[:, :, :], rw[:, :, 0, :].bitcast(F32),
                                    ALU.subtract).then_inc(d["self_dense"], 1)
            dense_vector(dve, jobs[KD:], KD + 2)


_OUT = "out_dram"


def _consts():
    c = np.zeros((P, C_END), np.float32)
    p = np.arange(P)
    c[:, C_ID:C_ID + P] = np.eye(P, dtype=np.float32)
    c[:, C_HM:C_HM + 8] = (p[:, None] // DH == np.arange(8)[None, :])
    c[:, C_E8:C_E8 + 8] = np.arange(8)
    return c


def kernel(x, itok_Sx32_0_1023, condB_uprev, itok_B_0_15, mask_SxS_bk0, mask_Sx32_bk1, L0_cond_Wq, L0_cond_bq,
           L0_cond_Wk, L0_cond_bk, L0_cond_Wv, L0_cond_bv, L0_cond_Wo, L0_cond_bo, L0_ffn_w1, L0_ffn_b1, L0_ffn_w2,
           L0_ffn_b2, L1_cond_fc1_w, L1_cond_fc1_b, L1_cond_fc2_w, L1_cond_fc2_b, L1_cond_experts_w,
           L1_cond_experts_b, L1_ffn_router_w, L1_ffn_expert_weights):
    import concourse.bacc as bacc
    from concourse.bass_utils import run_bass_kernel_spmd

    def rows(a):
        a = np.asarray(a)
        return np.ascontiguousarray(a.reshape(a.shape[0] // P, P, -1).transpose(1, 0, 2))

    def spread(*vs):
        return np.ascontiguousarray(np.broadcast_to(np.concatenate([np.asarray(v) for v in vs])[None, :],
                                                    (P, sum(v.shape[0] for v in vs))))

    def column(v):
        return np.asarray(v).reshape(-1, P).T

    A = np.asarray
    fc2b = np.zeros((2, P), np.float32)
    fc2b.reshape(-1)[0:SHARED] = A(L1_cond_fc2_b)
    arrays = {
        "consts": _consts(),
        "ramp": np.ascontiguousarray(np.broadcast_to(np.arange(1, S + 1, dtype=np.float16), (P, S))),
        "xT": rows(A(x).reshape(N, D).T),
        "wqkv": rows(np.concatenate([A(L0_cond_Wq).T, A(L0_cond_Wk).T, A(L0_cond_Wv).T], axis=1)),
        "bqkv": spread(L0_cond_bq, L0_cond_bk, L0_cond_bv),
        "idx": np.ascontiguousarray(A(itok_Sx32_0_1023).reshape(S // P, P, K_SPARSE).transpose(1, 0, 2)),
        "idm": np.ascontiguousarray(A(mask_Sx32_bk1).view(np.int32).reshape(S // P, P, K_SPARSE // 4).transpose(1, 0, 2)),
        "u": spread(condB_uprev),
        "expert_id": np.ascontiguousarray(A(itok_B_0_15).reshape(1, B)),
        "cols": np.ascontiguousarray(np.concatenate(
            [column(L0_cond_bo), column(L0_ffn_b1), column(L0_ffn_b2), column(L1_cond_fc1_b)], axis=1)),
        "cshared": np.ascontiguousarray(fc2b.T),
        "eb": A(L1_cond_experts_b),
        "WoT": rows(A(L0_cond_Wo).T).reshape(P, -1),
        "w1": rows(L0_ffn_w1).reshape(P, -1),
        "maskT": rows(np.ascontiguousarray(A(mask_SxS_bk0).T).view(np.int32)),
        "w2": rows(L0_ffn_w2).reshape(P, -1),
        "fc1": rows(A(L1_cond_fc1_w).T).reshape(P, -1),
        "fc2a": np.ascontiguousarray(rows(A(L1_cond_fc2_w).T)[:, :, 0:P]).reshape(P, -1),
        "fc2b": np.ascontiguousarray(rows(A(L1_cond_fc2_w).T)[:, :, P:SHARED]),
        "experts": np.ascontiguousarray(A(L1_cond_experts_w).transpose(2, 0, 1).reshape(KW, P, 16, PART).transpose(1, 2, 0, 3)),
        "rw": rows(A(L1_ffn_router_w).T),
        "ew": rows(A(L1_ffn_expert_weights).transpose(1, 0, 2).reshape(D, NE * D)).reshape(P, -1),
    }
    nc = bacc.Bacc("TRN2", target_bir_lowering=False, num_devices=1)
    io = {k: nc.dram_tensor(k + "_dram", v.shape, mybir.dt.from_np(v.dtype), kind="ExternalInput").ap()
          for k, v in arrays.items()}
    out = nc.dram_tensor(_OUT, (N, D), F32, kind="ExternalOutput").ap()
    bass_adaln_ffn(nc, io, out)
    r = run_bass_kernel_spmd(nc, [{k + "_dram": v for k, v in arrays.items()}], core_ids=[0])
    return r.results[0][_OUT].reshape(B, S, D)
```
